# Optimizing a Trainium2 kernel written in Bass

```python
import numpy as np
import jax
import jax.numpy as jnp

def _softmax(x, axis=-1):
    return jax.nn.softmax(x, axis=axis)

def _gelu(x):
    return jax.nn.gelu(x, approximate=True)

def _silu(x):
    return jax.nn.silu(x)

def _sigmoid(x):
    return jax.nn.sigmoid(x)

def _layernorm(x, axis=-1, eps=1e-05):
    m = jnp.mean(x, axis=axis, keepdims=True)
    v = jnp.var(x, axis=axis, keepdims=True)
    return (x - m) / jnp.sqrt(v + eps)

def _scatter_add(tgt, idx, src, axis=0):
    return tgt.at[idx].add(src)

def _segment_sum(src, seg, n):
    return jax.ops.segment_sum(src, seg, n)
kernel_name = 'mk_prb_d2_jaxref_r8_19a2d9'

def setup_inputs(seed: int=0):
    np.random.seed(seed)
    _w = jnp.asarray

    def _L0_attn_setup():
        import jax, jax.numpy as jnp
        import numpy as np
        N_HEAD = 16
        WINDOW = 128
        CAUSAL = False

        def _window_attention(x, w_in, b_in, w_out, b_out):
            B, T, D = x.shape
            H = N_HEAD
            hd = D // H
            scale = 1.0 / jnp.sqrt(jnp.float32(hd))
            qkv = jnp.einsum('btd,ed->bte', x, w_in) + b_in
            q, k, v = jnp.split(qkv, 3, axis=-1)
            q = q.reshape(B, T, H, hd).transpose(0, 2, 1, 3)
            k = k.reshape(B, T, H, hd).transpose(0, 2, 1, 3)
            v = v.reshape(B, T, H, hd).transpose(0, 2, 1, 3)
            scores = jnp.einsum('bhqd,bhkd->bhqk', q, k) * scale
            idx = jnp.arange(T)
            diff = idx[:, None] - idx[None, :]
            if CAUSAL:
                allowed = (diff >= 0) & (diff <= WINDOW)
            else:
                allowed = jnp.abs(diff) <= WINDOW
            NEG = jnp.float32(-1e+30)
            scores = jnp.where(allowed[None, None, :, :], scores, NEG)
            attn = jax.nn.softmax(scores, axis=-1)
            ctx = jnp.einsum('bhqk,bhkd->bhqd', attn, v)
            ctx = ctx.transpose(0, 2, 1, 3).reshape(B, T, D)
            out = jnp.einsum('btd,ed->bte', ctx, w_out) + b_out
            return x + out
        key = jax.random.key(seed)
        ks = jax.random.split(key, 5)
        B, T, D = (1, 512, 128)
        x = jax.random.normal(ks[0], (B, T, D), dtype=jnp.float32)
        w_in = jax.random.normal(ks[1], (3 * D, D), dtype=jnp.float32) * 0.02
        b_in = jax.random.normal(ks[2], (3 * D,), dtype=jnp.float32) * 0.02
        w_out = jax.random.normal(ks[3], (D, D), dtype=jnp.float32) * 0.02
        b_out = jax.random.normal(ks[4], (D,), dtype=jnp.float32) * 0.02
        return {'x': x, 'w_in': w_in, 'b_in': b_in, 'w_out': w_out, 'b_out': b_out}
    _L0_attn_in = _L0_attn_setup()

    def _L0_ffn_setup():
        import jax, jax.numpy as jnp
        import numpy as np
        B, S, IN, OUT = (4, 1024, 128, 128)
        EPS = 1e-06

        def _xla_quantized_matmul(x2d, weight_q, weight_scale):
            amax = jnp.max(jnp.abs(x2d), axis=-1, keepdims=True)
            x_scale = jnp.maximum(amax, EPS) / 127.0
            x_q = jnp.clip(jnp.round(x2d / x_scale), -128, 127).astype(jnp.int8)
            acc = jax.lax.dot_general(x_q, weight_q, (((1,), (1,)), ((), ())), preferred_element_type=jnp.int32)
            return acc.astype(jnp.float32) * x_scale * weight_scale[None, :]
        key = jax.random.key(seed)
        k1, k2, k3, k4 = jax.random.split(key, 4)
        x = jax.random.normal(k1, (B, S, IN), dtype=jnp.float32)
        weight_q = jax.random.randint(k2, (OUT, IN), -128, 128, dtype=jnp.int32).astype(jnp.int8)
        weight_scale = jax.random.uniform(k3, (OUT,), dtype=jnp.float32, minval=0.001, maxval=0.01)
        bias = jax.random.normal(k4, (OUT,), dtype=jnp.float32) * 0.01
        return {'x': x, 'weight_q': weight_q, 'weight_scale': weight_scale, 'bias': bias}
    _L0_ffn_in = _L0_ffn_setup()

    def _L1_attn_setup():
        import jax, jax.numpy as jnp
        import numpy as np
        D_MODEL = 128
        key = jax.random.key(seed)
        ks = jax.random.split(key, 7)
        B, S, D = (8, 256, D_MODEL)
        sc = 1.0 / np.sqrt(D)
        return {'inputs': jax.random.normal(ks[0], (B, S, D), dtype=jnp.float32), 'Wk': jax.random.normal(ks[1], (D, D), dtype=jnp.float32) * sc, 'bk': jax.random.normal(ks[2], (D,), dtype=jnp.float32) * 0.01, 'Wq': jax.random.normal(ks[3], (D, D), dtype=jnp.float32) * sc, 'bq': jax.random.normal(ks[4], (D,), dtype=jnp.float32) * 0.01, 'Wv': jax.random.normal(ks[5], (D, D), dtype=jnp.float32) * sc, 'bv': jax.random.normal(ks[6], (D,), dtype=jnp.float32) * 0.01}
    _L1_attn_in = _L1_attn_setup()

    def _L1_ffn_setup():
        import jax, jax.numpy as jnp
        import numpy as np
        DIM = 128
        HIDDEN = 256
        N_EXPERTS = 8
        TOP_K = 2
        EPS = 1e-06

        def rms_norm(x, scale, eps=EPS):
            ms = jnp.mean(jnp.square(x.astype(jnp.float32)), axis=-1, keepdims=True)
            s = scale.astype(jnp.float32) * jax.lax.rsqrt(ms + eps)
            return x * s.astype(x.dtype)

        def moe_linear(xf, ids, W):
            E = W.shape[0]
            out = jnp.zeros((xf.shape[0], W.shape[1]), dtype=xf.dtype)
            for e in range(E):
                out = out + jnp.where((ids == e)[:, None], xf @ W[e].T, 0.0)
            return out
        key = jax.random.key(seed)
        k1, k2, k3, k4 = jax.random.split(key, 4)
        x = jax.random.normal(k1, (4, 512, DIM), dtype=jnp.float32)
        norm_scale = jnp.ones((DIM,), dtype=jnp.float32)
        w_router = jax.random.normal(k2, (N_EXPERTS, DIM), dtype=jnp.float32) / np.sqrt(DIM)
        lim_up = np.sqrt(6.0 / (DIM + 2 * HIDDEN))
        w_up = jax.random.uniform(k3, (N_EXPERTS, 2 * HIDDEN, DIM), dtype=jnp.float32, minval=-lim_up, maxval=lim_up)
        lim_dn = np.sqrt(6.0 / (HIDDEN + DIM))
        w_down = jax.random.uniform(k4, (N_EXPERTS, DIM, HIDDEN), dtype=jnp.float32, minval=-lim_dn, maxval=lim_dn)
        return {'x': x, 'norm_scale': norm_scale, 'w_router': w_router, 'w_up': w_up, 'w_down': w_down}
    _L1_ffn_in = _L1_ffn_setup()
    _d = {'L0_attn_x': _L0_attn_in['x'], 'L0_attn_w_in': _L0_attn_in['w_in'], 'L0_attn_b_in': _L0_attn_in['b_in'], 'L0_attn_w_out': _L0_attn_in['w_out'], 'L0_attn_b_out': _L0_attn_in['b_out'], 'L0_ffn_weight_q': _L0_ffn_in['weight_q'], 'L0_ffn_weight_scale': _L0_ffn_in['weight_scale'], 'L0_ffn_bias': _L0_ffn_in['bias'], 'L1_attn_Wk': _L1_attn_in['Wk'], 'L1_attn_bk': _L1_attn_in['bk'], 'L1_attn_Wq': _L1_attn_in['Wq'], 'L1_attn_bq': _L1_attn_in['bq'], 'L1_attn_Wv': _L1_attn_in['Wv'], 'L1_attn_bv': _L1_attn_in['bv'], 'L1_ffn_norm_scale': _L1_ffn_in['norm_scale'], 'L1_ffn_w_router': _L1_ffn_in['w_router'], 'L1_ffn_w_up': _L1_ffn_in['w_up'], 'L1_ffn_w_down': _L1_ffn_in['w_down']}
    _x0 = _d['L0_attn_x']
    _d['L0_attn_x'] = jax.random.normal(jax.random.fold_in(jax.random.key(seed), 1), (8, 512, 128), dtype=_x0.dtype)
    del _x0
    return _d

def reference(L0_attn_x, L0_attn_w_in, L0_attn_b_in, L0_attn_w_out, L0_attn_b_out, L0_ffn_weight_q, L0_ffn_weight_scale, L0_ffn_bias, L1_attn_Wk, L1_attn_bk, L1_attn_Wq, L1_attn_bq, L1_attn_Wv, L1_attn_bv, L1_ffn_norm_scale, L1_ffn_w_router, L1_ffn_w_up, L1_ffn_w_down):

    def _L0_attn_ref(x, w_in, b_in, w_out, b_out):
        import jax, jax.numpy as jnp
        import numpy as np
        N_HEAD = 16
        WINDOW = 128
        CAUSAL = False

        def _window_attention(x, w_in, b_in, w_out, b_out):
            B, T, D = x.shape
            H = N_HEAD
            hd = D // H
            scale = 1.0 / jnp.sqrt(jnp.float32(hd))
            qkv = jnp.einsum('btd,ed->bte', x, w_in) + b_in
            q, k, v = jnp.split(qkv, 3, axis=-1)
            q = q.reshape(B, T, H, hd).transpose(0, 2, 1, 3)
            k = k.reshape(B, T, H, hd).transpose(0, 2, 1, 3)
            v = v.reshape(B, T, H, hd).transpose(0, 2, 1, 3)
            scores = jnp.einsum('bhqd,bhkd->bhqk', q, k) * scale
            idx = jnp.arange(T)
            diff = idx[:, None] - idx[None, :]
            if CAUSAL:
                allowed = (diff >= 0) & (diff <= WINDOW)
            else:
                allowed = jnp.abs(diff) <= WINDOW
            NEG = jnp.float32(-1e+30)
            scores = jnp.where(allowed[None, None, :, :], scores, NEG)
            attn = jax.nn.softmax(scores, axis=-1)
            ctx = jnp.einsum('bhqk,bhkd->bhqd', attn, v)
            ctx = ctx.transpose(0, 2, 1, 3).reshape(B, T, D)
            out = jnp.einsum('btd,ed->bte', ctx, w_out) + b_out
            return x + out
        return _window_attention(x, w_in, b_in, w_out, b_out)

    def _L0_ffn_ref(x, weight_q, weight_scale, bias):
        import jax, jax.numpy as jnp
        import numpy as np
        B, S, IN, OUT = (4, 1024, 128, 128)
        EPS = 1e-06

        def _xla_quantized_matmul(x2d, weight_q, weight_scale):
            amax = jnp.max(jnp.abs(x2d), axis=-1, keepdims=True)
            x_scale = jnp.maximum(amax, EPS) / 127.0
            x_q = jnp.clip(jnp.round(x2d / x_scale), -128, 127).astype(jnp.int8)
            acc = jax.lax.dot_general(x_q, weight_q, (((1,), (1,)), ((), ())), preferred_element_type=jnp.int32)
            return acc.astype(jnp.float32) * x_scale * weight_scale[None, :]
        orig_shape = x.shape
        x2d = x.reshape(-1, orig_shape[-1])
        out = _xla_quantized_matmul(x2d, weight_q, weight_scale)
        out = out.reshape(*orig_shape[:-1], out.shape[-1])
        out = out + bias
        return out

    def _L1_attn_ref(inputs, Wk, bk, Wq, bq, Wv, bv):
        import jax, jax.numpy as jnp
        import numpy as np
        D_MODEL = 128
        d = inputs.shape[-1]
        n = jnp.sqrt(jnp.asarray(d, dtype=jnp.float32))
        k = jnp.einsum('bsd,ed->bse', inputs, Wk) + bk
        q = jnp.einsum('bsd,ed->bse', inputs, Wq) + bq
        v = jnp.einsum('bsd,ed->bse', inputs, Wv) + bv
        scores = jnp.einsum('bqd,bkd->bqk', q, k) / n
        attn = jax.nn.softmax(scores, axis=1)
        out = jnp.einsum('bqk,bkd->bqd', attn, v) / n
        return out

    def _L1_ffn_ref(x, norm_scale, w_router, w_up, w_down):
        import jax, jax.numpy as jnp
        import numpy as np
        DIM = 128
        HIDDEN = 256
        N_EXPERTS = 8
        TOP_K = 2
        EPS = 1e-06

        def rms_norm(x, scale, eps=EPS):
            ms = jnp.mean(jnp.square(x.astype(jnp.float32)), axis=-1, keepdims=True)
            s = scale.astype(jnp.float32) * jax.lax.rsqrt(ms + eps)
            return x * s.astype(x.dtype)

        def moe_linear(xf, ids, W):
            E = W.shape[0]
            out = jnp.zeros((xf.shape[0], W.shape[1]), dtype=xf.dtype)
            for e in range(E):
                out = out + jnp.where((ids == e)[:, None], xf @ W[e].T, 0.0)
            return out
        B, S, D = x.shape
        skip = x
        xn = rms_norm(x, norm_scale)
        scores = (xn @ w_router.T).astype(jnp.float32)
        scores_topk, idx = jax.lax.top_k(scores, TOP_K)
        weights = jax.nn.softmax(scores_topk, axis=-1)
        xf = jnp.broadcast_to(xn[..., None, :], (B, S, TOP_K, D)).reshape(-1, D)
        ids = idx.reshape(-1)
        up = moe_linear(xf, ids, w_up)
        u, gate = jnp.split(up, 2, axis=-1)
        h = u * jax.nn.silu(gate)
        down = moe_linear(h, ids, w_down)
        down = down.reshape(B, S, TOP_K, D)
        out = jnp.sum(down * weights[..., None].astype(down.dtype), axis=-2)
        return out + skip
    x = L0_attn_x
    xn = _layernorm(x, axis=-1)
    x = x + _L0_attn_ref(xn, L0_attn_w_in, L0_attn_b_in, L0_attn_w_out, L0_attn_b_out) + _L0_ffn_ref(xn, L0_ffn_weight_q, L0_ffn_weight_scale, L0_ffn_bias)
    xn = _layernorm(x, axis=-1)
    x = x + _L1_attn_ref(xn, L1_attn_Wk, L1_attn_bk, L1_attn_Wq, L1_attn_bq, L1_attn_Wv, L1_attn_bv) + _L1_ffn_ref(xn, L1_ffn_norm_scale, L1_ffn_w_router, L1_ffn_w_up, L1_ffn_w_down)
    return x

_drawn_inputs = setup_inputs


def setup_inputs(seed=0):
    import zlib

    import numpy as np

    out = dict(_drawn_inputs(seed))
    spreads = {'L1_ffn_norm_scale': (1.0, 0.6)}
    factors = {'L0_attn_w_in': 8.0,
     'L0_attn_b_in': 8.0,
     'L0_attn_w_out': 8.0,
     'L0_attn_b_out': 8.0,
     'L0_ffn_bias': 25.61,
     'L1_attn_Wk': 8.0,
     'L1_attn_bk': 61.911,
     'L1_attn_Wq': 8.0,
     'L1_attn_bq': 200.0,
     'L1_attn_Wv': 8.0,
     'L1_attn_bv': 200.0}
    for name, (base, spread) in spreads.items():
        noise = np.random.default_rng([zlib.crc32(name.encode()), seed]).standard_normal(out[name].shape)
        drawn = base * np.exp(spread * noise) if base else spread * noise
        out[name] = jnp.asarray(drawn.astype(out[name].dtype))
    for name, factor in factors.items():
        out[name] = (out[name] * factor).astype(out[name].dtype)
    return out
```

```python
from contextlib import ExitStack

import concourse.bass as bass
from concourse import mybir

F32 = mybir.dt.float32
BF16 = mybir.dt.bfloat16
I32 = mybir.dt.int32
U32 = mybir.dt.uint32
ALU = mybir.AluOpType
ACT = mybir.ActivationFunctionType
AX = mybir.AxisListType

P = 128
NB = 8
T = 512
NT = T // P
H = 16
HD = P // H
HG = 4
STEPS = H // HG
UNITS = 2 * NT
SLOTS = STEPS * UNITS
MAGIC = 12582912.0
NEG = -1e30
QTERMS = (0, 0, 0, 1, 1, 2)
KTERMS = (0, 1, 2, 0, 1, 0)
NTERM = len(QTERMS)
MROW = NTERM * HD
NLOAD = 2 * 2 * NTERM + 2


def window(t):
    lo, hi = max(0, t - 1), min(NT, t + 2)
    return lo * P, (hi - lo) * P


def layer0(nc, ctx, x, w_inT, b_in, w_outT, b_out, wqT, wscale, fbias, x1_dram):
    parts_dram = nc.dram_tensor("parts_dram", [NB + 1, 2, 3, P, T], BF16).ap()
    base_dram = nc.dram_tensor("base_dram", [NB + 1, P, NT, P], F32).ap()

    def sb(name, shape, dt=F32):
        return ctx.enter_context(nc.sbuf_tensor(name, shape, dt))

    def sem(name):
        return ctx.enter_context(nc.semaphore(name))

    w_in = sb("w_in", [P, 3 * P])
    w_out = sb("w_out", [P, P])
    wq8 = sb("wq8", [P, P // 4], mybir.dt.int32)
    wq = sb("wq", [P, P], BF16)
    b_col = sb("b_col", [P, 2])
    bq_col = sb("bq_col", [P, 1])
    bv_row = sb("bv_row", [P, P])
    ws_row = sb("ws_row", [P, P])
    bo_row = sb("bo_row", [P, P])
    fb_row = sb("fb_row", [P, P])
    bsum_row = sb("bsum_row", [P, P])
    ident = sb("ident", [P, P])
    ident16 = sb("ident16", [P, P], BF16)
    mask_lo = sb("mask_lo", [P, P], BF16)
    mask_hi = sb("mask_hi", [P, P], BF16)
    mhalf = sb("mhalf", [P, NT])
    zrow = sb("zrow", [2, H // 2 * T], BF16)
    xb = sb("xb", [P, NT, P])
    stats = sb("stats", [P, NT, 6])
    mv = sb("mv", [P, NT, 2])
    veps = sb("veps", [P, NT])
    rstd = sb("rstd", [P, NT])
    xn = sb("xn", [P, NT, P])
    amax = sb("amax", [P, NT])
    xscale = sb("xscale", [P, NT])
    xrec = sb("xrec", [P, NT])
    t1 = sb("t1", [P, NT, P])
    t2 = sb("t2", [P, NT, P])
    xq = sb("xq", [P, NT, P], BF16)
    xqT = sb("xqT", [P, T], BF16)
    base0 = sb("base0", [P, NT, P])
    base1 = sb("base1", [P, NT, P])
    ffn = sb("ffn", [P, NT, P])
    base2 = sb("base2", [P, NT, P])
    base_r = sb("base_r", [P, NT, P])
    xnT = [sb(f"xnT{i}", [P, T]) for i in range(2)]
    qf, kf, rq, rk = (sb(n, [P, T]) for n in ("qf", "kf", "rq", "rk"))
    qp = sb("qp", [P, 3, T], BF16)
    kp = sb("kp", [P, 3, T], BF16)
    Qs = [sb(f"Qs{i}", [P, H // 2, T], BF16) for i in range(2)]
    Ks = [sb(f"Ks{i}", [P, H, T], BF16) for i in range(2)]
    Va = [sb(f"Va{i}", [P, NT, H, 32]) for i in range(2)]
    mneg = sb("mneg", [P, 2, NT * HG])
    mp = sb("mp", [P, 2, NT, 8], BF16)
    mT = sb("mT", [8, 2, T], BF16)
    Pb = sb("Pb", [P, NT, HG, 3 * P])
    cs = sb("cs", [P, HG, T])
    rec = sb("rec", [P, NT, H])
    ctxn = sb("ctxn", [P, NT, P])
    ctxT = sb("ctxT", [P, T])
    x1s = sb("x1s", [P, NT, P])

    A = [ctx.enter_context(nc.psum_tensor(f"A{i}", [P, 512], F32)) for i in range(2)]
    SB = [ctx.enter_context(nc.psum_tensor(f"SB{i}", [P, 2, 512], F32)) for i in range(2)]
    PV = ctx.enter_context(nc.psum_tensor("PV", [P, 512], F32))
    misc = ctx.enter_context(nc.psum_tensor("misc", [P, 512], F32))
    misc16 = misc[:, 0:256].bitcast(BF16)

    sp_passed, pool_passed, dve_passed = sem("sp_passed"), sem("pool_passed"), sem("dve_passed")
    names = """dma_w dma_x dma_base_r dma_base_w dma_pq dma_pk dma_stack dma_m dma_x1
    pool_const pool_zero pool_rs pool_ve pool_t1 pool_t2 pool_xq pool_b0 pool_b1 pool_b2 pool_rq pool_q3 pool_rk pool_k3
    pool_mask dve_const dve_bn dve_ag dve_xn dve_amax dve_xs dve_xr dve_ffn dve_max dve_mp dve_v dve_rec dve_ctx dve_x1
    act_bq act_xnT act_xqT act_qf act_q1 act_q2 act_kf act_k1 act_k2 act_exp act_pv act_mT act_ctxT
    pe_xnT pe_q pe_k pe_xqT pe_ffn pe_v pe_A pe_B pe_PV pe_mT pe_ctx pe_ctxT pe_out""".split()
    s = {n: sem(n) for n in names}
    (dma_w, dma_x, dma_base_r, dma_base_w, dma_pq, dma_pk, dma_stack, dma_m, dma_x1,
     pool_const, pool_zero, pool_rs, pool_ve, pool_t1, pool_t2, pool_xq, pool_b0, pool_b1, pool_b2,
     pool_rq, pool_q3, pool_rk, pool_k3,
     pool_mask, dve_const, dve_bn, dve_ag, dve_xn, dve_amax, dve_xs, dve_xr, dve_ffn, dve_max, dve_mp, dve_v,
     dve_rec, dve_ctx, dve_x1,
     act_bq, act_xnT, act_xqT, act_qf, act_q1, act_q2, act_kf, act_k1, act_k2, act_exp, act_pv, act_mT, act_ctxT,
     pe_xnT, pe_q, pe_k, pe_xqT, pe_ffn, pe_v, pe_A, pe_B, pe_PV, pe_mT, pe_ctx, pe_ctxT, pe_out) = (
        s[n] for n in names)

    NCONST = 8
    MASKS = (1, 3, 5, 6)
    NMASK = MASKS[-1]

    def batches(eng, body):
        body(0, 0, True, False)
        with eng.Fori(0, (NB - 2) // 2) as i:
            body(2 * i + 1, 1, False, False)
            body(2 * i + 2, 0, False, False)
        body(NB - 1, 1, False, True)

    block = ctx.enter_context(nc.Block())

    @block.sync
    def _(sp):
        def wait(sem, value):
            sp.wait_ge(sem, value)
            if not isinstance(value, int):
                sp.sem_inc(sp_passed)

        xv = x.rearrange("b (i p) d -> b p i d", p=P)
        x1v = x1_dram.rearrange("b (i p) d -> b p i d", p=P)

        def load_x(g):
            sp.dma_start(xb[:], xv[g]).then_inc(dma_x, 16)

        def store_parts(g, which):
            tile, done, ready = ((qp, dma_pq, pool_q3), (kp, dma_pk, pool_k3))[which]
            wait(ready, g + 1)
            sp.dma_start(parts_dram[g, which].rearrange("s e t -> e s t"), tile[:]).then_inc(done, 16)

        def load_stacks(g, pg):
            wait(dma_pq, 16 * (g + 1))
            wait(dma_pk, 16 * (g + 1))
            for par in range(2):
                for n in range(NTERM):
                    r0 = 64 * par + HD * n
                    for stack, which, part in ((Qs[pg][r0:r0 + HD, :, :], 0, QTERMS[n]),
                                               (Ks[pg][r0:r0 + HD, par:H:2, :], 1, KTERMS[n])):
                        src = parts_dram[g, which, part].rearrange("(a b d) t -> b d a t", b=2, d=HD)
                        sp.dma_start(stack, src[par]).then_inc(dma_stack, 16)
                r0 = 64 * par + MROW
                sp.dma_start(Qs[pg][r0:r0 + 2, :, :], zrow[:].rearrange("r (a t) -> r a t", t=T)).then_inc(dma_stack, 16)

        def place_max(step, hg, pg):
            wait(act_mT, step + 1)
            if not (isinstance(step, int) and step == 0):
                wait(dma_m, 32 * step)
            for par in range(2):
                r0 = 64 * par + MROW
                sp.dma_start(Qs[pg][r0:r0 + 2, 2 * hg:2 * hg + 2, :],
                             mT[4 * par:4 * par + 4, hg % 2, :]).then_inc(dma_m, 16)

        sp.dma_start(xb[:], xv[0]).then_inc(dma_x, 16)
        sp.dma_start(w_in[:], w_inT).then_inc(dma_w, 16)
        sp.dma_start(w_out[:], w_outT).then_inc(dma_w, 16)
        sp.dma_start(wq8[:], wqT).then_inc(dma_w, 16)
        sp.dma_start(b_col[:], b_in[0:2 * P].rearrange("(c p) -> p c", p=P),
                     allow_slow_non_contiguous=True).then_inc(dma_w, 16)
        for row, src in ((bv_row, b_in[2 * P:3 * P]), (ws_row, wscale), (bo_row, b_out), (fb_row, fbias)):
            sp.dma_start(row[:], src.partition_broadcast(P)).then_inc(dma_w, 16)
        wait(pool_zero, 9)
        store_parts(0, 0)
        store_parts(0, 1)
        load_stacks(0, 0)
        wait(pool_b0, 1)
        wait(dve_xn, 4)
        load_x(1)
        place_max(0, 0, 0)

        def body(b, p, first, last):
            o = 1 - p
            if not last:
                wait(pool_b0, b + 2)
                wait(dve_xn, NT * (b + 2))
                load_x((b + 2) % NB)
            if not first:
                wait(dma_base_w, 16 * b)
                sp.dma_start(base_r[:], base_dram[b - 1]).then_inc(dma_base_r, 16)
            if not last:
                store_parts(b + 1, 0)
            place_max(STEPS * b + 1, 1, p)
            if not last:
                store_parts(b + 1, 1)
                if not first:
                    wait(pe_B, SLOTS * b)
                load_stacks(b + 1, o)
            place_max(STEPS * b + 2, 2, p)
            if not first:
                wait(dve_x1, b)
                sp.dma_start(x1v[b - 1], x1s[:]).then_inc(dma_x1, 16)
            place_max(STEPS * b + 3, 3, p)
            if not last:
                wait(pool_b2, b + 3)
                sp.dma_start(base_dram[b + 2], base2[:]).then_inc(dma_base_w, 16)
                place_max(STEPS * b + 4, 0, o)

        wait(pool_b2, 1)
        sp.dma_start(base_dram[0], base2[:]).then_inc(dma_base_w, 16)
        wait(pool_b2, 2)
        sp.dma_start(base_dram[1], base2[:]).then_inc(dma_base_w, 16)
        batches(sp, body)
        wait(dve_x1, NB - 1)
        sp.dma_start(base_r[:], base_dram[NB - 1]).then_inc(dma_base_r, 16)
        wait(dve_x1, NB)
        sp.dma_start(x1v[NB - 1], x1s[:]).then_inc(dma_x1, 16)
        wait(dma_x1, 16 * NB)
        wait(dma_base_w, 16 * (NB + 1))
        wait(dma_stack, 16 * NLOAD * NB)

    @block.gpsimd
    def _(pool):
        def wait(sem, value):
            pool.wait_ge(sem, value)
            if not isinstance(value, int):
                pool.sem_inc(pool_passed)

        pool.memset(ident[:], 0.0).then_inc(pool_const, 1)
        pool.memset(ident16[:], 0.0).then_inc(pool_const, 1)
        pool.memset(mask_lo[:], 0.0).then_inc(pool_const, 1)
        pool.memset(mask_hi[:], 0.0).then_inc(pool_const, 1)
        pool.memset(mhalf[:], -0.5).then_inc(pool_const, 1)
        wait(pool_const, 5)
        for m in (ident, ident16):
            pool.affine_select(out=m[:], in_=m[:], compare_op=ALU.not_equal, fill=1.0, base=0,
                               pattern=[[-1, P]], channel_multiplier=1).then_inc(pool_const, 1)
        pool.affine_select(out=mask_lo[:], in_=mask_lo[:], compare_op=ALU.is_ge, fill=NEG, base=0,
                           pattern=[[1, P]], channel_multiplier=-1).then_inc(pool_const, 1)
        pool.affine_select(out=mask_hi[:], in_=mask_hi[:], compare_op=ALU.is_ge, fill=NEG, base=0,
                           pattern=[[-1, P]], channel_multiplier=1).then_inc(pool_const, 1)
        pool.memset(zrow[:], 0.0).then_inc(pool_zero, 1)
        n = 1
        for i in range(2):
            for view, value in ((Qs[i][:].bitcast(F32), 0.0), (Ks[i][:].bitcast(F32), 0.0),
                                (Ks[i][32:64, 0:H:2, :], 1.0), (Ks[i][96:128, 1:H:2, :], 1.0)):
                wait(pool_zero, n)
                pool.memset(view, value).then_inc(pool_zero, 1)
                n += 1
        wait(pool_zero, n)

        def rstd_of(g):
            wait(dve_ag, NT * (g + 1))
            pool.tensor_scalar(veps[:], mv[:, :, 1], 1e-5, None, ALU.add).then_inc(pool_ve, 1)
            wait(pool_ve, g + 1)
            pool.tensor_tensor(rstd[:], veps[:], mhalf[:], ALU.pow).then_inc(pool_rs, 1)

        def base_x(g):
            wait(dve_xn, NT * (g + 1))
            pool.tensor_tensor(base0[:], xb[:], xn[:], ALU.add).then_inc(pool_b0, 1)

        def quant_scale(g):
            wait(dve_xr, g + 1)
            for i in range(NT):
                pool.tensor_scalar(t1[:, i, :], xn[:, i, :], xrec[:, i:i + 1], MAGIC, ALU.mult, ALU.add)\
                    .then_inc(pool_t1, 1)

        def quant_clip(g):
            wait(pool_t1, NT * (g + 1))
            pool.tensor_scalar(t2[:], t1[:], MAGIC - 128, MAGIC + 127, ALU.max, ALU.min).then_inc(pool_t2, 1)

        def quant_int(g):
            wait(pool_t2, g + 1)
            if not (isinstance(g, int) and g == 0):
                wait(pe_xqT, g)
            pool.tensor_scalar(xq[:], t2[:], MAGIC, None, ALU.subtract).then_inc(pool_xq, 1)

        def base_bias(g):
            wait(pool_b0, g + 1)
            pool.tensor_tensor(base1[:], base0[:], bsum_row[:].unsqueeze(1).to_broadcast([P, NT, P]), ALU.add)\
                .then_inc(pool_b1, 1)

        def base_ffn(g):
            wait(pool_b1, g + 1)
            wait(dve_ffn, NT * (g + 1))
            if not (isinstance(g, int) and g == 0):
                wait(dma_base_w, 16 * g)
            pool.tensor_tensor(base2[:], base1[:], ffn[:], ALU.add).then_inc(pool_b2, 1)

        def rest(g, which):
            full, tile, out, done, first_part, last_part, n = (
                (qf, qp, rq, pool_rq, act_q1, pool_q3, act_qf), (kf, kp, rk, pool_rk, act_k1, pool_k3, act_kf))[which]
            wait(n, g + 1)
            wait(first_part, g + 1)
            pool.tensor_tensor(out[:], full[:], tile[:, 0, :], ALU.subtract).then_inc(done, 1)

        def third(g, which):
            tile, r, done, second, last = ((qp, rq, pool_q3, act_q2, dma_pq), (kp, rk, pool_k3, act_k2, dma_pk))[which]
            wait(second, g + 1)
            if not (isinstance(g, int) and g == 0):
                wait(last, 16 * g)
            pool.tensor_tensor(tile[:, 2, :], r[:], tile[:, 1, :], ALU.subtract).then_inc(done, 1)

        def masks(b, hg, kt):
            wait(act_exp, SLOTS * b + UNITS * hg + 2 * kt + 2)
            if kt > 0:
                blk = Pb[:, kt, :, 0:P]
                pool.affine_select(out=blk, in_=blk, compare_op=ALU.is_ge, fill=0.0, base=0,
                                   pattern=[[0, HG], [1, P]], channel_multiplier=-1).then_inc(pool_mask, 1)
            if kt < NT - 1:
                w = window(kt)[1]
                blk = Pb[:, kt, :, w - P:w]
                pool.affine_select(out=blk, in_=blk, compare_op=ALU.is_ge, fill=0.0, base=0,
                                   pattern=[[0, HG], [-1, P]], channel_multiplier=1).then_inc(pool_mask, 1)

        for g in range(2):
            rstd_of(g)
            base_x(g)
            quant_scale(g)
            quant_clip(g)
            quant_int(g)
            if g == 0:
                wait(dve_const, 2)
            base_bias(g)
            rest(g, 0)
            if g == 0:
                rest(g, 1)
                third(g, 0)
                third(g, 1)
            else:
                third(g, 0)
                rest(g, 1)
            base_ffn(g)

        def body(b, p, first, last):
            g = b + 2
            for u in range(SLOTS):
                if not last:
                    if u == 1:
                        third(b + 1, 1)
                    if u == 12:
                        rstd_of(g)
                    if u == 14:
                        base_x(g)
                    if u == 16:
                        quant_scale(g)
                    if u == 18:
                        quant_clip(g)
                    if u == 19:
                        quant_int(g)
                    if u == 22:
                        base_bias(g)
                    if u == 24:
                        base_ffn(g)
                    if u == 29:
                        rest(g, 0)
                    if u == 31:
                        third(g, 0)
                if u % 2 == 1:
                    masks(b, u // UNITS, (u % UNITS) // 2)
            if not last:
                rest(g, 1)

        batches(pool, body)

    @block.scalar
    def _(act):
        act.wait_ge(dma_w, 16 * NCONST)
        SC = float(HD) ** -0.5
        act.activation(bq_col[:], b_col[:, 0:1], ACT.Copy, scale=SC).then_inc(act_bq, 1)

        def evac_xnT(g, pg):
            act.wait_ge(pe_xnT, g + 1)
            act.activation(xnT[pg][:], misc[:], ACT.Copy).then_inc(act_xnT, 1)

        def evac_q(g):
            act.wait_ge(pe_q, g + 1)
            if isinstance(g, int) and g == 0:
                act.wait_ge(act_bq, 1)
            else:
                act.wait_ge(pool_rq, g)
                act.wait_ge(dma_pq, 16 * g)
            act.activation(qf[:], misc[:], ACT.Identity, bias=bq_col[:, 0:1], scale=SC).then_inc(act_qf, 1)
            act.activation(qp[:, 0, :], misc[:], ACT.Identity, bias=bq_col[:, 0:1], scale=SC).then_inc(act_q1, 1)

        def evac_k(g):
            act.wait_ge(pe_k, g + 1)
            if not (isinstance(g, int) and g == 0):
                act.wait_ge(pool_rk, g)
                act.wait_ge(dma_pk, 16 * g)
            act.activation(kf[:], misc[:], ACT.Identity, bias=b_col[:, 1:2]).then_inc(act_kf, 1)
            act.activation(kp[:, 0, :], misc[:], ACT.Identity, bias=b_col[:, 1:2]).then_inc(act_k1, 1)

        def second(g, which):
            tile, r, need, done = ((qp, rq, pool_rq, act_q2), (kp, rk, pool_rk, act_k2))[which]
            act.wait_ge(need, g + 1)
            act.activation(tile[:, 1, :], r[:], ACT.Copy).then_inc(done, 1)

        def evac_xqT(g):
            act.wait_ge(pe_xqT, g + 1)
            act.activation(xqT[:], misc16, ACT.Copy).then_inc(act_xqT, 1)

        def evac_mT(step, hg):
            act.wait_ge(pe_mT, step + 1)
            if not (isinstance(step, int) and step < 2):
                act.wait_ge(dma_m, 32 * (step - 1))
            act.activation(mT[:, hg % 2, :], misc16[0:8, :], ACT.Copy).then_inc(act_mT, 1)

        def exp(b, u):
            hg, kt, half = u // UNITS, (u % UNITS) // 2, u % 2
            w = window(kt)[1]
            act.wait_ge(pe_B, SLOTS * b + u + 1)
            if not (isinstance(b, int) and b == 0 and hg == 0) and half == 0:
                act.wait_ge(pe_PV, NT * (STEPS * b + hg - 1) + kt + 1)
            act.activation(Pb[:, kt, 2 * half:2 * half + 2, 0:w], SB[u % 2][:, :, 0:w], ACT.Exp).then_inc(act_exp, 1)

        def evac_pv(step, hg):
            act.wait_ge(pe_PV, NT * (step + 1))
            if hg == 0 and not (isinstance(step, int) and step == 0):
                act.wait_ge(pe_ctx, step)
            act.activation(cs[:, hg, :], PV[:], ACT.Copy).then_inc(act_pv, 1)

        def evac_ctxT(g):
            act.wait_ge(pe_ctxT, g + 1)
            act.activation(ctxT[:], misc[:], ACT.Copy).then_inc(act_ctxT, 1)

        evac_xnT(0, 0)
        evac_q(0)
        evac_k(0)
        evac_xqT(0)
        second(0, 0)
        second(0, 1)
        evac_mT(0, 0)
        evac_xnT(1, 1)
        evac_xqT(1)
        evac_q(1)
        second(1, 0)
        evac_k(1)

        def body(b, p, first, last):
            for u in range(SLOTS):
                exp(b, u)
                if u == 1 and not last:
                    second(b + 1, 1)
                if u % UNITS == 2 and not (first and u == 2):
                    evac_pv(STEPS * b + u // UNITS - 1, (u // UNITS - 1) % STEPS)
                if u % UNITS == 2 and not (last and u // UNITS == STEPS - 1):
                    evac_mT(STEPS * b + u // UNITS + 1, (u // UNITS + 1) % STEPS)
                if u == 9 and not first:
                    evac_ctxT(b - 1)
                if not last:
                    if u == 20:
                        evac_xqT(b + 2)
                    if u == 24:
                        evac_xnT(b + 2, p)
                    if u == 28:
                        evac_q(b + 2)
                    if u == 30:
                        second(b + 2, 0)
                    if u == 31:
                        evac_k(b + 2)

        batches(act, body)
        evac_pv(STEPS * NB - 1, STEPS - 1)
        evac_ctxT(NB - 1)

    @block.vector
    def _(dve):
        dve.wait_ge(dma_w, 16 * NCONST)
        nc.vector.tensor_copy(wq[:], wq8[:].bitcast(mybir.dt.int8)).then_inc(dve_const, 1)
        nc.vector.tensor_tensor(bsum_row[:], bo_row[:], fb_row[:], ALU.add).then_inc(dve_const, 1)
        for va in Va:
            nc.vector.memset(va[:], 0.0).then_inc(dve_const, 1)
        dve.wait_ge(dve_const, 4)
        for va in Va:
            nc.vector.memset(va[:, :, :, HD:HD + 1], 1.0).then_inc(dve_const, 1)

        def bn(g, tiles):
            dve.wait_ge(dma_x, 16 * (g + 1))
            for i in tiles:
                nc.vector.bn_stats(stats[:, i, :], xb[:, i, :]).then_inc(dve_bn, 1)

        def ag(g):
            for i in range(NT):
                dve.wait_ge(dve_bn, NT * g + i + 1)
                if not isinstance(g, int):
                    dve.sem_inc(dve_passed)
                nc.vector.bn_aggr(mv[:, i, :], stats[:, i, :]).then_inc(dve_ag, 1)

        def norm(g):
            dve.wait_ge(pool_rs, g + 1)
            if not (isinstance(g, int) and g == 0):
                dve.wait_ge(pe_xnT, g)
                dve.wait_ge(pool_t1, NT * g)
            for i in range(NT):
                nc.vector.tensor_scalar(xn[:, i, :], xb[:, i, :], mv[:, i, 0:1], rstd[:, i:i + 1],
                                        ALU.subtract, ALU.mult).then_inc(dve_xn, 1)

        def absmax(g):
            dve.wait_ge(dve_xn, NT * (g + 1))
            nc.vector.tensor_reduce(amax[:], xn[:], AX.X, ALU.max, apply_absolute_value=True).then_inc(dve_amax, 1)

        def scales(g):
            dve.wait_ge(dve_amax, g + 1)
            if not (isinstance(g, int) and g == 0):
                dve.wait_ge(dve_ffn, NT * g)
            nc.vector.tensor_scalar(xscale[:], amax[:], 1e-6, 1.0 / 127.0, ALU.max, ALU.mult).then_inc(dve_xs, 1)
            dve.wait_ge(dve_xs, g + 1)
            nc.vector.reciprocal(xrec[:], xscale[:]).then_inc(dve_xr, 1)

        def ffn_out(g):
            dve.wait_ge(pe_ffn, g + 1)
            if not (isinstance(g, int) and g == 0):
                dve.wait_ge(pool_b2, g)
            for i in range(NT):
                nc.vector.scalar_tensor_tensor(ffn[:, i, :], misc[:, i * P:(i + 1) * P], xscale[:, i:i + 1],
                                               ws_row[:], ALU.mult, ALU.mult).then_inc(dve_ffn, 1)

        def evac_v(g, pg):
            dve.wait_ge(pe_v, g + 1)
            if isinstance(g, int) and g == 0:
                dve.wait_ge(dve_const, 6)
            elif not (isinstance(g, int) and g == 1):
                dve.wait_ge(pe_PV, STEPS * NT * (g - 1))
            nc.vector.tensor_tensor(Va[pg][:, :, :, 0:HD], misc[:].rearrange("p (i h d) -> p i h d", i=NT, d=HD),
                                    bv_row[:].rearrange("p (h d) -> p h d", d=HD).unsqueeze(1)
                                    .to_broadcast([P, NT, H, HD]), ALU.add).then_inc(dve_v, 1)

        def maxima(step, u):
            for n in (2 * u, 2 * u + 1):
                qb = n // HG
                piece = 16 * step + n
                dve.wait_ge(pe_A, piece + 1)
                par = step_par(step)
                nc.vector.tensor_reduce(mneg[:, par, n:n + 1], A[n % 2][:, 0:window(qb)[1]], AX.X, ALU.max,
                                        negate=True).then_inc(dve_max, 1)

        def step_par(step):
            return cur[0]

        cur = [0]

        def max_parts(step, par):
            dve.wait_ge(dve_max, 16 * (step + 1))
            if not (isinstance(step, int) and step < 2):
                dve.wait_ge(pe_mT, step - 1)
            src = mneg[:, par, :].rearrange("p (q a b) -> p q b a", a=2, b=2)
            dst = mp[:, par, :, :].rearrange("p q (b s a) -> p q b s a", b=2, s=2)
            nc.vector.tensor_copy(dst[:, :, :, 0, :], src).then_inc(dve_mp, 1)
            dve.wait_ge(dve_mp, 2 * step + 1)
            nc.vector.tensor_tensor(dst[:, :, :, 1, :], src, dst[:, :, :, 0, :], ALU.subtract).then_inc(dve_mp, 1)

        def context(g, qb):
            v = misc[:].rearrange("p (h w) -> p h w", w=32)
            dve.wait_ge(pe_ctx, NT * g + qb + 1)
            nc.vector.reciprocal(rec[:, qb, :], v[:, :, HD:HD + 1].rearrange("p h w -> p (h w)")).then_inc(dve_rec, 1)
            dve.wait_ge(dve_rec, NT * g + qb + 1)
            nc.vector.tensor_tensor(ctxn[:, qb, :].rearrange("p (h d) -> p h d", d=HD), v[:, :, 0:HD],
                                    rec[:, qb, :].unsqueeze(2).to_broadcast([P, H, HD]), ALU.mult).then_inc(dve_ctx, 1)

        def out_x1(g):
            dve.wait_ge(pe_out, g + 1)
            dve.wait_ge(dma_base_r, 16 * (g + 1))
            nc.vector.tensor_tensor(x1s[:].rearrange("p i d -> p (i d)"), misc[:],
                                    base_r[:].rearrange("p i d -> p (i d)"), ALU.add).then_inc(dve_x1, 1)

        def pre(g):
            bn(g, range(NT))
            ag(g)
            norm(g)
            absmax(g)
            scales(g)

        pre(0)
        ffn_out(0)
        evac_v(0, 0)
        pre(1)
        cur[0] = 0
        for u in range(UNITS):
            maxima(0, u)
        max_parts(0, 0)
        ffn_out(1)
        cur[0] = 1
        for u in range(UNITS):
            maxima(1, u)

        def body(b, p, first, last):
            for u in range(SLOTS):
                hg = u // UNITS
                step = STEPS * b + hg
                if u % UNITS == 0 and not (last and hg == STEPS - 1):
                    max_parts(step + 1, (hg + 1) % 2)
                if not (last and hg >= 2):
                    cur[0] = hg % 2
                    maxima(step + 2, u % UNITS)
                if u == 3 and not last:
                    evac_v(b + 1, 1 - p)
                if 4 <= u < 8 and not first:
                    context(b - 1, u - 4)
                if u == 12 and not first:
                    out_x1(b - 1)
                if not last:
                    if u in (8, 9):
                        bn(b + 2, range(2 * (u - 8), 2 * (u - 8) + 2))
                    if u == 10:
                        ag(b + 2)
                    if u == 13:
                        norm(b + 2)
                    if u == 14:
                        absmax(b + 2)
                    if u == 15:
                        scales(b + 2)
                    if u == 22:
                        ffn_out(b + 2)
            if not first:
                dve.wait_ge(dma_x1, 16 * b)

        batches(dve, body)
        for qb in range(NT):
            context(NB - 1, qb)
        out_x1(NB - 1)

    @block.tensor
    def _(pe):
        def turn_xn(g, pg):
            pe.wait_ge(dve_xn, NT * (g + 1))
            for i in range(NT):
                mm = nc.tensor.transpose(misc[:, i * P:(i + 1) * P], xn[:, i, :], ident[:])
            mm.then_inc(pe_xnT, 1)

        def project(g, pg, which, done, before):
            pe.wait_ge(act_xnT, g + 1)
            pe.wait_ge(*before)
            nc.tensor.matmul(misc[:], w_in[:, which * P:(which + 1) * P], xnT[pg][:], start=True, stop=True)\
                .then_inc(done, 1)

        def values(g, pg):
            pe.wait_ge(act_k1, g + 1)
            for i in range(NT):
                mm = nc.tensor.matmul(misc[:, i * P:(i + 1) * P], xnT[pg][:, i * P:(i + 1) * P],
                                      w_in[:, 2 * P:3 * P], start=True, stop=True)
            mm.then_inc(pe_v, 1)

        def turn_xq(g, before):
            pe.wait_ge(pool_xq, g + 1)
            pe.wait_ge(*before)
            for i in range(NT):
                mm = nc.tensor.transpose(misc16[:, i * P:(i + 1) * P], xq[:, i, :], ident16[:])
            mm.then_inc(pe_xqT, 1)

        def ffn_mm(g):
            pe.wait_ge(act_xqT, g + 1)
            for i in range(NT):
                mm = nc.tensor.matmul(misc[:, i * P:(i + 1) * P], xqT[:, i * P:(i + 1) * P], wq[:],
                                      start=True, stop=True)
            mm.then_inc(pe_ffn, 1)

        def piece(step, n, hgs, pg):
            qb, h = n // HG, HG * hgs + n % HG
            lo, w = window(qb)
            idx = 16 * step + n
            if not (isinstance(step, int) and step == 0 and n < 2):
                pe.wait_ge(dve_max, idx - 1)
            out = A[n % 2]
            nc.tensor.matmul(out[:, 0:w], Qs[pg][:, h // 2, qb * P:(qb + 1) * P], Ks[pg][:, h, lo:lo + w],
                             start=True, stop=True)
            if qb > 0:
                mm = nc.tensor.matmul(out[:, 0:P], ident16[:], mask_lo[:], start=False, stop=True,
                                      skip_group_check=True)
            if qb < NT - 1:
                mm = nc.tensor.matmul(out[:, w - P:w], ident16[:], mask_hi[:], start=False, stop=True,
                                      skip_group_check=True)
            mm.then_inc(pe_A, 1)

        def turn_max(step, par, before):
            pe.wait_ge(dve_mp, 2 * (step + 1))
            pe.wait_ge(*before)
            for qb in range(NT):
                mm = nc.tensor.transpose(misc16[0:8, qb * P:(qb + 1) * P], mp[:, par, qb, :], ident16[:])
            mm.then_inc(pe_mT, 1)

        def scores(b, u, p):
            hg, kt, half = u // UNITS, (u % UNITS) // 2, u % 2
            lo, w = window(kt)
            if u % UNITS == 0:
                pe.wait_ge(dma_m, 32 * (STEPS * b + hg + 1))
            if not (isinstance(b, int) and b == 0 and u < 2):
                pe.wait_ge(act_exp, SLOTS * b + u - 1)
            for j in range(2):
                h = HG * hg + 2 * half + j
                mm = nc.tensor.matmul(SB[u % 2][:, j, 0:w], Ks[p][:, h, kt * P:(kt + 1) * P],
                                      Qs[p][:, h // 2, lo:lo + w], start=True, stop=True)
            mm.then_inc(pe_B, 1)

        def attend(step, hg, kt, p):
            pe.wait_ge(pool_mask, NMASK * step + MASKS[kt])
            if kt == 0 and not (isinstance(step, int) and step == 0):
                pe.wait_ge(act_pv, step)
            lo, w = window(kt)
            for c in range(HG):
                mm = nc.tensor.matmul(PV[32 * c:32 * c + 32, lo:lo + w], Va[p][:, kt, HG * hg + c, :],
                                      Pb[:, kt, c, 0:w], start=kt == 0, stop=True, skip_group_check=True,
                                      tile_position=(0, 32 * c))
            mm.then_inc(pe_PV, 1)

        def turn_ctx(g, qb, before):
            pe.wait_ge(act_pv, STEPS * (g + 1))
            pe.wait_ge(*before)
            for hg in range(STEPS):
                mm = nc.tensor.transpose(misc[:, hg * P:(hg + 1) * P], cs[:, hg, qb * P:(qb + 1) * P], ident[:])
            mm.then_inc(pe_ctx, 1)

        def turn_ctxn(g):
            pe.wait_ge(dve_ctx, NT * (g + 1))
            for qb in range(NT):
                mm = nc.tensor.transpose(misc[:, qb * P:(qb + 1) * P], ctxn[:, qb, :], ident[:])
            mm.then_inc(pe_ctxT, 1)

        def out_mm(g, before):
            pe.wait_ge(act_ctxT, g + 1)
            pe.wait_ge(*before)
            for i in range(NT):
                mm = nc.tensor.matmul(misc[:, i * P:(i + 1) * P], ctxT[:, i * P:(i + 1) * P], w_out[:],
                                      start=True, stop=True)
            mm.then_inc(pe_out, 1)

        pe.wait_ge(pool_const, 9)
        pe.wait_ge(dma_w, 16 * NCONST)
        pe.wait_ge(dve_const, 1)
        turn_xn(0, 0)
        project(0, 0, 0, pe_q, (act_xnT, 1))
        project(0, 0, 1, pe_k, (act_q1, 1))
        turn_xq(0, (act_k1, 1))
        ffn_mm(0)
        pe.wait_ge(dve_ffn, NT)
        values(0, 0)
        pe.wait_ge(dma_stack, 16 * NLOAD)
        for n in range(16):
            piece(0, n, 0, 0)
        turn_max(0, 0, (dve_v, 1))
        pe.wait_ge(act_mT, 1)
        turn_xn(1, 1)
        turn_xq(1, (act_xnT, 2))
        ffn_mm(1)
        project(1, 1, 0, pe_q, (dve_ffn, 2 * NT))
        project(1, 1, 1, pe_k, (act_q1, 2))
        for n in range(16):
            piece(1, n, 1, 0)

        def body(b, p, first, last):
            o = 1 - p
            for u in range(SLOTS):
                hg, v = u // UNITS, u % UNITS
                step = STEPS * b + hg
                scores(b, u, p)
                if not (last and hg >= 2):
                    if u == 2 * UNITS:
                        pe.wait_ge(dma_stack, 16 * NLOAD * (b + 2))
                    for n in (2 * v, 2 * v + 1):
                        piece(step + 2, n, (hg + 2) % STEPS, p if hg < 2 else o)
                if u == 2:
                    turn_max(step + 1, 1, (act_k1, b + 2) if not last else (act_k1, b + 1))
                elif u == 10:
                    turn_max(step + 1, 0, (act_ctxT, b) if not first else (act_mT, step + 1))
                elif u == 18:
                    turn_max(step + 1, 1, (dve_x1, b) if not first else (act_mT, step + 1))
                elif u == 26 and not last:
                    turn_max(step + 1, 0, (act_xnT, b + 3))
                if u == 3 and not last:
                    pe.wait_ge(act_mT, STEPS * b + 2)
                    values(b + 1, o)
                if not first:
                    if 4 <= u < 8:
                        turn_ctx(b - 1, u - 4, ((dve_v, b + 2) if not last else (act_mT, STEPS * b + 2))
                                 if u == 4 else (dve_ctx, NT * (b - 1) + u - 4))
                    if u == 9:
                        turn_ctxn(b - 1)
                    if u == 11:
                        out_mm(b - 1, (act_mT, STEPS * b + 3))
                if not last:
                    if u == 20:
                        turn_xq(b + 2, (act_mT, STEPS * b + 4))
                    if u == 22:
                        ffn_mm(b + 2)
                    if u == 24:
                        pe.wait_ge(dve_ffn, NT * (b + 3))
                        turn_xn(b + 2, p)
                    if u == 28:
                        project(b + 2, p, 0, pe_q, (act_mT, STEPS * b + 5))
                    if u == 30:
                        project(b + 2, p, 1, pe_k, (act_q1, b + 3))
                if v == 1 and not (first and hg == 0):
                    attend(step - 1, (hg - 1) % STEPS, NT - 1, p if hg else o)
                elif v >= 3 and v % 2 == 1:
                    attend(step, hg, (v - 3) // 2, p)

        batches(pe, body)
        attend(STEPS * NB - 1, STEPS - 1, NT - 1, 1)
        for qb in range(NT):
            turn_ctx(NB - 1, qb, (act_mT, STEPS * NB) if qb == 0 else (dve_ctx, NT * (NB - 1) + qb))
        turn_ctxn(NB - 1)
        out_mm(NB - 1, (act_ctxT, NB))


NE = 8
HID = 256
TOPK = 2
TOKENS = NB * T
ROW = P + 2
CAP = TOKENS + P
NTILES = -(-(TOKENS * TOPK + NE * (P - 1)) // P // 8) * 8


def layer1(nc, ctx, x1, WqT, bq, WkT, bk, WvT, bv, nscale, wrT, xs, x2b, tab, w_up, w_dn, w_up_in, w_dn_in):

    def sb(name, shape, dt=F32):
        return ctx.enter_context(nc.sbuf_tensor(name, shape, dt))

    def sem(name):
        return ctx.enter_context(nc.semaphore(name))

    wq, wk, wv = (sb(n, [P, P]) for n in ("l1_wq", "l1_wk", "l1_wv"))
    bqc, bqs, bkc, nsc = (sb(n, [P, 1]) for n in ("l1_bq", "l1_bqs", "l1_bk", "l1_ns"))
    bvr = sb("l1_bv", [P, P])
    nsr = sb("l1_nsr", [P, P])
    wr = sb("l1_wr", [P, NE])
    wrs = sb("l1_wrs", [P, NE])
    ident = sb("l1_ident", [P, P])
    tri = sb("l1_tri", [P, P], BF16)
    ones = sb("l1_ones", [P, P], BF16)
    mhalf = sb("l1_mhalf", [P, NT])
    iota8i = sb("iota8i", [P, NE], I32)
    iota8 = sb("iota8", [P, NE])
    ebase = sb("ebase", [P, NE])
    dest_i = sb("dest_i", [P, NT * TOPK], I32)
    dest = sb("dest", [P, NT * TOPK])
    part_i = sb("part_i", [P, 1], I32)
    part_f = sb("part_f", [P, 1])
    tile_i = sb("tile_i", [1, NTILES], I32)
    tile_f = sb("tile_f", [1, NTILES])
    nine_i = sb("nine_i", [1, NE + 1], I32)
    nine_f = sb("nine_f", [1, NE + 1])
    upto = sb("upto", [1, NE, NE])
    padrow = sb("padrow", [P, ROW])

    xb = [sb(f"l1_xb{i}", [P, NT, P]) for i in range(2)]
    stats = sb("l1_stats", [P, NT, 6])
    mv = sb("l1_mv", [P, NT, 2])
    veps = sb("l1_veps", [P, NT])
    rstd = sb("l1_rstd", [P, NT])
    xn = [sb(f"l1_xn{i}", [P, NT, P]) for i in range(2)]
    junk = sb("l1_junk", [P, NT, P])
    ssq = sb("l1_ssq", [P, NT])
    meps = sb("l1_meps", [P, NT])
    rr = [sb(f"l1_rr{i}", [P, NT]) for i in range(2)]
    base = [sb(f"l1_base{i}", [P, NT, P]) for i in range(2)]
    xnT = sb("l1_xnT", [P, T])
    qT = [sb(f"l1_qT{i}", [P, T]) for i in range(2)]
    kT = [sb(f"l1_kT{i}", [P, T]) for i in range(2)]
    v = [sb(f"l1_v{i}", [P, NT, P]) for i in range(2)]
    mneg = sb("l1_mneg", [P, NT])
    ssum = sb("l1_ssum", [P, NT])
    srec = sb("l1_srec", [P, NT])
    vs = sb("l1_vs", [P, NT, P])
    pr = sb("l1_pr", [P, NT, T])
    sc = sb("sc", [P, NT, NE])
    mx = sb("mx", [P, NT, NE])
    ix = sb("ix", [P, NT, NE], U32)
    ixf = sb("ixf", [P, NT, NE])
    oh = [sb(f"oh{i}", [P, NT, TOPK, NE]) for i in range(2)]
    dm = sb("dm", [P, NT])
    em = sb("em", [P, NT])
    den = sb("den", [P, NT])
    w1 = sb("w1", [P, NT])
    w2 = sb("w2", [P, NT])
    M = [sb(f"M{i}", [P, NT, NE], BF16) for i in range(2)]
    S = [sb(f"S{i}", [P, NE], BF16) for i in range(2)]
    msum = sb("msum", [P, NE])
    Re = sb("Re", [P, NT, NE])
    prod = sb("prod", [P, NT, TOPK, NE])
    posf = sb("posf", [P, NT, TOPK])
    pos = [sb(f"pos{i}", [P, NT, TOPK], U32) for i in range(2)]
    pay = [sb(f"pay{i}", [P, TOPK, NT, ROW]) for i in range(2)]
    cnt = sb("cnt", [P, NE])
    padp = sb("padp", [P, NE])
    padi = sb("padi", [P, NE], U32)
    nt_a = sb("nt_a", [P, NE])
    nt_f = sb("nt_f", [P, NE])
    cprod = sb("cprod", [1, NE, NE])
    cum = sb("cum", [1, NE])
    vals = sb("vals", [1, NE + 1])
    cx = sb("cx", [1, NE])
    le = sb("le", [1, NTILES, NE])
    et = sb("et", [1, NTILES])
    oh9 = sb("oh9", [1, NTILES, NE + 1])
    pv9 = sb("pv9", [1, NTILES, NE + 1])
    bt = sb("bt", [1, NTILES])
    bt2 = sb("bt2", [1, NTILES])

    Sb = [ctx.enter_context(nc.psum_tensor(f"l1_S{i}", [P, 512], F32)) for i in range(NT)]
    XV = ctx.enter_context(nc.psum_tensor("l1_XV", [P, 512], F32))
    QK = ctx.enter_context(nc.psum_tensor("l1_QK", [P, 512], F32))
    RT = ctx.enter_context(nc.psum_tensor("l1_RT", [P, 512], F32))
    OU = ctx.enter_context(nc.psum_tensor("l1_OU", [P, 512], F32))
    sp_passed, pool_passed, dve_passed = (sem("l1s_passed_" + n) for n in ("sp", "pool", "dve"))
    names = """w x pad_hw const cdve ve rs rms_e rr base pay2 sq xnT qT kT exp em bqs
        bn ag xn max v rec vs out payx ra rb fin
        p_xnT p_q p_k p_v p_r p_rank p_S p_out p_cnt sc_dma pad_dma""".split()
    s = {n: sem("l1s_" + n) for n in names}
    dma_w, dma_x, dma_pad_hw, dma_ex = s["w"], s["x"], s["pad_hw"], sem("l1s_ex")
    pool_const, pool_ve, pool_rs, pool_me, pool_rr, pool_base = (s[n] for n in "const ve rs rms_e rr base".split())
    act_pay2, act_sq, act_xnT, act_q, act_k, act_exp, act_em, act_bqs = (
        s[n] for n in "pay2 sq xnT qT kT exp em bqs".split())
    dve_const, dve_bn, dve_ag, dve_xn, dve_max, dve_v, dve_rec, dve_vs, dve_out, dve_payx, dve_ra, dve_rb, dve_fin = (
        s[n] for n in "cdve bn ag xn max v rec vs out payx ra rb fin".split())
    pe_xnT, pe_q, pe_k, pe_v, pe_r, pe_rank, pe_S, pe_out, pe_cnt = (
        s[n] for n in "p_xnT p_q p_k p_v p_r p_rank p_S p_out p_cnt".split())
    dma_rows, dma_pads = [sem(f"l1s_rows{i}") for i in range(2)], s["pad_dma"]

    NW = 11
    NCP = 11
    RA = 13
    RB = 11
    ISC = float(P) ** -0.5

    def batches(eng, body):
        body(0, 0, False, 0)
        with eng.Fori(0, (NB - 2) // 2) as i:
            body(2 * i + 1, 1, False, i + 1)
            body(2 * i + 2, 0, False, i + 1)
        body(NB - 1, 1, True, 0)

    block = ctx.enter_context(nc.Block())

    @block.sync
    def _(sp):
        def wait(sem, value):
            sp.wait_ge(sem, value)
            if not isinstance(value, int):
                sp.sem_inc(sp_passed)

        xv = x1.rearrange("b (i p) d -> b p i d", p=P)
        sp.dma_start(xb[0][:], xv[0]).then_inc(dma_x, 16)
        for dst, src in ((wq, WqT), (wk, WkT), (wv, WvT), (wr, wrT)):
            sp.dma_start(dst[:], src).then_inc(dma_w, 16)
        for dst, src in ((bqc, bq), (bkc, bk), (nsc, nscale)):
            sp.dma_start(dst[:], src.rearrange("(p a) -> p a", a=1)).then_inc(dma_w, 16)
        for dst, src in ((bvr, bv), (nsr, nscale)):
            sp.dma_start(dst[:], src.partition_broadcast(P)).then_inc(dma_w, 16)
        wait(dma_x, 16)
        sp.dma_start(xb[1][:], xv[1]).then_inc(dma_x, 16)
        sp.dma_start(w_up[:], w_up_in).then_inc(dma_ex, 16)
        sp.dma_start(w_dn[:], w_dn_in).then_inc(dma_ex, 16)
        wait(dve_const, 4)
        sp.dma_start(xs[NE * CAP:NE * CAP + P, :], padrow[:]).then_inc(dma_pad_hw, 16)

        def body(g, p, last, prior):
            if not last:
                wait(pool_base, g + 1)
                wait(dma_x, 16 * (g + 2))
                sp.dma_start(xb[p][:], xv[(g + 2) % NB]).then_inc(dma_x, 16)

        batches(sp, body)
        wait(dma_pad_hw, 16)
        wait(dma_ex, 32)

    @block.gpsimd
    def _(pool):
        def wait(sem, value):
            pool.wait_ge(sem, value)
            if not isinstance(value, int):
                pool.sem_inc(pool_passed)

        pool.memset(ident[:], 0.0).then_inc(pool_const, 1)
        pool.memset(tri[:], 1.0).then_inc(pool_const, 1)
        pool.memset(ones[:], 1.0).then_inc(pool_const, 1)
        pool.memset(mhalf[:], -0.5).then_inc(pool_const, 1)
        wait(pool_const, 4)
        pool.affine_select(out=ident[:], in_=ident[:], compare_op=ALU.not_equal, fill=1.0, base=0,
                           pattern=[[-1, P]], channel_multiplier=1).then_inc(pool_const, 1)
        pool.affine_select(out=tri[:], in_=tri[:], compare_op=ALU.is_gt, fill=0.0, base=0,
                           pattern=[[1, P]], channel_multiplier=-1).then_inc(pool_const, 1)
        pool.iota(iota8i[:], [[1, NE]], base=0, channel_multiplier=0).then_inc(pool_const, 1)
        pool.iota(dest_i[:], [[TOPK * P, NT], [1, TOPK]], base=0, channel_multiplier=TOPK).then_inc(pool_const, 1)
        pool.iota(part_i[:], [[1, 1]], base=0, channel_multiplier=1).then_inc(pool_const, 1)
        pool.iota(tile_i[:], [[1, NTILES]], base=0, channel_multiplier=0).then_inc(pool_const, 1)
        pool.iota(nine_i[:], [[1, NE + 1]], base=0, channel_multiplier=0).then_inc(pool_const, 1)

        def rstd_of(g):
            wait(dve_ag, NT * (g + 1))
            pool.tensor_scalar(veps[:], mv[:, :, 1], 1e-5, None, ALU.add).then_inc(pool_ve, 1)
            wait(pool_ve, g + 1)
            pool.tensor_tensor(rstd[:], veps[:], mhalf[:], ALU.pow).then_inc(pool_rs, 1)

        def rms_of(g, pg):
            wait(act_sq, NT * (g + 1))
            pool.tensor_scalar(meps[:], ssq[:], 1.0 / P, 1e-6, ALU.mult, ALU.add).then_inc(pool_me, 1)
            wait(pool_me, g + 1)
            pool.tensor_tensor(rr[pg][:], meps[:], mhalf[:], ALU.pow).then_inc(pool_rr, 1)

        def base_of(g, pg):
            wait(dve_xn, NT * (g + 1))
            if not (isinstance(g, int) and g < 2):
                wait(dve_out, g - 1)
            pool.tensor_tensor(base[pg][:], xb[pg][:], xn[pg][:], ALU.add).then_inc(pool_base, 1)

        def scatter(g, p):
            wait(dve_rb, RB * (g + 1))
            wait(act_pay2, g + 1)
            for i in range(NT):
                for k in range(TOPK):
                    pool.indirect_dma_start(
                        out=xs[:, :], out_offset=bass.IndirectOffsetOnAxis(ap=pos[p][:, i, k:k + 1], axis=0),
                        in_=pay[p][:, k, i, :], in_offset=None).then_inc(dma_rows[p], 16)

        rstd_of(0)
        rms_of(0, 0)
        rstd_of(1)
        base_of(0, 0)

        def body(g, p, last, prior):
            if not last:
                rms_of(g + 1, 1 - p)
                rstd_of(g + 2)
                base_of(g + 1, 1 - p)
            scatter(g, p)

        batches(pool, body)
        wait(dve_fin, 3)
        for e in range(NE):
            pool.indirect_dma_start(out=xs[:, :], out_offset=bass.IndirectOffsetOnAxis(ap=padi[:, e:e + 1], axis=0),
                                    in_=padrow[:], in_offset=None).then_inc(dma_pads, 16)
        for rows in dma_rows:
            wait(rows, 16 * TOPK * NT * NB // 2)
        wait(dma_pads, 16 * NE)

    @block.scalar
    def _(act):
        act.wait_ge(dma_w, 16 * 9)
        act.activation(bqs[:], bqc[:], ACT.Copy, scale=ISC).then_inc(act_bqs, 1)

        def squares(g, pg):
            act.wait_ge(pool_rr, g)
            for i in range(NT):
                act.wait_ge(dve_xn, NT * g + i + 1)
                act.activation(junk[:, i, :], xn[pg][:, i, :], ACT.Square, accum_out=ssq[:, i:i + 1]).then_inc(act_sq, 1)

        def evac_xnT(g):
            act.wait_ge(pe_xnT, g + 1)
            act.activation(xnT[:], XV[:], ACT.Copy).then_inc(act_xnT, 1)

        def evac_q(g, pg):
            act.wait_ge(pe_q, g + 1)
            act.activation(qT[pg][:], QK[:], ACT.Identity, bias=bqs[:, 0:1], scale=ISC).then_inc(act_q, 1)

        def evac_k(g, pg):
            act.wait_ge(pe_k, g + 1)
            act.activation(kT[pg][:], QK[:], ACT.Identity, bias=bkc[:, 0:1]).then_inc(act_k, 1)

        def gate_exp(g):
            act.wait_ge(dve_ra, RA * (g + 1))
            act.wait_ge(dve_rb, RB * g)
            act.activation(em[:], dm[:], ACT.Exp).then_inc(act_em, 1)

        def copy_rows(g, pg):
            act.wait_ge(dve_payx, NT * (g + 1))
            act.activation(pay[pg][:, 1, :, 0:P], pay[pg][:, 0, :, 0:P], ACT.Copy).then_inc(act_pay2, 1)

        act.wait_ge(act_bqs, 1)
        squares(0, 0)
        squares(1, 1)
        evac_xnT(0)
        evac_q(0, 0)
        evac_k(0, 0)
        copy_rows(0, 0)

        def body(g, p, last, prior):
            for kt in range(NT):
                act.wait_ge(dve_max, NT * g + kt + 1)
                act.wait_ge(pe_out, g)
                act.wait_ge(dve_rec, NT * g)
                act.activation(pr[:, kt, :], Sb[kt][:], ACT.Exp, bias=mneg[:, kt:kt + 1],
                               accum_out=ssum[:, kt:kt + 1]).then_inc(act_exp, 1)
            gate_exp(g)
            if not last:
                evac_xnT(g + 1)
                evac_q(g + 1, 1 - p)
                evac_k(g + 1, 1 - p)
                squares(g + 2, p)
                copy_rows(g + 1, 1 - p)

        batches(act, body)

    @block.vector
    def _(dve):
        dve.wait_ge(pool_const, NCP)
        nc.vector.tensor_copy(iota8[:], iota8i[:]).then_inc(dve_const, 1)
        nc.vector.tensor_scalar(ebase[:], iota8i[:], float(CAP), None, ALU.mult).then_inc(dve_const, 1)
        nc.vector.memset(padrow[:], 0.0).then_inc(dve_const, 1)
        dve.wait_ge(dve_const, 3)
        nc.vector.memset(padrow[:, P + 1:P + 2].bitcast(I32), TOKENS * TOPK).then_inc(dve_const, 1)
        nc.vector.tensor_scalar(dest[:], dest_i[:], -float(TOPK * T), None, ALU.add).then_inc(dve_const, 1)
        nc.vector.tensor_copy(part_f[:], part_i[:]).then_inc(dve_const, 1)
        nc.vector.tensor_copy(tile_f[:], tile_i[:]).then_inc(dve_const, 1)
        nc.vector.tensor_copy(nine_f[:], nine_i[:]).then_inc(dve_const, 1)
        nc.vector.memset(S[0][:], 0.0).then_inc(dve_const, 1)
        nc.vector.tensor_tensor(upto[:], iota8[0:1, :].unsqueeze(1).to_broadcast([1, NE, NE]),
                                iota8[0:1, :].unsqueeze(2).to_broadcast([1, NE, NE]), ALU.is_le).then_inc(dve_const, 1)
        dve.wait_ge(dma_w, 16 * 9)
        nc.vector.tensor_scalar(wrs[:], wr[:], nsc[:, 0:1], None, ALU.mult).then_inc(dve_const, 1)
        dve.wait_ge(dve_const, 11)

        def stat(g, pg):
            dve.wait_ge(dma_x, 16 * (g + 1))
            dve.wait_ge(pool_ve, g)
            for i in range(NT):
                nc.vector.bn_stats(stats[:, i, :], xb[pg][:, i, :]).then_inc(dve_bn, 1)
            for i in range(NT):
                dve.wait_ge(dve_bn, NT * g + i + 1)
                if not isinstance(g, int):
                    dve.sem_inc(dve_passed)
                nc.vector.bn_aggr(mv[:, i, :], stats[:, i, :]).then_inc(dve_ag, 1)

        def norm_of(g, pg):
            dve.wait_ge(pool_rs, g + 1)
            for i in range(NT):
                nc.vector.tensor_scalar(xn[pg][:, i, :], xb[pg][:, i, :], mv[:, i, 0:1], rstd[:, i:i + 1],
                                        ALU.subtract, ALU.mult).then_inc(dve_xn, 1)

        def row_of(g, pg, before):
            dve.wait_ge(dma_rows[pg], 16 * TOPK * NT * before)
            dve.wait_ge(pool_rr, g + 1)
            dve.wait_ge(dve_xn, NT * (g + 1))
            for i in range(NT):
                nc.vector.scalar_tensor_tensor(pay[pg][:, 0, i, 0:P], xn[pg][:, i, :], rr[pg][:, i:i + 1], nsr[:],
                                               ALU.mult, ALU.mult).then_inc(dve_payx, 1)

        def evac_v(g, pg):
            dve.wait_ge(pe_v, g + 1)
            nc.vector.tensor_tensor(v[pg][:], XV[:].rearrange("p (i d) -> p i d", i=NT),
                                    bvr[:].unsqueeze(1).to_broadcast([P, NT, P]), ALU.add).then_inc(dve_v, 1)

        def route_a(g, pg):
            done = [RA * g]

            def step(ins, wait=True):
                ins.then_inc(dve_ra, 1)
                done[0] = done[0] + 1
                if wait:
                    dve.wait_ge(dve_ra, done[0])
                    if not isinstance(g, int):
                        dve.sem_inc(dve_passed)

            dve.wait_ge(pe_r, g + 1)
            dve.wait_ge(act_em, g)
            step(nc.vector.tensor_tensor(sc[:], RT[:, 0:NT * NE].rearrange("p (i e) -> p i e", e=NE),
                                         rr[pg][:].unsqueeze(2).to_broadcast([P, NT, NE]), ALU.mult))
            for i in range(NT):
                step(nc.vector.max(mx[:, i, :], sc[:, i, :]), i == NT - 1)
            for i in range(NT):
                step(nc.vector.max_index(ix[:, i, :], mx[:, i, :], sc[:, i, :]), i == NT - 1)
            step(nc.vector.tensor_copy(ixf[:], ix[:]))
            step(nc.vector.tensor_tensor(oh[pg][:], iota8[:].unsqueeze(1).unsqueeze(1).to_broadcast([P, NT, TOPK, NE]),
                                         ixf[:, :, 0:TOPK].unsqueeze(3).to_broadcast([P, NT, TOPK, NE]), ALU.is_equal))
            step(nc.vector.tensor_tensor(M[pg][:], oh[pg][:, :, 0, :], oh[pg][:, :, 1, :], ALU.add), False)
            step(nc.vector.tensor_tensor(dm[:], mx[:, :, 1], mx[:, :, 0], ALU.subtract))
            assert True

        def ranks(g):
            dve.wait_ge(pe_rank, g + 1)
            dve.wait_ge(dve_rb, RB * g)
            nc.vector.tensor_tensor(Re[:], RT[:, 64:64 + NT * NE].rearrange("p (i e) -> p i e", e=NE),
                                    ebase[:].unsqueeze(1).to_broadcast([P, NT, NE]), ALU.add).then_inc(dve_rb, 1)

        def route_b(g, p):
            done = [RB * g]

            def step(ins, wait=True):
                ins.then_inc(dve_rb, 1)
                done[0] = done[0] + 1
                if wait:
                    dve.wait_ge(dve_rb, done[0])

            done[0] = done[0] + 1
            dve.wait_ge(dve_rb, done[0])
            step(nc.vector.tensor_tensor(prod[:], oh[p][:], Re[:].unsqueeze(2).to_broadcast([P, NT, TOPK, NE]),
                                         ALU.mult))
            step(nc.vector.tensor_reduce(posf[:], prod[:], AX.X, ALU.add))
            step(nc.vector.tensor_copy(pos[p][:], posf[:]), False)
            step(nc.vector.tensor_reduce(msum[:], M[p][:].rearrange("p i e -> p e i"), AX.X, ALU.add))
            step(nc.vector.tensor_tensor(S[1 - p][:], S[p][:], msum[:], ALU.add), False)
            step(nc.vector.tensor_scalar(dest[:], dest[:], float(TOPK * T), None, ALU.add))
            dve.wait_ge(act_em, g + 1)
            step(nc.vector.tensor_scalar(den[:], em[:], 1.0, None, ALU.add))
            step(nc.vector.tensor_copy(
                pay[p][:, :, :, P + 1].bitcast(I32).rearrange("p k i -> p i k"),
                dest[:].rearrange("p (i k) -> p i k", k=TOPK)))
            step(nc.vector.reciprocal(pay[p][:, 0, :, P], den[:]))
            step(nc.vector.tensor_tensor(pay[p][:, 1, :, P], em[:], pay[p][:, 0, :, P], ALU.mult), False)

        for g in range(2):
            stat(g, g)
            norm_of(g, g)
        row_of(0, 0, 0)
        evac_v(0, 0)
        route_a(0, 0)

        def body(g, p, last, prior):
            o = 1 - p
            for kt in range(NT):
                dve.wait_ge(pe_S, NT * g + kt + 1)
                dve.wait_ge(act_exp, NT * g)
                nc.vector.tensor_reduce(mneg[:, kt:kt + 1], Sb[kt][:], AX.X, ALU.max, negate=True)\
                    .then_inc(dve_max, 1)
            ranks(g)
            if not last:
                stat(g + 2, p)
            for kt in range(NT):
                dve.wait_ge(act_exp, NT * g + kt + 1)
                dve.wait_ge(pe_out, g)
                nc.vector.reciprocal(srec[:, kt:kt + 1], ssum[:, kt:kt + 1]).then_inc(dve_rec, 1)
                dve.wait_ge(dve_rec, NT * g + kt + 1)
                dve.wait_ge(dve_v, g + 1)
                nc.vector.tensor_scalar(vs[:, kt, :], v[p][:, kt, :], srec[:, kt:kt + 1], ISC, ALU.mult, ALU.mult)\
                    .then_inc(dve_vs, 1)
            route_b(g, p)
            if not last:
                evac_v(g + 1, o)
                norm_of(g + 2, p)
                route_a(g + 1, o)
            dve.wait_ge(pe_out, g + 1)
            dve.wait_ge(pool_base, g + 1)
            nc.vector.tensor_tensor(x2b[:, bass.ds(g * NT, NT), :], OU[:].rearrange("p (i d) -> p i d", i=NT),
                                    base[p][:], ALU.add).then_inc(dve_out, 1)
            if not last:
                row_of(g + 1, o, prior)

        batches(dve, body)
        fin = [0]

        def step(ins, wait=True):
            ins.then_inc(dve_fin, 1)
            fin[0] += 1
            if wait:
                dve.wait_ge(dve_fin, fin[0])

        dve.wait_ge(pe_cnt, 1)
        step(nc.vector.tensor_copy(cnt[:], RT[:, 128:128 + NE]))
        step(nc.vector.scalar_tensor_tensor(padp[:], cnt[:], part_f[:, 0:1], ebase[:], ALU.add, ALU.add))
        step(nc.vector.tensor_copy(padi[:], padp[:]), False)
        step(nc.vector.tensor_scalar(nt_a[:], cnt[:], 1.0 / P, (P - 1) / P - (P - 1) / (2 * P), ALU.mult, ALU.add))
        step(nc.vector.tensor_scalar(nt_f[:], nt_a[:], MAGIC, MAGIC, ALU.add, ALU.subtract))
        step(nc.vector.tensor_tensor(cprod[:], upto[:], nt_f[0:1, :].unsqueeze(1).to_broadcast([1, NE, NE]), ALU.mult))
        step(nc.vector.tensor_reduce(cum[:], cprod[:], AX.X, ALU.add))
        step(nc.vector.tensor_tensor(cx[:], cum[:], nt_f[0:1, :], ALU.subtract))
        step(nc.vector.scalar_tensor_tensor(vals[:, 0:NE], cx[:], -float(P), ebase[0:1, :], ALU.mult, ALU.add), False)
        step(nc.vector.memset(vals[:, NE:NE + 1], float(NE * CAP)))
        step(nc.vector.tensor_tensor(le[:], cum[:].unsqueeze(1).to_broadcast([1, NTILES, NE]),
                                     tile_f[:].unsqueeze(2).to_broadcast([1, NTILES, NE]), ALU.is_le))
        step(nc.vector.tensor_reduce(et[:], le[:], AX.X, ALU.add))
        step(nc.vector.tensor_tensor(oh9[:], nine_f[:].unsqueeze(1).to_broadcast([1, NTILES, NE + 1]),
                                     et[:].unsqueeze(2).to_broadcast([1, NTILES, NE + 1]), ALU.is_equal))
        step(nc.vector.tensor_tensor(pv9[:], oh9[:], vals[:].unsqueeze(1).to_broadcast([1, NTILES, NE + 1]), ALU.mult))
        step(nc.vector.tensor_reduce(bt[:], pv9[:], AX.X, ALU.add))
        step(nc.vector.scalar_tensor_tensor(bt2[:], tile_f[:], float(P), bt[:], ALU.mult, ALU.add))
        step(nc.vector.tensor_scalar(tab[:, 0, :], bt2[:], float(NE * CAP), None, ALU.min), False)
        step(nc.vector.tensor_scalar(tab[:, 1, :], et[:], float(NE - 1), None, ALU.min))

    @block.tensor
    def _(pe):
        pe.wait_ge(pool_const, NCP)
        pe.wait_ge(dma_w, 16 * 9)
        pe.wait_ge(dve_const, 11)

        def turn(g, pg):
            pe.wait_ge(dve_xn, NT * (g + 1))
            pe.wait_ge(dve_v, g)
            for i in range(NT):
                mm = nc.tensor.transpose(XV[:, i * P:(i + 1) * P], xn[pg][:, i, :], ident[:])
            mm.then_inc(pe_xnT, 1)

        def rank(g, p):
            pe.wait_ge(dve_ra, RA * (g + 1))
            pe.wait_ge(dve_rb, RB * g)
            for i in range(NT):
                out = RT[:, 64 + i * NE:64 + (i + 1) * NE]
                nc.tensor.matmul(out, tri[:], M[p][:, i, :], start=True, stop=False)
                for j in range(i):
                    nc.tensor.matmul(out, ones[:], M[p][:, j, :], start=False, stop=False)
                mm = nc.tensor.matmul(out, ones[:], S[p][:], start=False, stop=True)
            mm.then_inc(pe_rank, 1)

        def q(g):
            pe.wait_ge(act_xnT, g + 1)
            pe.wait_ge(act_k, g)
            nc.tensor.matmul(QK[:], wq[:], xnT[:], start=True, stop=True).then_inc(pe_q, 1)

        def k(g):
            pe.wait_ge(act_q, g + 1)
            nc.tensor.matmul(QK[:], wk[:], xnT[:], start=True, stop=True).then_inc(pe_k, 1)

        def values(g):
            for i in range(NT):
                mm = nc.tensor.matmul(XV[:, i * P:(i + 1) * P], xnT[:, i * P:(i + 1) * P], wv[:],
                                      start=True, stop=True)
            mm.then_inc(pe_v, 1)

        def router(g):
            if not (isinstance(g, int) and g == 0):
                pe.wait_ge(dve_rb, RB * (g - 1) + 1)
            for i in range(NT):
                mm = nc.tensor.matmul(RT[:, i * NE:(i + 1) * NE], xnT[:, i * P:(i + 1) * P], wrs[:],
                                      start=True, stop=True)
            mm.then_inc(pe_r, 1)

        turn(0, 0)
        q(0)
        values(0)
        k(0)
        router(0)

        def body(g, p, last, prior):
            o = 1 - p
            pe.wait_ge(act_k, g + 1)
            pe.wait_ge(act_exp, NT * g)
            for kt in range(NT):
                nc.tensor.matmul(Sb[kt][:], kT[p][:, kt * P:(kt + 1) * P], qT[p][:], start=True, stop=True)\
                    .then_inc(pe_S, 1)
            rank(g, p)
            if not last:
                turn(g + 1, o)
                q(g + 1)
                values(g + 1)
                k(g + 1)
                router(g + 1)
            pe.wait_ge(dve_vs, NT * (g + 1))
            pe.wait_ge(dve_out, g)
            for i in range(NT):
                for kt in range(NT):
                    mm = nc.tensor.matmul(OU[:, i * P:(i + 1) * P], pr[:, kt, i * P:(i + 1) * P], vs[:, kt, :],
                                          start=kt == 0, stop=kt == NT - 1)
            mm.then_inc(pe_out, 1)

        batches(pe, body)
        pe.wait_ge(dve_rb, RB * NB)
        nc.tensor.matmul(RT[:, 128:128 + NE], ones[:], S[0][:], start=True, stop=True).then_inc(pe_cnt, 1)


def experts(nc, ctx, xs, yk, w_up, w_dn, tab):

    def sb(name, shape, dt=F32):
        return ctx.enter_context(nc.sbuf_tensor(name, shape, dt))

    def sem(name):
        return ctx.enter_context(nc.semaphore(name))

    R = 8
    xt = [sb(f"xt{i}", [P, ROW]) for i in range(R)]
    xT = [sb(f"xT{i}", [P, P]) for i in range(2)]
    sg = [sb(f"sg{i}", [P, HID]) for i in range(2)]
    h = [sb(f"h{i}", [P, HID]) for i in range(2)]
    hT = [sb(f"hT{i}", [P, HID]) for i in range(2)]
    y = [sb(f"y{i}", [P, P]) for i in range(R)]
    ident = sb("ex_ident", [P, P])
    XT = [ctx.enter_context(nc.psum_tensor(f"XT{i}", [P, 512], F32)) for i in range(2)]
    UP = [ctx.enter_context(nc.psum_tensor(f"UP{i}", [P, 512], F32)) for i in range(2)]
    HT = [ctx.enter_context(nc.psum_tensor(f"HT{i}", [P, 512], F32)) for i in range(2)]
    DN = [ctx.enter_context(nc.psum_tensor(f"DN{i}", [P, 512], F32)) for i in range(2)]
    dma_w, id_ready, act_xT, act_silu, act_y, dve_h, dve_hT, pe_xT, pe_up, pe_hT, pe_dn = (
        sem("ex_" + n) for n in "w id xT silu yo h hT pxT pup phT pdn".split())
    sp_passed, pool_passed = sem("ex_sp_passed"), sem("ex_pool_passed")
    dma_t = [sem(f"ex_t{i}") for i in range(R)]
    dma_y = [sem(f"ex_y{i}") for i in range(R)]

    def tiles(eng, body):
        body(0, 0)
        with eng.Fori(1, NTILES // R - 1) as i:
            body(i * R, i)
        body(NTILES - R, NTILES // R - 1)

    def lag(t0, t, n):
        return not isinstance(t0, int) or t0 + t >= n

    def more(t0, r):
        return not isinstance(t0, int) or t0 + r + 1 < NTILES

    block = ctx.enter_context(nc.Block())

    @block.sync
    def _(sp):
        def wait(sem, value):
            sp.wait_ge(sem, value)
            if not isinstance(value, int):
                sp.sem_inc(sp_passed)

        def load(t, r):
            row = sp.value_load(tab[0:1, 0, bass.ds(t, 1)], min_val=0, max_val=NE * CAP)
            sp.dma_start(xt[r][:], xs[bass.ds(row, P), :]).then_inc(dma_t[r], 16)

        for r in range(R):
            load(r, r)
        with sp.Fori(1, NTILES // R) as i:
            for r in range(R):
                wait(dma_y[r], 16 * i)
                load(R * i + r, r)

    @block.gpsimd
    def _(pool):
        def wait(sem, value):
            pool.wait_ge(sem, value)
            if not isinstance(value, int):
                pool.sem_inc(pool_passed)

        pool.memset(ident[:], 0.0).then_inc(id_ready, 1)
        wait(id_ready, 1)
        pool.affine_select(out=ident[:], in_=ident[:], compare_op=ALU.not_equal, fill=1.0, base=0,
                           pattern=[[-1, P]], channel_multiplier=1).then_inc(id_ready, 1)

        def body(t0, i):
            for r in range(R):
                wait(act_y, t0 + r + 1)
                pool.indirect_dma_start(
                    out=yk[:, :], out_offset=bass.IndirectOffsetOnAxis(ap=xt[r][:, P + 1:P + 2].bitcast(U32), axis=0),
                    in_=y[r][:], in_offset=None, bounds_check=TOKENS * TOPK - 1, oob_is_err=False)\
                    .then_inc(dma_y[r], 16)

        tiles(pool, body)
        for r in range(R):
            wait(dma_y[r], 16 * (NTILES // R))

    @block.scalar
    def _(act):
        def evac_xT(t, r):
            act.wait_ge(pe_xT, t + 1)
            act.activation(xT[r % 2][:], XT[r % 2][:, 0:P], ACT.Copy).then_inc(act_xT, 1)

        def evac_y(t, r):
            act.wait_ge(pe_dn, t + 1)
            act.activation(y[r][:], DN[r % 2][:, 0:P], ACT.Copy).then_inc(act_y, 1)

        evac_xT(0, 0)

        def body(t0, i):
            for r in range(R):
                t = t0 + r
                if lag(t0, 0, R):
                    act.wait_ge(dma_y[r], 16 * i)
                if more(t0, r):
                    evac_xT(t + 1, (r + 1) % R)
                act.wait_ge(pe_up, t + 1)
                if lag(t0, r, 2):
                    act.wait_ge(dve_h, t - 1)
                act.activation(sg[r % 2][:], UP[r % 2][:, HID:2 * HID], ACT.Silu).then_inc(act_silu, 1)
                if lag(t0, r, 2):
                    evac_y(t - 2, (r - 2) % R)

        tiles(act, body)
        for t in (NTILES - 2, NTILES - 1):
            evac_y(t, t % R)

    @block.vector
    def _(dve):
        def turned(t, r):
            dve.wait_ge(pe_hT, t + 1)
            nc.vector.tensor_copy(hT[r % 2][:], HT[r % 2][:, 0:HID]).then_inc(dve_hT, 1)

        def body(t0, i):
            for r in range(R):
                t = t0 + r
                if lag(t0, r, 1):
                    turned(t - 1, r - 1)
                dve.wait_ge(act_silu, t + 1)
                nc.vector.scalar_tensor_tensor(h[r % 2][:], sg[r % 2][:], xt[r][:, P:P + 1], UP[r % 2][:, 0:HID],
                                               ALU.mult, ALU.mult).then_inc(dve_h, 1)

        tiles(dve, body)
        turned(NTILES - 1, NTILES - 1)

    @block.tensor
    def _(pe):
        def turn(t, r, before):
            pe.wait_ge(dma_t[r], 16 * before)
            nc.tensor.transpose(XT[r % 2][:, 0:P], xt[r][:, 0:P], ident[:]).then_inc(pe_xT, 1)

        def expert_of(t):
            return pe.value_load(tab[0:1, 1, bass.ds(t, 1)], min_val=0, max_val=NE - 1)

        def turn_h(t, r, some):
            pe.wait_ge(dve_h, t + 1)
            if some:
                pe.wait_ge(dve_hT, t - 1)
            for j in range(2):
                mm = nc.tensor.transpose(HT[r % 2][:, j * P:(j + 1) * P], h[r % 2][:, j * P:(j + 1) * P], ident[:])
            mm.then_inc(pe_hT, 1)

        def down(t, r, some, e):
            pe.wait_ge(dve_hT, t + 1)
            if some:
                pe.wait_ge(act_y, t - 1)
            for j in range(2):
                mm = nc.tensor.matmul(DN[r % 2][:, 0:P], hT[r % 2][:, j * P:(j + 1) * P],
                                      w_dn[:, bass.ds(e * 2 + j, 1), :].rearrange("p a d -> p (a d)"),
                                      start=j == 0, stop=j == 1)
            mm.then_inc(pe_dn, 1)

        pe.wait_ge(id_ready, 2)
        turn(0, 0, 1)

        def body(t0, i):
            experts_of = {0: expert_of(t0)}
            for r in range(R):
                t = t0 + r
                pe.wait_ge(act_xT, t + 1)
                if lag(t0, r, 2):
                    pe.wait_ge(dve_h, t - 1)
                nc.tensor.matmul(UP[r % 2][:], xT[r % 2][:],
                                 w_up[:, bass.ds(experts_of[r], 1), :].rearrange("p a d -> p (a d)"),
                                 start=True, stop=True).then_inc(pe_up, 1)
                if r < R - 1:
                    experts_of[r + 1] = expert_of(t + 1)
                if r < 2 and lag(t0, r, 2):
                    experts_of[r - 2] = expert_of(t - 2)
                if more(t0, r):
                    turn(t + 1, (r + 1) % R, i + 1 if r < R - 1 else i + 2)
                if lag(t0, r, 1):
                    turn_h(t - 1, (r - 1) % R, lag(t0, r, 3))
                if lag(t0, r, 2):
                    down(t - 2, (r - 2) % R, lag(t0, r, 4), experts_of[r - 2])

        tiles(pe, body)
        turn_h(NTILES - 1, NTILES - 1, True)
        for t in (NTILES - 2, NTILES - 1):
            down(t, t, True, expert_of(t))


def combine(nc, ctx, yk, x2b, out):
    yb = ctx.enter_context(nc.sbuf_tensor("yb", [P, NB, NT, TOPK, P], F32))
    ysum = ctx.enter_context(nc.sbuf_tensor("ysum", [P, NB, NT, P], F32))
    res = ctx.enter_context(nc.sbuf_tensor("res", [P, NB, NT, P], F32))
    loaded = [ctx.enter_context(nc.semaphore(f"cb_load{b}")) for b in range(NB)]
    added, done, stored = (ctx.enter_context(nc.semaphore("cb_" + n)) for n in ("added", "done", "stored"))
    yv = yk.rearrange("(b i p k) d -> b p i (k d)", b=NB, i=NT, k=TOPK)
    ov = out.rearrange("b (i p) d -> b p i d", p=P)
    block = ctx.enter_context(nc.Block())

    @block.sync
    def _(sp):
        for b in range(NB):
            sp.dma_start(yb[:, b].rearrange("p i k d -> p i (k d)"), yv[b]).then_inc(loaded[b], 16)

    @block.vector
    def _(dve):
        for b in range(NB):
            dve.wait_ge(loaded[b], 16)
            nc.vector.tensor_tensor(ysum[:, b], yb[:, b, :, 0, :], yb[:, b, :, 1, :], ALU.add).then_inc(added, 1)
            dve.wait_ge(added, b + 1)
            nc.vector.tensor_tensor(res[:, b], ysum[:, b], x2b[:, b * NT:(b + 1) * NT, :], ALU.add).then_inc(done, 1)

    @block.scalar
    def _(act):
        for b in range(NB):
            act.wait_ge(done, b + 1)
            act.dma_start(ov[b], res[:, b]).then_inc(stored, 16)
        act.wait_ge(stored, 16 * NB)


def build(nc, x, w_inT, b_in, w_outT, b_out, wqT, wscale, fbias, WqT, bq, WkT, bk, WvT, bv, nscale, wrT,
          w_up_in, w_dn_in, out):
    x1 = nc.dram_tensor("x1_dram", [NB, T, P], F32).ap()
    xs = nc.dram_tensor("expert_rows", [NE * CAP + P, ROW], F32).ap()
    yk = nc.dram_tensor("results", [TOKENS * TOPK, P], F32).ap()
    with ExitStack() as ctx:
        layer0(nc, ctx, x, w_inT, b_in, w_outT, b_out, wqT, wscale, fbias, x1)
    with ExitStack() as outer:
        def sb(name, shape, dt=F32):
            return outer.enter_context(nc.sbuf_tensor(name, shape, dt))

        x2b = sb("x2b", [P, NB * NT, P])
        tab = sb("tab", [1, 2, NTILES], I32)
        w_up = sb("w_up", [P, NE, 2 * HID])
        w_dn = sb("w_dn", [P, NE * 2, P])
        with ExitStack() as ctx:
            layer1(nc, ctx, x1, WqT, bq, WkT, bk, WvT, bv, nscale, wrT, xs, x2b, tab, w_up, w_dn, w_up_in, w_dn_in)
        with ExitStack() as ctx:
            experts(nc, ctx, xs, yk, w_up, w_dn, tab)
        with ExitStack() as ctx:
            combine(nc, ctx, yk, x2b, out)


def kernel(**inputs):
    import concourse.bacc as bacc
    import numpy as np
    from concourse.bass_utils import run_bass_kernel_spmd

    a = {k: np.asarray(v) for k, v in inputs.items()}
    arrays = {
        "x": a["L0_attn_x"], "w_inT": a["L0_attn_w_in"].T, "b_in": a["L0_attn_b_in"],
        "w_outT": a["L0_attn_w_out"].T, "b_out": a["L0_attn_b_out"],
        "wqT": np.ascontiguousarray(a["L0_ffn_weight_q"].T).view(np.int32), "wscale": a["L0_ffn_weight_scale"], "fbias": a["L0_ffn_bias"],
        "WqT": a["L1_attn_Wq"].T, "bq": a["L1_attn_bq"], "WkT": a["L1_attn_Wk"].T, "bk": a["L1_attn_bk"],
        "WvT": a["L1_attn_Wv"].T, "bv": a["L1_attn_bv"],
        "nscale": a["L1_ffn_norm_scale"], "wrT": a["L1_ffn_w_router"].T,
        "w_up": a["L1_ffn_w_up"].transpose(2, 0, 1),
        "w_dn": a["L1_ffn_w_down"].reshape(NE, P, HID // P, P).transpose(3, 0, 2, 1).reshape(P, NE * 2, P),
    }
    arrays = {"in_" + k: np.ascontiguousarray(v) for k, v in arrays.items()}
    nc = bacc.Bacc("TRN2", target_bir_lowering=False, num_devices=1)
    args = [nc.dram_tensor(k, v.shape, mybir.dt.from_np(v.dtype), kind="ExternalInput").ap()
            for k, v in arrays.items()]
    args.append(nc.dram_tensor("out", [NB, T, P], F32, kind="ExternalOutput").ap())
    build(nc, *args)
    r = run_bass_kernel_spmd(nc, [arrays], core_ids=[0])
    return r.results[0]["out"]
```

```python
from contextlib import ExitStack

import concourse.bass as bass
from concourse import mybir

F32 = mybir.dt.float32
BF16 = mybir.dt.bfloat16
I32 = mybir.dt.int32
U32 = mybir.dt.uint32
ALU = mybir.AluOpType
ACT = mybir.ActivationFunctionType
AX = mybir.AxisListType

P = 128
NB = 8
T = 512
NT = T // P
H = 16
HD = P // H
HG = 4
STEPS = H // HG
UNITS = 2 * NT
SLOTS = STEPS * UNITS
MAGIC = 12582912.0
NEG = -1e30
ONE_PAIR = 1.0 + 16256 / 2 ** 23
QTERMS = (0, 0, 0, 1, 1, 2)
KTERMS = (0, 1, 2, 0, 1, 0)
NTERM = len(QTERMS)
MROW = NTERM * HD
QRUNS = ((0, 3, 0), (3, 2, 1), (5, 1, 2))
KRUNS = ((0, 3), (3, 2), (5, 1))
NLOAD = 2 * (len(QRUNS) + len(KRUNS) + 1)


def window(t):
    lo, hi = max(0, t - 1), min(NT, t + 2)
    return lo * P, (hi - lo) * P


def piece_of(k):
    short, j = k % 2 == 0, k // 2
    return ((0, NT - 1) if short else (1, NT - 2))[j // HG], j % HG


def ahead(u, first):
    if first and u < UNITS // 2:
        return [(1 + u // 2, v) for v in ((4, 5), (6, 7), (0, 1), (2, 3))[u]]
    return [(2, u % UNITS)]


def k_slot(h):
    return h % 2 * (H // 2) + h // 2


def layer0(nc, ctx, x, w_inT, b_in, w_outT, b_out, wqT, wscale, fbias, x1_dram):
    parts_dram = nc.dram_tensor("parts_dram", [NB + 1, 2, 3, P, T], BF16).ap()
    base_dram = nc.dram_tensor("base_dram", [NB + 1, P, NT, P], F32).ap()

    def sb(name, shape, dt=F32):
        return ctx.enter_context(nc.sbuf_tensor(name, shape, dt))

    def sem(name):
        return ctx.enter_context(nc.semaphore(name))

    w_in = sb("w_in", [P, 3 * P])
    w_out = sb("w_out", [P, P])
    wq8 = sb("wq8", [P, P // 4], mybir.dt.int32)
    wq = sb("wq", [P, P], BF16)
    b_col = sb("b_col", [P, 2])
    bq_col = sb("bq_col", [P, 1])
    bv_row = sb("bv_row", [P, P])
    ws_row = sb("ws_row", [P, P])
    bo_row = sb("bo_row", [P, P])
    fb_row = sb("fb_row", [P, P])
    bsum_row = sb("bsum_row", [P, P])
    ident = sb("ident", [P, P])
    ident16 = sb("ident16", [P, P], BF16)
    mask_lo = sb("mask_lo", [P, P], BF16)
    mask_hi = sb("mask_hi", [P, P], BF16)
    mhalf = sb("mhalf", [P, NT])
    xb = sb("xb", [P, NT, P])
    stats = sb("stats", [P, NT, 6])
    mv = sb("mv", [P, NT, 2])
    veps = sb("veps", [P, NT])
    rstd = sb("rstd", [P, NT])
    xn = sb("xn", [P, NT, P])
    amax = sb("amax", [P, NT])
    xscale = sb("xscale", [P, NT])
    xrec = sb("xrec", [P, NT])
    t1 = sb("t1", [P, NT, P])
    t2 = sb("t2", [P, NT, P])
    xq = sb("xq", [P, NT, P], BF16)
    xqT = sb("xqT", [P, T], BF16)
    base0 = sb("base0", [P, NT, P])
    base1 = sb("base1", [P, NT, P])
    ffn = sb("ffn", [P, NT, P])
    base2 = sb("base2", [P, NT, P])
    base_r = sb("base_r", [P, NT, P])
    xnT = [sb(f"xnT{i}", [P, T]) for i in range(2)]
    qf, kf, rq, rk = (sb(n, [P, T]) for n in ("qf", "kf", "rq", "rk"))
    qp = sb("qp", [P, 3, T], BF16)
    kp = sb("kp", [P, 3, T], BF16)
    Qs = [sb(f"Qs{i}", [P, H // 2, T], BF16) for i in range(2)]
    Ks = [sb(f"Ks{i}", [P, H, T], BF16) for i in range(2)]
    Va = [sb(f"Va{i}", [P, NT, H, 32]) for i in range(2)]
    mneg = sb("mneg", [P, 2, NT * HG])
    mp = sb("mp", [P, 2, NT, 8], BF16)
    mT = sb("mT", [8, 2, T], BF16)
    Pb = sb("Pb", [P, NT, HG, 3 * P])
    cs = sb("cs", [P, HG, T])
    rec = sb("rec", [P, NT, H])
    ctxn = sb("ctxn", [P, NT, P])
    ctxT = sb("ctxT", [P, T])
    x1s = sb("x1s", [P, NT, P])

    A = [ctx.enter_context(nc.psum_tensor(f"A{i}", [P, 512], F32)) for i in range(2)]
    SB = [ctx.enter_context(nc.psum_tensor(f"SB{i}", [P, 2, 512], F32)) for i in range(2)]
    PV = ctx.enter_context(nc.psum_tensor("PV", [P, 512], F32))
    misc = ctx.enter_context(nc.psum_tensor("misc", [P, 512], F32))
    misc16 = misc[:, 0:256].bitcast(BF16)

    sp_passed, pool_passed, dve_passed = sem("sp_passed"), sem("pool_passed"), sem("dve_passed")
    names = """dma_w dma_x dma_base_r dma_base_w dma_pq dma_pk dma_stack dma_m dma_x1
    pool_const pool_fill dve_fill pool_rs pool_ve pool_t1 pool_t2 pool_xq pool_b0 pool_b1 pool_b2 pool_rq pool_q3 pool_rk pool_k3
    pool_mask dve_const dve_bn dve_ag dve_xn dve_amax dve_xs dve_xr dve_ffn dve_max dve_mp dve_v dve_rec dve_ctx dve_x1
    act_bq act_xnT act_xqT act_qf act_q1 act_q2 act_kf act_k1 act_k2 act_exp act_pv act_mT act_ctxT
    pe_xnT pe_q pe_k pe_xqT pe_ffn pe_v pe_A pe_B pe_PV pe_mT pe_ctx pe_ctxT pe_out""".split()
    s = {n: sem(n) for n in names}
    (dma_w, dma_x, dma_base_r, dma_base_w, dma_pq, dma_pk, dma_stack, dma_m, dma_x1,
     pool_const, pool_fill, dve_fill, pool_rs, pool_ve, pool_t1, pool_t2, pool_xq, pool_b0, pool_b1, pool_b2,
     pool_rq, pool_q3, pool_rk, pool_k3,
     pool_mask, dve_const, dve_bn, dve_ag, dve_xn, dve_amax, dve_xs, dve_xr, dve_ffn, dve_max, dve_mp, dve_v,
     dve_rec, dve_ctx, dve_x1,
     act_bq, act_xnT, act_xqT, act_qf, act_q1, act_q2, act_kf, act_k1, act_k2, act_exp, act_pv, act_mT, act_ctxT,
     pe_xnT, pe_q, pe_k, pe_xqT, pe_ffn, pe_v, pe_A, pe_B, pe_PV, pe_mT, pe_ctx, pe_ctxT, pe_out) = (
        s[n] for n in names)

    NCONST = 8
    MASKS = (1, 3, 5, 6)
    NMASK = MASKS[-1]

    def batches(eng, body):
        body(0, 0, True, False)
        with eng.Fori(0, (NB - 2) // 2) as i:
            body(2 * i + 1, 1, False, False)
            body(2 * i + 2, 0, False, False)
        body(NB - 1, 1, False, True)

    block = ctx.enter_context(nc.Block())

    @block.sync
    def _(sp):
        def wait(sem, value):
            sp.wait_ge(sem, value)
            if not isinstance(value, int):
                sp.sem_inc(sp_passed)

        xv = x.rearrange("b (i p) d -> b p i d", p=P)
        x1v = x1_dram.rearrange("b (i p) d -> b p i d", p=P)

        def load_x(g):
            sp.dma_start(xb[:], xv[g]).then_inc(dma_x, 16)

        def store_parts(g, which):
            tile, done, ready = ((qp, dma_pq, pool_q3), (kp, dma_pk, pool_k3))[which]
            wait(ready, g + 1)
            sp.dma_start(parts_dram[g, which].rearrange("s e t -> e s t"), tile[:]).then_inc(done, 16)

        def load_q(g, pg):
            wait(dma_pq, 16 * (g + 1))
            for par in range(2):
                for n, count, part in QRUNS:
                    r0 = 64 * par + HD * n
                    src = parts_dram[g, 0, part].rearrange("(b d a) t -> b d (a t)", b=2, d=HD)[par]
                    sp.dma_start(Qs[pg][r0:r0 + count * HD, :, :].rearrange("r a t -> r (a t)"),
                                 src.unsqueeze(0).to_broadcast([count, HD, H // 2 * T])).then_inc(dma_stack, 16)
                r0 = 64 * par + MROW
                sp.dma_start(Qs[pg][r0:r0 + 2, :, :], Qs[pg][r0 + 2:r0 + 4, :, :]).then_inc(dma_stack, 16)

        def load_k(g, pg):
            wait(dma_pk, 16 * (g + 1))
            for par in range(2):
                for n, count in KRUNS:
                    r0 = 64 * par + HD * n
                    src = parts_dram[g, 1].rearrange("s (b d a) t -> b s d (a t)", b=2, d=HD)[par, 0:count]
                    heads = Ks[pg][r0:r0 + count * HD, par * H // 2:(par + 1) * H // 2, :]
                    sp.dma_start(heads.rearrange("r a t -> r (a t)"), src).then_inc(dma_stack, 16)

        def place_max(step, hg, pg):
            wait(act_mT, step + 1)
            if not (isinstance(step, int) and step == 0):
                wait(dma_m, 32 * step)
            for par in range(2):
                r0 = 64 * par + MROW
                sp.dma_start(Qs[pg][r0:r0 + 2, 2 * hg:2 * hg + 2, :],
                             mT[4 * par:4 * par + 4, hg % 2, :]).then_inc(dma_m, 16)

        sp.dma_start(xb[:], xv[0]).then_inc(dma_x, 16)
        sp.dma_start(w_in[:], w_inT).then_inc(dma_w, 16)
        sp.dma_start(w_out[:], w_outT).then_inc(dma_w, 16)
        sp.dma_start(wq8[:], wqT).then_inc(dma_w, 16)
        sp.dma_start(b_col[:], b_in[0:2 * P].rearrange("(c p) -> p c", p=P),
                     allow_slow_non_contiguous=True).then_inc(dma_w, 16)
        for row, src in ((bv_row, b_in[2 * P:3 * P]), (ws_row, wscale), (bo_row, b_out), (fb_row, fbias)):
            sp.dma_start(row[:], src.partition_broadcast(P)).then_inc(dma_w, 16)
        wait(pool_b0, 1)
        wait(dve_xn, NT)
        load_x(1)
        store_parts(0, 0)
        store_parts(0, 1)
        wait(pool_fill, 2)
        load_q(0, 0)
        wait(dve_fill, 2)
        load_k(0, 0)
        wait(pool_b2, 1)
        sp.dma_start(base_dram[0], base2[:]).then_inc(dma_base_w, 16)
        store_parts(1, 0)
        store_parts(1, 1)
        place_max(0, 0, 0)
        wait(pool_b2, 2)
        sp.dma_start(base_dram[1], base2[:]).then_inc(dma_base_w, 16)
        wait(pool_fill, 4)
        wait(dve_fill, 4)

        def body(b, p, first, last):
            o = 1 - p
            if not last:
                wait(pool_b0, b + 2)
                wait(dve_xn, NT * (b + 2))
                load_x((b + 2) % NB)
                if not first:
                    wait(pe_B, SLOTS * b)
                load_q(b + 1, o)
            place_max(STEPS * b + 1, 1, p)
            if not last:
                load_k(b + 1, o)
            if not first:
                wait(dma_base_w, 16 * b)
                sp.dma_start(base_r[:], base_dram[b - 1]).then_inc(dma_base_r, 16)
            place_max(STEPS * b + 2, 2, p)
            if not first:
                wait(dve_x1, b)
                sp.dma_start(x1v[b - 1], x1s[:]).then_inc(dma_x1, 16)
            place_max(STEPS * b + 3, 3, p)
            if not last:
                store_parts(b + 2, 0)
                place_max(STEPS * b + 4, 0, o)
                store_parts(b + 2, 1)
                wait(pool_b2, b + 3)
                sp.dma_start(base_dram[b + 2], base2[:]).then_inc(dma_base_w, 16)

        batches(sp, body)
        wait(dve_x1, NB - 1)
        sp.dma_start(base_r[:], base_dram[NB - 1]).then_inc(dma_base_r, 16)
        wait(dve_x1, NB)
        sp.dma_start(x1v[NB - 1], x1s[:]).then_inc(dma_x1, 16)
        wait(dma_x1, 16 * NB)
        wait(dma_base_w, 16 * (NB + 1))
        wait(dma_stack, 16 * NLOAD * NB)

    @block.gpsimd
    def _(pool):
        def wait(sem, value):
            pool.wait_ge(sem, value)
            if not isinstance(value, int):
                pool.sem_inc(pool_passed)

        pool.memset(ident[:], 0.0).then_inc(pool_const, 1)
        pool.memset(ident16[:], 0.0).then_inc(pool_const, 1)
        pool.memset(mask_lo[:], 0.0).then_inc(pool_const, 1)
        pool.memset(mask_hi[:], 0.0).then_inc(pool_const, 1)
        pool.memset(mhalf[:], -0.5).then_inc(pool_const, 1)
        wait(pool_const, 5)
        for m in (ident, ident16):
            pool.affine_select(out=m[:], in_=m[:], compare_op=ALU.not_equal, fill=1.0, base=0,
                               pattern=[[-1, P]], channel_multiplier=1).then_inc(pool_const, 1)
        pool.affine_select(out=mask_lo[:], in_=mask_lo[:], compare_op=ALU.is_ge, fill=NEG, base=0,
                           pattern=[[1, P]], channel_multiplier=-1).then_inc(pool_const, 1)
        pool.affine_select(out=mask_hi[:], in_=mask_hi[:], compare_op=ALU.is_ge, fill=NEG, base=0,
                           pattern=[[-1, P]], channel_multiplier=1).then_inc(pool_const, 1)
        def fill_q(i):
            pool.memset(Qs[i][:].bitcast(F32), 0.0).then_inc(pool_fill, 1)

        def fill_k(i):
            pool.memset(Ks[i][:].bitcast(F32), ONE_PAIR).then_inc(pool_fill, 1)

        fill_k(0)

        def rstd_of(g):
            wait(dve_ag, NT * (g + 1))
            pool.tensor_scalar(veps[:], mv[:, :, 1], 1e-5, None, ALU.add).then_inc(pool_ve, 1)
            wait(pool_ve, g + 1)
            pool.tensor_tensor(rstd[:], veps[:], mhalf[:], ALU.pow).then_inc(pool_rs, 1)

        def base_x(g):
            wait(dve_xn, NT * (g + 1))
            if not (isinstance(g, int) and g == 0):
                wait(pool_b1, g)
            pool.tensor_tensor(base0[:], xb[:], xn[:], ALU.add).then_inc(pool_b0, 1)

        def quant_scale(g):
            wait(dve_xr, g + 1)
            for i in range(NT):
                pool.tensor_scalar(t1[:, i, :], xn[:, i, :], xrec[:, i:i + 1], MAGIC, ALU.mult, ALU.add)\
                    .then_inc(pool_t1, 1)

        def quant_clip(g):
            wait(pool_t1, NT * (g + 1))
            pool.tensor_scalar(t2[:], t1[:], MAGIC - 128, MAGIC + 127, ALU.max, ALU.min).then_inc(pool_t2, 1)

        def quant_int(g):
            wait(pool_t2, g + 1)
            if not (isinstance(g, int) and g == 0):
                wait(pe_xqT, g)
            pool.tensor_scalar(xq[:], t2[:], MAGIC, None, ALU.subtract).then_inc(pool_xq, 1)

        def base_bias(g):
            wait(pool_b0, g + 1)
            pool.tensor_tensor(base1[:], base0[:], bsum_row[:].unsqueeze(1).to_broadcast([P, NT, P]), ALU.add)\
                .then_inc(pool_b1, 1)

        def base_ffn(g):
            wait(pool_b1, g + 1)
            wait(dve_ffn, NT * (g + 1))
            if not (isinstance(g, int) and g == 0):
                wait(dma_base_w, 16 * g)
            pool.tensor_tensor(base2[:], base1[:], ffn[:], ALU.add).then_inc(pool_b2, 1)

        def rest(g, which):
            full, tile, out, done, first_part, last_part, n = (
                (qf, qp, rq, pool_rq, act_q1, pool_q3, act_qf), (kf, kp, rk, pool_rk, act_k1, pool_k3, act_kf))[which]
            wait(n, g + 1)
            wait(first_part, g + 1)
            pool.tensor_tensor(out[:], full[:], tile[:, 0, :], ALU.subtract).then_inc(done, 1)

        def third(g, which):
            tile, r, done, second, last = ((qp, rq, pool_q3, act_q2, dma_pq), (kp, rk, pool_k3, act_k2, dma_pk))[which]
            wait(second, g + 1)
            if not (isinstance(g, int) and g == 0):
                wait(last, 16 * g)
            pool.tensor_tensor(tile[:, 2, :], r[:], tile[:, 1, :], ALU.subtract).then_inc(done, 1)

        def masks(b, hg, kt):
            wait(act_exp, SLOTS * b + UNITS * hg + 2 * kt + 2)
            if kt > 0:
                blk = Pb[:, kt, :, 0:P]
                pool.affine_select(out=blk, in_=blk, compare_op=ALU.is_ge, fill=0.0, base=0,
                                   pattern=[[0, HG], [1, P]], channel_multiplier=-1).then_inc(pool_mask, 1)
            if kt < NT - 1:
                w = window(kt)[1]
                blk = Pb[:, kt, :, w - P:w]
                pool.affine_select(out=blk, in_=blk, compare_op=ALU.is_ge, fill=0.0, base=0,
                                   pattern=[[0, HG], [-1, P]], channel_multiplier=1).then_inc(pool_mask, 1)

        rstd_of(0)
        base_x(0)
        fill_q(0)
        quant_scale(0)
        rest(0, 0)
        quant_clip(0)
        third(0, 0)
        rest(0, 1)
        rstd_of(1)
        third(0, 1)
        quant_int(0)
        wait(dve_const, 2)
        base_bias(0)
        fill_k(1)
        base_x(1)
        base_ffn(0)
        quant_scale(1)
        quant_clip(1)
        quant_int(1)
        rest(1, 0)
        third(1, 0)
        fill_q(1)
        rest(1, 1)
        third(1, 1)
        base_bias(1)
        base_ffn(1)

        def body(b, p, first, last):
            g = b + 2
            for u in range(SLOTS):
                if not last:
                    if u == 8:
                        rstd_of(g)
                    if u == 14:
                        base_x(g)
                    if u == 16:
                        quant_scale(g)
                    if u == 18:
                        quant_clip(g)
                    if u == 20:
                        quant_int(g)
                    if u == 22:
                        rest(g, 0)
                    if u == 24:
                        rest(g, 1)
                        third(g, 0)
                    if u == 26:
                        third(g, 1)
                    if u == 28:
                        base_bias(g)
                    if u == 30:
                        base_ffn(g)
                if u % 2 == 1:
                    masks(b, u // UNITS, (u % UNITS) // 2)

        batches(pool, body)

    @block.scalar
    def _(act):
        act.wait_ge(dma_w, 16 * NCONST)
        SC = float(HD) ** -0.5
        act.activation(bq_col[:], b_col[:, 0:1], ACT.Copy, scale=SC).then_inc(act_bq, 1)

        def evac_xnT(g, pg):
            act.wait_ge(pe_xnT, g + 1)
            act.activation(xnT[pg][:], misc[:], ACT.Copy).then_inc(act_xnT, 1)

        def evac_q(g):
            act.wait_ge(pe_q, g + 1)
            if isinstance(g, int) and g == 0:
                act.wait_ge(act_bq, 1)
            else:
                act.wait_ge(pool_rq, g)
                act.wait_ge(dma_pq, 16 * g)
            act.activation(qf[:], misc[:], ACT.Identity, bias=bq_col[:, 0:1], scale=SC).then_inc(act_qf, 1)
            act.activation(qp[:, 0, :], misc[:], ACT.Identity, bias=bq_col[:, 0:1], scale=SC).then_inc(act_q1, 1)

        def evac_k(g):
            act.wait_ge(pe_k, g + 1)
            if not (isinstance(g, int) and g == 0):
                act.wait_ge(pool_rk, g)
                act.wait_ge(dma_pk, 16 * g)
            act.activation(kf[:], misc[:], ACT.Identity, bias=b_col[:, 1:2]).then_inc(act_kf, 1)
            act.activation(kp[:, 0, :], misc[:], ACT.Identity, bias=b_col[:, 1:2]).then_inc(act_k1, 1)

        def second(g, which):
            tile, r, need, done = ((qp, rq, pool_rq, act_q2), (kp, rk, pool_rk, act_k2))[which]
            act.wait_ge(need, g + 1)
            act.activation(tile[:, 1, :], r[:], ACT.Copy).then_inc(done, 1)

        def evac_xqT(g):
            act.wait_ge(pe_xqT, g + 1)
            act.activation(xqT[:], misc16, ACT.Copy).then_inc(act_xqT, 1)

        def evac_mT(step, hg):
            act.wait_ge(pe_mT, step + 1)
            if not (isinstance(step, int) and step < 2):
                act.wait_ge(dma_m, 32 * (step - 1))
            act.activation(mT[:, hg % 2, :], misc16[0:8, :], ACT.Copy).then_inc(act_mT, 1)

        def exp(b, u):
            hg, kt, half = u // UNITS, (u % UNITS) // 2, u % 2
            w = window(kt)[1]
            act.wait_ge(pe_B, SLOTS * b + u + 1)
            if not (isinstance(b, int) and b == 0 and hg == 0) and half == 0:
                act.wait_ge(pe_PV, NT * (STEPS * b + hg - 1) + kt + 1)
            act.activation(Pb[:, kt, 2 * half:2 * half + 2, 0:w], SB[u % 2][:, :, 0:w], ACT.Exp).then_inc(act_exp, 1)

        def evac_pv(step, hg):
            act.wait_ge(pe_PV, NT * (step + 1))
            if hg == 0 and not (isinstance(step, int) and step == 0):
                act.wait_ge(pe_ctx, step)
            act.activation(cs[:, hg, :], PV[:], ACT.Copy).then_inc(act_pv, 1)

        def evac_ctxT(g):
            act.wait_ge(pe_ctxT, g + 1)
            act.activation(ctxT[:], misc[:], ACT.Copy).then_inc(act_ctxT, 1)

        evac_xnT(0, 0)
        evac_q(0)
        second(0, 0)
        evac_k(0)
        second(0, 1)
        evac_xqT(0)
        evac_xnT(1, 1)
        evac_q(1)
        second(1, 0)
        evac_k(1)
        evac_xqT(1)
        second(1, 1)
        evac_mT(0, 0)

        def body(b, p, first, last):
            for u in range(SLOTS):
                exp(b, u)
                if u % UNITS == 4 and not (first and u == 4):
                    evac_pv(STEPS * b + u // UNITS - 1, (u // UNITS - 1) % STEPS)
                if (u % UNITS == 2 if u >= UNITS or not first else u == 3) and not (last and u // UNITS == STEPS - 1):
                    evac_mT(STEPS * b + u // UNITS + 1, (u // UNITS + 1) % STEPS)
                if u == 12 and not first:
                    evac_ctxT(b - 1)
                if not last:
                    if u == 16:
                        evac_xnT(b + 2, p)
                    if u == 20:
                        evac_q(b + 2)
                    if u == 22:
                        evac_k(b + 2)
                    if u == 23:
                        second(b + 2, 0)
                    if u == 24:
                        evac_xqT(b + 2)
                    if u == 25:
                        second(b + 2, 1)

        batches(act, body)
        evac_pv(STEPS * NB - 1, STEPS - 1)
        evac_ctxT(NB - 1)

    @block.vector
    def _(dve):
        def bn(g, tiles):
            dve.wait_ge(dma_x, 16 * (g + 1))
            for i in tiles:
                nc.vector.bn_stats(stats[:, i, :], xb[:, i, :]).then_inc(dve_bn, 1)

        def ag(g):
            for i in range(NT):
                dve.wait_ge(dve_bn, NT * g + i + 1)
                if not isinstance(g, int):
                    dve.sem_inc(dve_passed)
                nc.vector.bn_aggr(mv[:, i, :], stats[:, i, :]).then_inc(dve_ag, 1)

        def norm(g, tiles):
            if 0 in tiles:
                dve.wait_ge(pool_rs, g + 1)
                if not (isinstance(g, int) and g == 0):
                    dve.wait_ge(pe_xnT, g)
                    dve.wait_ge(pool_t1, NT * g)
            for i in tiles:
                nc.vector.tensor_scalar(xn[:, i, :], xb[:, i, :], mv[:, i, 0:1], rstd[:, i:i + 1],
                                        ALU.subtract, ALU.mult).then_inc(dve_xn, 1)

        def absmax(g):
            dve.wait_ge(dve_xn, NT * (g + 1))
            nc.vector.tensor_reduce(amax[:], xn[:], AX.X, ALU.max, apply_absolute_value=True).then_inc(dve_amax, 1)

        def scales(g):
            dve.wait_ge(dve_amax, g + 1)
            if not (isinstance(g, int) and g == 0):
                dve.wait_ge(dve_ffn, NT * g)
            nc.vector.tensor_scalar(xscale[:], amax[:], 1e-6, 1.0 / 127.0, ALU.max, ALU.mult).then_inc(dve_xs, 1)
            dve.wait_ge(dve_xs, g + 1)
            nc.vector.reciprocal(xrec[:], xscale[:]).then_inc(dve_xr, 1)

        def ffn_out(g, tiles):
            if 0 in tiles:
                dve.wait_ge(pe_ffn, g + 1)
                if not (isinstance(g, int) and g == 0):
                    dve.wait_ge(pool_b2, g)
            for i in tiles:
                nc.vector.scalar_tensor_tensor(ffn[:, i, :], misc[:, i * P:(i + 1) * P], xscale[:, i:i + 1],
                                               ws_row[:], ALU.mult, ALU.mult).then_inc(dve_ffn, 1)

        def evac_v(g, pg):
            dve.wait_ge(pe_v, g + 1)
            if isinstance(g, int) and g == 0:
                dve.wait_ge(dve_const, 6)
            elif not (isinstance(g, int) and g == 1):
                dve.wait_ge(pe_PV, STEPS * NT * (g - 1))
            nc.vector.tensor_tensor(Va[pg][:, :, :, 0:HD], misc[:].rearrange("p (i h d) -> p i h d", i=NT, d=HD),
                                    bv_row[:].rearrange("p (h d) -> p h d", d=HD).unsqueeze(1)
                                    .to_broadcast([P, NT, H, HD]), ALU.add).then_inc(dve_v, 1)

        def maxima(step, u, par):
            for n in (2 * u, 2 * u + 1):
                qb, h = piece_of(n)
                dve.wait_ge(pe_A, 16 * step + n + 1)
                nc.vector.tensor_reduce(mneg[:, par, qb * HG + h:qb * HG + h + 1], A[n % 2][:, 0:window(qb)[1]], AX.X, ALU.max,
                                        negate=True).then_inc(dve_max, 1)

        def max_parts(step, par):
            dve.wait_ge(dve_max, 16 * (step + 1))
            if not (isinstance(step, int) and step < 2):
                dve.wait_ge(pe_mT, step - 1)
            src = mneg[:, par, :].rearrange("p (q a b) -> p q b a", a=2, b=2)
            dst = mp[:, par, :, :].rearrange("p q (b s a) -> p q b s a", b=2, s=2)
            nc.vector.tensor_copy(dst[:, :, :, 0, :], src).then_inc(dve_mp, 1)
            dve.wait_ge(dve_mp, 2 * step + 1)
            nc.vector.tensor_tensor(dst[:, :, :, 1, :], src, dst[:, :, :, 0, :], ALU.subtract).then_inc(dve_mp, 1)

        def context(g, qb):
            v = misc[:].rearrange("p (h w) -> p h w", w=32)
            dve.wait_ge(pe_ctx, NT * g + qb + 1)
            nc.vector.reciprocal(rec[:, qb, :], v[:, :, HD:HD + 1].rearrange("p h w -> p (h w)")).then_inc(dve_rec, 1)
            dve.wait_ge(dve_rec, NT * g + qb + 1)
            nc.vector.tensor_tensor(ctxn[:, qb, :].rearrange("p (h d) -> p h d", d=HD), v[:, :, 0:HD],
                                    rec[:, qb, :].unsqueeze(2).to_broadcast([P, H, HD]), ALU.mult).then_inc(dve_ctx, 1)

        def out_x1(g):
            dve.wait_ge(pe_out, g + 1)
            dve.wait_ge(dma_base_r, 16 * (g + 1))
            nc.vector.tensor_tensor(x1s[:].rearrange("p i d -> p (i d)"), misc[:],
                                    base_r[:].rearrange("p i d -> p (i d)"), ALU.add).then_inc(dve_x1, 1)

        def clear_k(i):
            for par in range(2):
                heads = slice(H // 2, H) if par == 0 else slice(0, H // 2)
                nc.vector.memset(Ks[i][64 * par:64 * par + 64, heads, :].bitcast(F32), 0.0).then_inc(dve_fill, 1)

        bn(0, range(NT))
        ag(0)
        norm(0, range(NT))
        absmax(0)
        scales(0)
        dve.wait_ge(dma_w, 16 * NCONST)
        nc.vector.tensor_copy(wq[:], wq8[:].bitcast(mybir.dt.int8)).then_inc(dve_const, 1)
        nc.vector.tensor_tensor(bsum_row[:], bo_row[:], fb_row[:], ALU.add).then_inc(dve_const, 1)
        dve.wait_ge(pool_fill, 1)
        clear_k(0)
        bn(1, range(NT))
        ag(1)
        norm(1, range(NT))
        for va in Va:
            nc.vector.memset(va[:], 0.0).then_inc(dve_const, 1)
        dve.wait_ge(dve_const, 4)
        for va in Va:
            nc.vector.memset(va[:, :, :, HD:HD + 1], 1.0).then_inc(dve_const, 1)
        ffn_out(0, range(NT))
        evac_v(0, 0)
        absmax(1)
        scales(1)
        dve.wait_ge(pool_fill, 3)
        clear_k(1)
        for u in range(UNITS):
            maxima(0, u, 0)
            if u == 6:
                ffn_out(1, range(NT))
        max_parts(0, 0)
        for u in range(UNITS // 2):
            maxima(1, u, 1)

        def body(b, p, first, last):
            for u in range(SLOTS):
                hg = u // UNITS
                step = STEPS * b + hg
                if u == 2 and first:
                    max_parts(1, 1)
                for n, v in ahead(u, first):
                    if not (last and hg + n >= STEPS):
                        maxima(step + n, v, (hg + n) % 2)
                if u % UNITS == 1 and not (first and hg == 0) and not (last and hg == STEPS - 1):
                    max_parts(step + 1, (hg + 1) % 2)
                if u == 3 and not last:
                    evac_v(b + 1, 1 - p)
                if u in (5, 7, 9, 11) and not first:
                    context(b - 1, (u - 5) // 2)
                if u == 15 and not first:
                    out_x1(b - 1)
                if not last:
                    if u in (4, 6):
                        bn(b + 2, range(u - 4, u - 2))
                    if u == 7:
                        ag(b + 2)
                    if 10 <= u < 14:
                        norm(b + 2, [u - 10])
                    if u == 14:
                        absmax(b + 2)
                    if u == 15:
                        scales(b + 2)
                    if u >= SLOTS - NT:
                        ffn_out(b + 2, [u - (SLOTS - NT)])
            if not first:
                dve.wait_ge(dma_x1, 16 * b)

        batches(dve, body)
        for qb in range(NT):
            context(NB - 1, qb)
        out_x1(NB - 1)

    @block.tensor
    def _(pe):
        def turn_xn(g, before):
            pe.wait_ge(dve_xn, NT * (g + 1))
            pe.wait_ge(*before)
            for i in range(NT):
                mm = nc.tensor.transpose(misc[:, i * P:(i + 1) * P], xn[:, i, :], ident[:])
            mm.then_inc(pe_xnT, 1)

        def project(g, pg, which, done, before):
            pe.wait_ge(act_xnT, g + 1)
            pe.wait_ge(*before)
            nc.tensor.matmul(misc[:], w_in[:, which * P:(which + 1) * P], xnT[pg][:], start=True, stop=True)\
                .then_inc(done, 1)

        def values(g, pg, before):
            pe.wait_ge(act_xnT, g + 1)
            pe.wait_ge(*before)
            for i in range(NT):
                mm = nc.tensor.matmul(misc[:, i * P:(i + 1) * P], xnT[pg][:, i * P:(i + 1) * P],
                                      w_in[:, 2 * P:3 * P], start=True, stop=True)
            mm.then_inc(pe_v, 1)

        def turn_xq(g, before):
            pe.wait_ge(pool_xq, g + 1)
            pe.wait_ge(*before)
            for i in range(NT):
                mm = nc.tensor.transpose(misc16[:, i * P:(i + 1) * P], xq[:, i, :], ident16[:])
            mm.then_inc(pe_xqT, 1)

        def ffn_mm(g, before):
            pe.wait_ge(act_xqT, g + 1)
            pe.wait_ge(*before)
            for i in range(NT):
                mm = nc.tensor.matmul(misc[:, i * P:(i + 1) * P], xqT[:, i * P:(i + 1) * P], wq[:],
                                      start=True, stop=True)
            mm.then_inc(pe_ffn, 1)

        def piece(step, n, hgs, pg):
            qb, h = piece_of(n)
            h += HG * hgs
            lo, w = window(qb)
            idx = 16 * step + n
            if not (isinstance(step, int) and step == 0 and n < 2):
                pe.wait_ge(dve_max, idx - 1)
            out = A[n % 2]
            nc.tensor.matmul(out[:, 0:w], Qs[pg][:, h // 2, qb * P:(qb + 1) * P], Ks[pg][:, k_slot(h), lo:lo + w],
                             start=True, stop=True)
            if qb > 0:
                mm = nc.tensor.matmul(out[:, 0:P], ident16[:], mask_lo[:], start=False, stop=True,
                                      skip_group_check=True)
            if qb < NT - 1:
                mm = nc.tensor.matmul(out[:, w - P:w], ident16[:], mask_hi[:], start=False, stop=True,
                                      skip_group_check=True)
            mm.then_inc(pe_A, 1)

        def turn_max(step, par, before):
            pe.wait_ge(dve_mp, 2 * (step + 1))
            pe.wait_ge(*before)
            for qb in range(NT):
                mm = nc.tensor.transpose(misc16[0:8, qb * P:(qb + 1) * P], mp[:, par, qb, :], ident16[:])
            mm.then_inc(pe_mT, 1)

        def scores(b, u, p):
            hg, kt, half = u // UNITS, (u % UNITS) // 2, u % 2
            lo, w = window(kt)
            if u % UNITS == 0:
                pe.wait_ge(dma_m, 32 * (STEPS * b + hg + 1))
            if not (isinstance(b, int) and b == 0 and u < 2):
                pe.wait_ge(act_exp, SLOTS * b + u - 1)
            for j in range(2):
                h = HG * hg + 2 * half + j
                mm = nc.tensor.matmul(SB[u % 2][:, j, 0:w], Ks[p][:, k_slot(h), kt * P:(kt + 1) * P],
                                      Qs[p][:, h // 2, lo:lo + w], start=True, stop=True)
            mm.then_inc(pe_B, 1)

        def attend(step, hg, kt, p):
            pe.wait_ge(pool_mask, NMASK * step + MASKS[kt])
            if kt == 0 and not (isinstance(step, int) and step == 0):
                pe.wait_ge(act_pv, step)
            lo, w = window(kt)
            for c in range(HG):
                mm = nc.tensor.matmul(PV[32 * c:32 * c + 32, lo:lo + w], Va[p][:, kt, HG * hg + c, :],
                                      Pb[:, kt, c, 0:w], start=kt == 0, stop=True, skip_group_check=True,
                                      tile_position=(0, 32 * c))
            mm.then_inc(pe_PV, 1)

        def turn_ctx(g, qb, before):
            pe.wait_ge(act_pv, STEPS * (g + 1))
            pe.wait_ge(*before)
            for hg in range(STEPS):
                mm = nc.tensor.transpose(misc[:, hg * P:(hg + 1) * P], cs[:, hg, qb * P:(qb + 1) * P], ident[:])
            mm.then_inc(pe_ctx, 1)

        def turn_ctxn(g, before):
            pe.wait_ge(dve_ctx, NT * (g + 1))
            pe.wait_ge(*before)
            for qb in range(NT):
                mm = nc.tensor.transpose(misc[:, qb * P:(qb + 1) * P], ctxn[:, qb, :], ident[:])
            mm.then_inc(pe_ctxT, 1)

        def out_mm(g):
            pe.wait_ge(act_ctxT, g + 1)
            for i in range(NT):
                mm = nc.tensor.matmul(misc[:, i * P:(i + 1) * P], ctxT[:, i * P:(i + 1) * P], w_out[:],
                                      start=True, stop=True)
            mm.then_inc(pe_out, 1)

        pe.wait_ge(pool_const, 9)
        pe.wait_ge(dma_w, 16 * NCONST)
        pe.wait_ge(dve_const, 1)
        turn_xn(0, (dve_xn, NT))
        project(0, 0, 0, pe_q, (act_xnT, 1))
        project(0, 0, 1, pe_k, (act_q1, 1))
        turn_xq(0, (act_k1, 1))
        pe.wait_ge(dve_const, 1)
        ffn_mm(0, (act_xqT, 1))
        values(0, 0, (dve_ffn, NT))
        turn_xn(1, (dve_v, 1))
        project(1, 1, 0, pe_q, (act_xnT, 2))
        project(1, 1, 1, pe_k, (act_q1, 2))
        pe.wait_ge(dma_stack, 16 * NLOAD)
        for n in range(2 * UNITS):
            piece(0, n, 0, 0)
            if n == 7:
                turn_xq(1, (act_k1, 2))
            if n == 11:
                ffn_mm(1, (act_xqT, 2))
        turn_max(0, 0, (dve_ffn, 2 * NT))
        for n in range(UNITS):
            piece(1, n, 1, 0)

        def body(b, p, first, last):
            o = 1 - p
            for u in range(SLOTS):
                hg, v = u // UNITS, u % UNITS
                step = STEPS * b + hg
                if not last and u == 2 * UNITS:
                    pe.wait_ge(dma_stack, 16 * NLOAD * (b + 2))
                scores(b, u, p)
                for k, unit in ahead(u, first):
                    if not (last and hg + k >= STEPS):
                        for n in (2 * unit, 2 * unit + 1):
                            piece(step + k, n, (hg + k) % STEPS, p if hg + k < STEPS else o)
                if u == 2 and not first:
                    turn_max(step + 1, 1, (dve_ffn, NT * ((b + 2) if not last else NB)))
                elif u == 3 and first:
                    turn_max(step + 1, 1, (act_mT, 1))
                elif u == 10:
                    turn_max(step + 1, 0, (dve_ctx, NT * (b - 1) + 3) if not first else (act_mT, step + 1))
                elif u == 18:
                    turn_max(step + 1, 1, (act_xnT, b + 3) if not last else (dve_x1, b))
                elif u == 26 and not last:
                    turn_max(step + 1, 0, (act_xqT, b + 3))
                if u == 3 and not last:
                    values(b + 1, o, (act_mT, STEPS * b + 2))
                if not first:
                    if u in (5, 7, 9, 11):
                        turn_ctx(b - 1, (u - 5) // 2, {5: (dve_v, b + 2) if not last else (act_mT, STEPS * b + 2),
                                                       11: (act_mT, STEPS * b + 3)}
                                 .get(u, (dve_ctx, NT * (b - 1) + (u - 5) // 2)))
                    if u == 12:
                        turn_ctxn(b - 1, (act_mT, STEPS * b + 3))
                    if u == 14:
                        out_mm(b - 1)
                if not last:
                    if u == 16:
                        turn_xn(b + 2, (dve_x1, b) if not first else (act_mT, STEPS * b + 3))
                    if u == 20:
                        project(b + 2, p, 0, pe_q, (act_mT, STEPS * b + 4))
                    if u == 22:
                        project(b + 2, p, 1, pe_k, (act_q1, b + 3))
                    if u == 24:
                        turn_xq(b + 2, (act_k1, b + 3))
                    if u == 28:
                        ffn_mm(b + 2, (act_mT, STEPS * b + 5))
                if v in (1, 3) and not (first and hg == 0):
                    attend(step - 1, (hg - 1) % STEPS, NT - 2 + v // 2, p if hg else o)
                elif v in (5, 7):
                    attend(step, hg, (v - 5) // 2, p)

        batches(pe, body)
        attend(STEPS * NB - 1, STEPS - 1, NT - 2, 1)
        attend(STEPS * NB - 1, STEPS - 1, NT - 1, 1)
        for qb in range(NT):
            turn_ctx(NB - 1, qb, (act_mT, STEPS * NB) if qb == 0 else (dve_ctx, NT * (NB - 1) + qb))
        turn_ctxn(NB - 1, (act_mT, STEPS * NB))
        out_mm(NB - 1)


NE = 8
HID = 256
TOPK = 2
TOKENS = NB * T
ROW = P + 2
CAP = TOKENS + P
NTILES = -(-(TOKENS * TOPK + NE * (P - 1)) // P // 8) * 8


def layer1(nc, ctx, x1, WqT, bq, WkT, bk, WvT, bv, nscale, wrT, xs, x2b, tab, w_up, w_dn, w_up_in, w_dn_in):

    def sb(name, shape, dt=F32):
        return ctx.enter_context(nc.sbuf_tensor(name, shape, dt))

    def sem(name):
        return ctx.enter_context(nc.semaphore(name))

    wq, wk, wv = (sb(n, [P, P]) for n in ("l1_wq", "l1_wk", "l1_wv"))
    bqc, bqs, bkc, nsc = (sb(n, [P, 1]) for n in ("l1_bq", "l1_bqs", "l1_bk", "l1_ns"))
    bvr = sb("l1_bv", [P, P])
    nsr = sb("l1_nsr", [P, P])
    wr = sb("l1_wr", [P, NE])
    wrs = sb("l1_wrs", [P, NE])
    ident = sb("l1_ident", [P, P])
    tri = sb("l1_tri", [P, P], BF16)
    ones = sb("l1_ones", [P, P], BF16)
    mhalf = sb("l1_mhalf", [P, NT])
    iota8i = sb("iota8i", [P, NE], I32)
    iota8 = sb("iota8", [P, NE])
    ebase = sb("ebase", [P, NE])
    dest_i = sb("dest_i", [P, NT * TOPK], I32)
    dest = sb("dest", [P, NT * TOPK])
    part_i = sb("part_i", [P, 1], I32)
    part_f = sb("part_f", [P, 1])
    tile_i = sb("tile_i", [1, NTILES], I32)
    tile_f = sb("tile_f", [1, NTILES])
    nine_i = sb("nine_i", [1, NE + 1], I32)
    nine_f = sb("nine_f", [1, NE + 1])
    upto = sb("upto", [1, NE, NE])
    padrow = sb("padrow", [P, ROW])

    xb = [sb(f"l1_xb{i}", [P, NT, P]) for i in range(2)]
    stats = sb("l1_stats", [P, NT, 6])
    mv = sb("l1_mv", [P, NT, 2])
    veps = sb("l1_veps", [P, NT])
    rstd = sb("l1_rstd", [P, NT])
    xn = [sb(f"l1_xn{i}", [P, NT, P]) for i in range(2)]
    junk = sb("l1_junk", [P, NT, P])
    ssq = sb("l1_ssq", [P, NT])
    meps = sb("l1_meps", [P, NT])
    rr = [sb(f"l1_rr{i}", [P, NT]) for i in range(2)]
    base = [sb(f"l1_base{i}", [P, NT, P]) for i in range(2)]
    xnT = sb("l1_xnT", [P, T])
    qT = [sb(f"l1_qT{i}", [P, T]) for i in range(2)]
    kT = [sb(f"l1_kT{i}", [P, T]) for i in range(2)]
    v = [sb(f"l1_v{i}", [P, NT, P]) for i in range(2)]
    mneg = sb("l1_mneg", [P, NT])
    ssum = sb("l1_ssum", [P, NT])
    srec = sb("l1_srec", [P, NT])
    vs = sb("l1_vs", [P, NT, P])
    pr = sb("l1_pr", [P, NT, T])
    sc = sb("sc", [P, NT, NE])
    mx = sb("mx", [P, NT, NE])
    ix = sb("ix", [P, NT, NE], U32)
    ixf = sb("ixf", [P, NT, NE])
    oh = [sb(f"oh{i}", [P, NT, TOPK, NE]) for i in range(2)]
    dm = sb("dm", [P, NT])
    em = sb("em", [P, NT])
    den = sb("den", [P, NT])
    w1 = sb("w1", [P, NT])
    w2 = sb("w2", [P, NT])
    M = [sb(f"M{i}", [P, NT, NE], BF16) for i in range(2)]
    S = [sb(f"S{i}", [P, NE], BF16) for i in range(2)]
    msum = sb("msum", [P, NE])
    Re = sb("Re", [P, NT, NE])
    prod = sb("prod", [P, NT, TOPK, NE])
    posf = sb("posf", [P, NT, TOPK])
    pos = [sb(f"pos{i}", [P, NT, TOPK], U32) for i in range(2)]
    pay = [sb(f"pay{i}", [P, TOPK, NT, ROW]) for i in range(2)]
    cnt = sb("cnt", [P, NE])
    padp = sb("padp", [P, NE])
    padi = sb("padi", [P, NE], U32)
    nt_a = sb("nt_a", [P, NE])
    nt_f = sb("nt_f", [P, NE])
    cprod = sb("cprod", [1, NE, NE])
    cum = sb("cum", [1, NE])
    vals = sb("vals", [1, NE + 1])
    cx = sb("cx", [1, NE])
    le = sb("le", [1, NTILES, NE])
    et = sb("et", [1, NTILES])
    oh9 = sb("oh9", [1, NTILES, NE + 1])
    pv9 = sb("pv9", [1, NTILES, NE + 1])
    bt = sb("bt", [1, NTILES])
    bt2 = sb("bt2", [1, NTILES])

    Sb = [ctx.enter_context(nc.psum_tensor(f"l1_S{i}", [P, 512], F32)) for i in range(NT)]
    XV = ctx.enter_context(nc.psum_tensor("l1_XV", [P, 512], F32))
    QK = ctx.enter_context(nc.psum_tensor("l1_QK", [P, 512], F32))
    RT = ctx.enter_context(nc.psum_tensor("l1_RT", [P, 512], F32))
    OU = ctx.enter_context(nc.psum_tensor("l1_OU", [P, 512], F32))
    sp_passed, pool_passed, dve_passed = (sem("l1s_passed_" + n) for n in ("sp", "pool", "dve"))
    names = """w x pad_hw const cdve ve rs rms_e rr base pay2 sq xnT qT kT exp em bqs
        bn ag xn max v rec vs out payx ra rb fin
        p_xnT p_q p_k p_v p_r p_rank p_S p_out p_cnt sc_dma pad_dma""".split()
    s = {n: sem("l1s_" + n) for n in names}
    dma_w, dma_x, dma_pad_hw, dma_ex = s["w"], s["x"], s["pad_hw"], sem("l1s_ex")
    pool_const, pool_ve, pool_rs, pool_me, pool_rr, pool_base = (s[n] for n in "const ve rs rms_e rr base".split())
    act_pay2, act_sq, act_xnT, act_q, act_k, act_exp, act_em, act_bqs = (
        s[n] for n in "pay2 sq xnT qT kT exp em bqs".split())
    dve_const, dve_bn, dve_ag, dve_xn, dve_max, dve_v, dve_rec, dve_vs, dve_out, dve_payx, dve_ra, dve_rb, dve_fin = (
        s[n] for n in "cdve bn ag xn max v rec vs out payx ra rb fin".split())
    pe_xnT, pe_q, pe_k, pe_v, pe_r, pe_rank, pe_S, pe_out, pe_cnt = (
        s[n] for n in "p_xnT p_q p_k p_v p_r p_rank p_S p_out p_cnt".split())
    dma_rows, dma_pads = [sem(f"l1s_rows{i}") for i in range(2)], s["pad_dma"]

    NW = 11
    NCP = 11
    RA = 13
    RB = 11
    ISC = float(P) ** -0.5

    def batches(eng, body):
        body(0, 0, False, 0)
        with eng.Fori(0, (NB - 2) // 2) as i:
            body(2 * i + 1, 1, False, i + 1)
            body(2 * i + 2, 0, False, i + 1)
        body(NB - 1, 1, True, 0)

    block = ctx.enter_context(nc.Block())

    @block.sync
    def _(sp):
        def wait(sem, value):
            sp.wait_ge(sem, value)
            if not isinstance(value, int):
                sp.sem_inc(sp_passed)

        xv = x1.rearrange("b (i p) d -> b p i d", p=P)
        sp.dma_start(xb[0][:], xv[0]).then_inc(dma_x, 16)
        for dst, src in ((wq, WqT), (wk, WkT), (wv, WvT), (wr, wrT)):
            sp.dma_start(dst[:], src).then_inc(dma_w, 16)
        for dst, src in ((bqc, bq), (bkc, bk), (nsc, nscale)):
            sp.dma_start(dst[:], src.rearrange("(p a) -> p a", a=1)).then_inc(dma_w, 16)
        for dst, src in ((bvr, bv), (nsr, nscale)):
            sp.dma_start(dst[:], src.partition_broadcast(P)).then_inc(dma_w, 16)
        wait(dma_x, 16)
        sp.dma_start(xb[1][:], xv[1]).then_inc(dma_x, 16)
        sp.dma_start(w_up[:], w_up_in).then_inc(dma_ex, 16)
        sp.dma_start(w_dn[:], w_dn_in).then_inc(dma_ex, 16)
        wait(dve_const, 4)
        sp.dma_start(xs[NE * CAP:NE * CAP + P, :], padrow[:]).then_inc(dma_pad_hw, 16)

        def body(g, p, last, prior):
            if not last:
                wait(pool_base, g + 1)
                wait(dma_x, 16 * (g + 2))
                sp.dma_start(xb[p][:], xv[(g + 2) % NB]).then_inc(dma_x, 16)

        batches(sp, body)
        wait(dma_pad_hw, 16)
        wait(dma_ex, 32)

    @block.gpsimd
    def _(pool):
        def wait(sem, value):
            pool.wait_ge(sem, value)
            if not isinstance(value, int):
                pool.sem_inc(pool_passed)

        pool.memset(ident[:], 0.0).then_inc(pool_const, 1)
        pool.memset(tri[:], 1.0).then_inc(pool_const, 1)
        pool.memset(ones[:], 1.0).then_inc(pool_const, 1)
        pool.memset(mhalf[:], -0.5).then_inc(pool_const, 1)
        wait(pool_const, 4)
        pool.affine_select(out=ident[:], in_=ident[:], compare_op=ALU.not_equal, fill=1.0, base=0,
                           pattern=[[-1, P]], channel_multiplier=1).then_inc(pool_const, 1)
        pool.affine_select(out=tri[:], in_=tri[:], compare_op=ALU.is_gt, fill=0.0, base=0,
                           pattern=[[1, P]], channel_multiplier=-1).then_inc(pool_const, 1)
        pool.iota(iota8i[:], [[1, NE]], base=0, channel_multiplier=0).then_inc(pool_const, 1)
        pool.iota(dest_i[:], [[TOPK * P, NT], [1, TOPK]], base=0, channel_multiplier=TOPK).then_inc(pool_const, 1)
        pool.iota(part_i[:], [[1, 1]], base=0, channel_multiplier=1).then_inc(pool_const, 1)
        pool.iota(tile_i[:], [[1, NTILES]], base=0, channel_multiplier=0).then_inc(pool_const, 1)
        pool.iota(nine_i[:], [[1, NE + 1]], base=0, channel_multiplier=0).then_inc(pool_const, 1)

        def rstd_of(g):
            wait(dve_ag, NT * (g + 1))
            pool.tensor_scalar(veps[:], mv[:, :, 1], 1e-5, None, ALU.add).then_inc(pool_ve, 1)
            wait(pool_ve, g + 1)
            pool.tensor_tensor(rstd[:], veps[:], mhalf[:], ALU.pow).then_inc(pool_rs, 1)

        def rms_of(g, pg):
            wait(act_sq, NT * (g + 1))
            pool.tensor_scalar(meps[:], ssq[:], 1.0 / P, 1e-6, ALU.mult, ALU.add).then_inc(pool_me, 1)
            wait(pool_me, g + 1)
            pool.tensor_tensor(rr[pg][:], meps[:], mhalf[:], ALU.pow).then_inc(pool_rr, 1)

        def base_of(g, pg):
            wait(dve_xn, NT * (g + 1))
            if not (isinstance(g, int) and g < 2):
                wait(dve_out, g - 1)
            pool.tensor_tensor(base[pg][:], xb[pg][:], xn[pg][:], ALU.add).then_inc(pool_base, 1)

        def scatter(g, p):
            wait(dve_rb, RB * (g + 1))
            wait(act_pay2, g + 1)
            for i in range(NT):
                for k in range(TOPK):
                    pool.indirect_dma_start(
                        out=xs[:, :], out_offset=bass.IndirectOffsetOnAxis(ap=pos[p][:, i, k:k + 1], axis=0),
                        in_=pay[p][:, k, i, :], in_offset=None).then_inc(dma_rows[p], 16)

        rstd_of(0)
        rms_of(0, 0)
        rstd_of(1)
        base_of(0, 0)

        def body(g, p, last, prior):
            if not last:
                rms_of(g + 1, 1 - p)
                rstd_of(g + 2)
                base_of(g + 1, 1 - p)
            scatter(g, p)

        batches(pool, body)
        wait(dve_fin, 3)
        for e in range(NE):
            pool.indirect_dma_start(out=xs[:, :], out_offset=bass.IndirectOffsetOnAxis(ap=padi[:, e:e + 1], axis=0),
                                    in_=padrow[:], in_offset=None).then_inc(dma_pads, 16)
        for rows in dma_rows:
            wait(rows, 16 * TOPK * NT * NB // 2)
        wait(dma_pads, 16 * NE)

    @block.scalar
    def _(act):
        act.wait_ge(dma_w, 16 * 9)
        act.activation(bqs[:], bqc[:], ACT.Copy, scale=ISC).then_inc(act_bqs, 1)

        def squares(g, pg):
            act.wait_ge(pool_rr, g)
            for i in range(NT):
                act.wait_ge(dve_xn, NT * g + i + 1)
                act.activation(junk[:, i, :], xn[pg][:, i, :], ACT.Square, accum_out=ssq[:, i:i + 1]).then_inc(act_sq, 1)

        def evac_xnT(g):
            act.wait_ge(pe_xnT, g + 1)
            act.activation(xnT[:], XV[:], ACT.Copy).then_inc(act_xnT, 1)

        def evac_q(g, pg):
            act.wait_ge(pe_q, g + 1)
            act.activation(qT[pg][:], QK[:], ACT.Identity, bias=bqs[:, 0:1], scale=ISC).then_inc(act_q, 1)

        def evac_k(g, pg):
            act.wait_ge(pe_k, g + 1)
            act.activation(kT[pg][:], QK[:], ACT.Identity, bias=bkc[:, 0:1]).then_inc(act_k, 1)

        def gate_exp(g):
            act.wait_ge(dve_ra, RA * (g + 1))
            act.wait_ge(dve_rb, RB * g)
            act.activation(em[:], dm[:], ACT.Exp).then_inc(act_em, 1)

        def copy_rows(g, pg):
            act.wait_ge(dve_payx, NT * (g + 1))
            act.activation(pay[pg][:, 1, :, 0:P], pay[pg][:, 0, :, 0:P], ACT.Copy).then_inc(act_pay2, 1)

        act.wait_ge(act_bqs, 1)
        squares(0, 0)
        squares(1, 1)
        evac_xnT(0)
        evac_q(0, 0)
        evac_k(0, 0)
        copy_rows(0, 0)

        def body(g, p, last, prior):
            for kt in range(NT):
                act.wait_ge(dve_max, NT * g + kt + 1)
                act.wait_ge(pe_out, g)
                act.wait_ge(dve_rec, NT * g)
                act.activation(pr[:, kt, :], Sb[kt][:], ACT.Exp, bias=mneg[:, kt:kt + 1],
                               accum_out=ssum[:, kt:kt + 1]).then_inc(act_exp, 1)
            gate_exp(g)
            if not last:
                evac_xnT(g + 1)
                evac_q(g + 1, 1 - p)
                evac_k(g + 1, 1 - p)
                squares(g + 2, p)
                copy_rows(g + 1, 1 - p)

        batches(act, body)

    @block.vector
    def _(dve):
        dve.wait_ge(pool_const, NCP)
        nc.vector.tensor_copy(iota8[:], iota8i[:]).then_inc(dve_const, 1)
        nc.vector.tensor_scalar(ebase[:], iota8i[:], float(CAP), None, ALU.mult).then_inc(dve_const, 1)
        nc.vector.memset(padrow[:], 0.0).then_inc(dve_const, 1)
        dve.wait_ge(dve_const, 3)
        nc.vector.memset(padrow[:, P + 1:P + 2].bitcast(I32), TOKENS * TOPK).then_inc(dve_const, 1)
        nc.vector.tensor_scalar(dest[:], dest_i[:], -float(TOPK * T), None, ALU.add).then_inc(dve_const, 1)
        nc.vector.tensor_copy(part_f[:], part_i[:]).then_inc(dve_const, 1)
        nc.vector.tensor_copy(tile_f[:], tile_i[:]).then_inc(dve_const, 1)
        nc.vector.tensor_copy(nine_f[:], nine_i[:]).then_inc(dve_const, 1)
        nc.vector.memset(S[0][:], 0.0).then_inc(dve_const, 1)
        nc.vector.tensor_tensor(upto[:], iota8[0:1, :].unsqueeze(1).to_broadcast([1, NE, NE]),
                                iota8[0:1, :].unsqueeze(2).to_broadcast([1, NE, NE]), ALU.is_le).then_inc(dve_const, 1)
        dve.wait_ge(dma_w, 16 * 9)
        nc.vector.tensor_scalar(wrs[:], wr[:], nsc[:, 0:1], None, ALU.mult).then_inc(dve_const, 1)
        dve.wait_ge(dve_const, 11)

        def stat(g, pg):
            dve.wait_ge(dma_x, 16 * (g + 1))
            dve.wait_ge(pool_ve, g)
            for i in range(NT):
                nc.vector.bn_stats(stats[:, i, :], xb[pg][:, i, :]).then_inc(dve_bn, 1)
            for i in range(NT):
                dve.wait_ge(dve_bn, NT * g + i + 1)
                if not isinstance(g, int):
                    dve.sem_inc(dve_passed)
                nc.vector.bn_aggr(mv[:, i, :], stats[:, i, :]).then_inc(dve_ag, 1)

        def norm_of(g, pg):
            dve.wait_ge(pool_rs, g + 1)
            for i in range(NT):
                nc.vector.tensor_scalar(xn[pg][:, i, :], xb[pg][:, i, :], mv[:, i, 0:1], rstd[:, i:i + 1],
                                        ALU.subtract, ALU.mult).then_inc(dve_xn, 1)

        def row_of(g, pg, before):
            dve.wait_ge(dma_rows[pg], 16 * TOPK * NT * before)
            dve.wait_ge(pool_rr, g + 1)
            dve.wait_ge(dve_xn, NT * (g + 1))
            for i in range(NT):
                nc.vector.scalar_tensor_tensor(pay[pg][:, 0, i, 0:P], xn[pg][:, i, :], rr[pg][:, i:i + 1], nsr[:],
                                               ALU.mult, ALU.mult).then_inc(dve_payx, 1)

        def evac_v(g, pg):
            dve.wait_ge(pe_v, g + 1)
            nc.vector.tensor_tensor(v[pg][:], XV[:].rearrange("p (i d) -> p i d", i=NT),
                                    bvr[:].unsqueeze(1).to_broadcast([P, NT, P]), ALU.add).then_inc(dve_v, 1)

        def route_a(g, pg):
            done = [RA * g]

            def step(ins, wait=True):
                ins.then_inc(dve_ra, 1)
                done[0] = done[0] + 1
                if wait:
                    dve.wait_ge(dve_ra, done[0])
                    if not isinstance(g, int):
                        dve.sem_inc(dve_passed)

            dve.wait_ge(pe_r, g + 1)
            dve.wait_ge(act_em, g)
            step(nc.vector.tensor_tensor(sc[:], RT[:, 0:NT * NE].rearrange("p (i e) -> p i e", e=NE),
                                         rr[pg][:].unsqueeze(2).to_broadcast([P, NT, NE]), ALU.mult))
            for i in range(NT):
                step(nc.vector.max(mx[:, i, :], sc[:, i, :]), i == NT - 1)
            for i in range(NT):
                step(nc.vector.max_index(ix[:, i, :], mx[:, i, :], sc[:, i, :]), i == NT - 1)
            step(nc.vector.tensor_copy(ixf[:], ix[:]))
            step(nc.vector.tensor_tensor(oh[pg][:], iota8[:].unsqueeze(1).unsqueeze(1).to_broadcast([P, NT, TOPK, NE]),
                                         ixf[:, :, 0:TOPK].unsqueeze(3).to_broadcast([P, NT, TOPK, NE]), ALU.is_equal))
            step(nc.vector.tensor_tensor(M[pg][:], oh[pg][:, :, 0, :], oh[pg][:, :, 1, :], ALU.add), False)
            step(nc.vector.tensor_tensor(dm[:], mx[:, :, 1], mx[:, :, 0], ALU.subtract))
            assert True

        def ranks(g):
            dve.wait_ge(pe_rank, g + 1)
            dve.wait_ge(dve_rb, RB * g)
            nc.vector.tensor_tensor(Re[:], RT[:, 64:64 + NT * NE].rearrange("p (i e) -> p i e", e=NE),
                                    ebase[:].unsqueeze(1).to_broadcast([P, NT, NE]), ALU.add).then_inc(dve_rb, 1)

        def route_b(g, p):
            done = [RB * g]

            def step(ins, wait=True):
                ins.then_inc(dve_rb, 1)
                done[0] = done[0] + 1
                if wait:
                    dve.wait_ge(dve_rb, done[0])

            done[0] = done[0] + 1
            dve.wait_ge(dve_rb, done[0])
            step(nc.vector.tensor_tensor(prod[:], oh[p][:], Re[:].unsqueeze(2).to_broadcast([P, NT, TOPK, NE]),
                                         ALU.mult))
            step(nc.vector.tensor_reduce(posf[:], prod[:], AX.X, ALU.add))
            step(nc.vector.tensor_copy(pos[p][:], posf[:]), False)
            step(nc.vector.tensor_reduce(msum[:], M[p][:].rearrange("p i e -> p e i"), AX.X, ALU.add))
            step(nc.vector.tensor_tensor(S[1 - p][:], S[p][:], msum[:], ALU.add), False)
            step(nc.vector.tensor_scalar(dest[:], dest[:], float(TOPK * T), None, ALU.add))
            dve.wait_ge(act_em, g + 1)
            step(nc.vector.tensor_scalar(den[:], em[:], 1.0, None, ALU.add))
            step(nc.vector.tensor_copy(
                pay[p][:, :, :, P + 1].bitcast(I32).rearrange("p k i -> p i k"),
                dest[:].rearrange("p (i k) -> p i k", k=TOPK)))
            step(nc.vector.reciprocal(pay[p][:, 0, :, P], den[:]))
            step(nc.vector.tensor_tensor(pay[p][:, 1, :, P], em[:], pay[p][:, 0, :, P], ALU.mult), False)

        for g in range(2):
            stat(g, g)
            norm_of(g, g)
        row_of(0, 0, 0)
        evac_v(0, 0)
        route_a(0, 0)

        def body(g, p, last, prior):
            o = 1 - p
            for kt in range(NT):
                dve.wait_ge(pe_S, NT * g + kt + 1)
                dve.wait_ge(act_exp, NT * g)
                nc.vector.tensor_reduce(mneg[:, kt:kt + 1], Sb[kt][:], AX.X, ALU.max, negate=True)\
                    .then_inc(dve_max, 1)
            ranks(g)
            if not last:
                stat(g + 2, p)
            for kt in range(NT):
                dve.wait_ge(act_exp, NT * g + kt + 1)
                dve.wait_ge(pe_out, g)
                nc.vector.reciprocal(srec[:, kt:kt + 1], ssum[:, kt:kt + 1]).then_inc(dve_rec, 1)
                dve.wait_ge(dve_rec, NT * g + kt + 1)
                dve.wait_ge(dve_v, g + 1)
                nc.vector.tensor_scalar(vs[:, kt, :], v[p][:, kt, :], srec[:, kt:kt + 1], ISC, ALU.mult, ALU.mult)\
                    .then_inc(dve_vs, 1)
            route_b(g, p)
            if not last:
                evac_v(g + 1, o)
                norm_of(g + 2, p)
                route_a(g + 1, o)
            dve.wait_ge(pe_out, g + 1)
            dve.wait_ge(pool_base, g + 1)
            nc.vector.tensor_tensor(x2b[:, bass.ds(g * NT, NT), :], OU[:].rearrange("p (i d) -> p i d", i=NT),
                                    base[p][:], ALU.add).then_inc(dve_out, 1)
            if not last:
                row_of(g + 1, o, prior)

        batches(dve, body)
        fin = [0]

        def step(ins, wait=True):
            ins.then_inc(dve_fin, 1)
            fin[0] += 1
            if wait:
                dve.wait_ge(dve_fin, fin[0])

        dve.wait_ge(pe_cnt, 1)
        step(nc.vector.tensor_copy(cnt[:], RT[:, 128:128 + NE]))
        step(nc.vector.scalar_tensor_tensor(padp[:], cnt[:], part_f[:, 0:1], ebase[:], ALU.add, ALU.add))
        step(nc.vector.tensor_copy(padi[:], padp[:]), False)
        step(nc.vector.tensor_scalar(nt_a[:], cnt[:], 1.0 / P, (P - 1) / P - (P - 1) / (2 * P), ALU.mult, ALU.add))
        step(nc.vector.tensor_scalar(nt_f[:], nt_a[:], MAGIC, MAGIC, ALU.add, ALU.subtract))
        step(nc.vector.tensor_tensor(cprod[:], upto[:], nt_f[0:1, :].unsqueeze(1).to_broadcast([1, NE, NE]), ALU.mult))
        step(nc.vector.tensor_reduce(cum[:], cprod[:], AX.X, ALU.add))
        step(nc.vector.tensor_tensor(cx[:], cum[:], nt_f[0:1, :], ALU.subtract))
        step(nc.vector.scalar_tensor_tensor(vals[:, 0:NE], cx[:], -float(P), ebase[0:1, :], ALU.mult, ALU.add), False)
        step(nc.vector.memset(vals[:, NE:NE + 1], float(NE * CAP)))
        step(nc.vector.tensor_tensor(le[:], cum[:].unsqueeze(1).to_broadcast([1, NTILES, NE]),
                                     tile_f[:].unsqueeze(2).to_broadcast([1, NTILES, NE]), ALU.is_le))
        step(nc.vector.tensor_reduce(et[:], le[:], AX.X, ALU.add))
        step(nc.vector.tensor_tensor(oh9[:], nine_f[:].unsqueeze(1).to_broadcast([1, NTILES, NE + 1]),
                                     et[:].unsqueeze(2).to_broadcast([1, NTILES, NE + 1]), ALU.is_equal))
        step(nc.vector.tensor_tensor(pv9[:], oh9[:], vals[:].unsqueeze(1).to_broadcast([1, NTILES, NE + 1]), ALU.mult))
        step(nc.vector.tensor_reduce(bt[:], pv9[:], AX.X, ALU.add))
        step(nc.vector.scalar_tensor_tensor(bt2[:], tile_f[:], float(P), bt[:], ALU.mult, ALU.add))
        step(nc.vector.tensor_scalar(tab[:, 0, :], bt2[:], float(NE * CAP), None, ALU.min), False)
        step(nc.vector.tensor_scalar(tab[:, 1, :], et[:], float(NE - 1), None, ALU.min))

    @block.tensor
    def _(pe):
        pe.wait_ge(pool_const, NCP)
        pe.wait_ge(dma_w, 16 * 9)
        pe.wait_ge(dve_const, 11)

        def turn(g, pg):
            pe.wait_ge(dve_xn, NT * (g + 1))
            pe.wait_ge(dve_v, g)
            for i in range(NT):
                mm = nc.tensor.transpose(XV[:, i * P:(i + 1) * P], xn[pg][:, i, :], ident[:])
            mm.then_inc(pe_xnT, 1)

        def rank(g, p):
            pe.wait_ge(dve_ra, RA * (g + 1))
            pe.wait_ge(dve_rb, RB * g)
            for i in range(NT):
                out = RT[:, 64 + i * NE:64 + (i + 1) * NE]
                nc.tensor.matmul(out, tri[:], M[p][:, i, :], start=True, stop=False)
                for j in range(i):
                    nc.tensor.matmul(out, ones[:], M[p][:, j, :], start=False, stop=False)
                mm = nc.tensor.matmul(out, ones[:], S[p][:], start=False, stop=True)
            mm.then_inc(pe_rank, 1)

        def q(g):
            pe.wait_ge(act_xnT, g + 1)
            pe.wait_ge(act_k, g)
            nc.tensor.matmul(QK[:], wq[:], xnT[:], start=True, stop=True).then_inc(pe_q, 1)

        def k(g):
            pe.wait_ge(act_q, g + 1)
            nc.tensor.matmul(QK[:], wk[:], xnT[:], start=True, stop=True).then_inc(pe_k, 1)

        def values(g):
            for i in range(NT):
                mm = nc.tensor.matmul(XV[:, i * P:(i + 1) * P], xnT[:, i * P:(i + 1) * P], wv[:],
                                      start=True, stop=True)
            mm.then_inc(pe_v, 1)

        def router(g):
            if not (isinstance(g, int) and g == 0):
                pe.wait_ge(dve_rb, RB * (g - 1) + 1)
            for i in range(NT):
                mm = nc.tensor.matmul(RT[:, i * NE:(i + 1) * NE], xnT[:, i * P:(i + 1) * P], wrs[:],
                                      start=True, stop=True)
            mm.then_inc(pe_r, 1)

        turn(0, 0)
        q(0)
        values(0)
        k(0)
        router(0)

        def body(g, p, last, prior):
            o = 1 - p
            pe.wait_ge(act_k, g + 1)
            pe.wait_ge(act_exp, NT * g)
            for kt in range(NT):
                nc.tensor.matmul(Sb[kt][:], kT[p][:, kt * P:(kt + 1) * P], qT[p][:], start=True, stop=True)\
                    .then_inc(pe_S, 1)
            rank(g, p)
            if not last:
                turn(g + 1, o)
                q(g + 1)
                values(g + 1)
                k(g + 1)
                router(g + 1)
            pe.wait_ge(dve_vs, NT * (g + 1))
            pe.wait_ge(dve_out, g)
            for i in range(NT):
                for kt in range(NT):
                    mm = nc.tensor.matmul(OU[:, i * P:(i + 1) * P], pr[:, kt, i * P:(i + 1) * P], vs[:, kt, :],
                                          start=kt == 0, stop=kt == NT - 1)
            mm.then_inc(pe_out, 1)

        batches(pe, body)
        pe.wait_ge(dve_rb, RB * NB)
        nc.tensor.matmul(RT[:, 128:128 + NE], ones[:], S[0][:], start=True, stop=True).then_inc(pe_cnt, 1)


def experts(nc, ctx, xs, yk, w_up, w_dn, tab):

    def sb(name, shape, dt=F32):
        return ctx.enter_context(nc.sbuf_tensor(name, shape, dt))

    def sem(name):
        return ctx.enter_context(nc.semaphore(name))

    R = 8
    xt = [sb(f"xt{i}", [P, ROW]) for i in range(R)]
    xT = [sb(f"xT{i}", [P, P]) for i in range(2)]
    sg = [sb(f"sg{i}", [P, HID]) for i in range(2)]
    h = [sb(f"h{i}", [P, HID]) for i in range(2)]
    hT = [sb(f"hT{i}", [P, HID]) for i in range(2)]
    y = [sb(f"y{i}", [P, P]) for i in range(R)]
    ident = sb("ex_ident", [P, P])
    XT = [ctx.enter_context(nc.psum_tensor(f"XT{i}", [P, 512], F32)) for i in range(2)]
    UP = [ctx.enter_context(nc.psum_tensor(f"UP{i}", [P, 512], F32)) for i in range(2)]
    HT = [ctx.enter_context(nc.psum_tensor(f"HT{i}", [P, 512], F32)) for i in range(2)]
    DN = [ctx.enter_context(nc.psum_tensor(f"DN{i}", [P, 512], F32)) for i in range(2)]
    dma_w, id_ready, act_xT, act_silu, act_y, dve_h, dve_hT, pe_xT, pe_up, pe_hT, pe_dn = (
        sem("ex_" + n) for n in "w id xT silu yo h hT pxT pup phT pdn".split())
    sp_passed, pool_passed = sem("ex_sp_passed"), sem("ex_pool_passed")
    dma_t = [sem(f"ex_t{i}") for i in range(R)]
    dma_y = [sem(f"ex_y{i}") for i in range(R)]

    def tiles(eng, body):
        body(0, 0)
        with eng.Fori(1, NTILES // R - 1) as i:
            body(i * R, i)
        body(NTILES - R, NTILES // R - 1)

    def lag(t0, t, n):
        return not isinstance(t0, int) or t0 + t >= n

    def more(t0, r):
        return not isinstance(t0, int) or t0 + r + 1 < NTILES

    block = ctx.enter_context(nc.Block())

    @block.sync
    def _(sp):
        def wait(sem, value):
            sp.wait_ge(sem, value)
            if not isinstance(value, int):
                sp.sem_inc(sp_passed)

        def load(t, r):
            row = sp.value_load(tab[0:1, 0, bass.ds(t, 1)], min_val=0, max_val=NE * CAP)
            sp.dma_start(xt[r][:], xs[bass.ds(row, P), :]).then_inc(dma_t[r], 16)

        for r in range(R):
            load(r, r)
        with sp.Fori(1, NTILES // R) as i:
            for r in range(R):
                wait(dma_y[r], 16 * i)
                load(R * i + r, r)

    @block.gpsimd
    def _(pool):
        def wait(sem, value):
            pool.wait_ge(sem, value)
            if not isinstance(value, int):
                pool.sem_inc(pool_passed)

        pool.memset(ident[:], 0.0).then_inc(id_ready, 1)
        wait(id_ready, 1)
        pool.affine_select(out=ident[:], in_=ident[:], compare_op=ALU.not_equal, fill=1.0, base=0,
                           pattern=[[-1, P]], channel_multiplier=1).then_inc(id_ready, 1)

        def body(t0, i):
            for r in range(R):
                wait(act_y, t0 + r + 1)
                pool.indirect_dma_start(
                    out=yk[:, :], out_offset=bass.IndirectOffsetOnAxis(ap=xt[r][:, P + 1:P + 2].bitcast(U32), axis=0),
                    in_=y[r][:], in_offset=None, bounds_check=TOKENS * TOPK - 1, oob_is_err=False)\
                    .then_inc(dma_y[r], 16)

        tiles(pool, body)
        for r in range(R):
            wait(dma_y[r], 16 * (NTILES // R))

    @block.scalar
    def _(act):
        def evac_xT(t, r):
            act.wait_ge(pe_xT, t + 1)
            act.activation(xT[r % 2][:], XT[r % 2][:, 0:P], ACT.Copy).then_inc(act_xT, 1)

        def evac_y(t, r):
            act.wait_ge(pe_dn, t + 1)
            act.activation(y[r][:], DN[r % 2][:, 0:P], ACT.Copy).then_inc(act_y, 1)

        evac_xT(0, 0)

        def body(t0, i):
            for r in range(R):
                t = t0 + r
                if lag(t0, 0, R):
                    act.wait_ge(dma_y[r], 16 * i)
                if more(t0, r):
                    evac_xT(t + 1, (r + 1) % R)
                act.wait_ge(pe_up, t + 1)
                if lag(t0, r, 2):
                    act.wait_ge(dve_h, t - 1)
                act.activation(sg[r % 2][:], UP[r % 2][:, HID:2 * HID], ACT.Silu).then_inc(act_silu, 1)
                if lag(t0, r, 2):
                    evac_y(t - 2, (r - 2) % R)

        tiles(act, body)
        for t in (NTILES - 2, NTILES - 1):
            evac_y(t, t % R)

    @block.vector
    def _(dve):
        def turned(t, r):
            dve.wait_ge(pe_hT, t + 1)
            nc.vector.tensor_copy(hT[r % 2][:], HT[r % 2][:, 0:HID]).then_inc(dve_hT, 1)

        def body(t0, i):
            for r in range(R):
                t = t0 + r
                if lag(t0, r, 1):
                    turned(t - 1, r - 1)
                dve.wait_ge(act_silu, t + 1)
                nc.vector.scalar_tensor_tensor(h[r % 2][:], sg[r % 2][:], xt[r][:, P:P + 1], UP[r % 2][:, 0:HID],
                                               ALU.mult, ALU.mult).then_inc(dve_h, 1)

        tiles(dve, body)
        turned(NTILES - 1, NTILES - 1)

    @block.tensor
    def _(pe):
        def turn(t, r, before):
            pe.wait_ge(dma_t[r], 16 * before)
            nc.tensor.transpose(XT[r % 2][:, 0:P], xt[r][:, 0:P], ident[:]).then_inc(pe_xT, 1)

        def expert_of(t):
            return pe.value_load(tab[0:1, 1, bass.ds(t, 1)], min_val=0, max_val=NE - 1)

        def turn_h(t, r, some):
            pe.wait_ge(dve_h, t + 1)
            if some:
                pe.wait_ge(dve_hT, t - 1)
            for j in range(2):
                mm = nc.tensor.transpose(HT[r % 2][:, j * P:(j + 1) * P], h[r % 2][:, j * P:(j + 1) * P], ident[:])
            mm.then_inc(pe_hT, 1)

        def down(t, r, some, e):
            pe.wait_ge(dve_hT, t + 1)
            if some:
                pe.wait_ge(act_y, t - 1)
            for j in range(2):
                mm = nc.tensor.matmul(DN[r % 2][:, 0:P], hT[r % 2][:, j * P:(j + 1) * P],
                                      w_dn[:, bass.ds(e * 2 + j, 1), :].rearrange("p a d -> p (a d)"),
                                      start=j == 0, stop=j == 1)
            mm.then_inc(pe_dn, 1)

        pe.wait_ge(id_ready, 2)
        turn(0, 0, 1)

        def body(t0, i):
            experts_of = {0: expert_of(t0)}
            for r in range(R):
                t = t0 + r
                pe.wait_ge(act_xT, t + 1)
                if lag(t0, r, 2):
                    pe.wait_ge(dve_h, t - 1)
                nc.tensor.matmul(UP[r % 2][:], xT[r % 2][:],
                                 w_up[:, bass.ds(experts_of[r], 1), :].rearrange("p a d -> p (a d)"),
                                 start=True, stop=True).then_inc(pe_up, 1)
                if r < R - 1:
                    experts_of[r + 1] = expert_of(t + 1)
                if r < 2 and lag(t0, r, 2):
                    experts_of[r - 2] = expert_of(t - 2)
                if more(t0, r):
                    turn(t + 1, (r + 1) % R, i + 1 if r < R - 1 else i + 2)
                if lag(t0, r, 1):
                    turn_h(t - 1, (r - 1) % R, lag(t0, r, 3))
                if lag(t0, r, 2):
                    down(t - 2, (r - 2) % R, lag(t0, r, 4), experts_of[r - 2])

        tiles(pe, body)
        turn_h(NTILES - 1, NTILES - 1, True)
        for t in (NTILES - 2, NTILES - 1):
            down(t, t, True, expert_of(t))


def combine(nc, ctx, yk, x2b, out):
    yb = ctx.enter_context(nc.sbuf_tensor("yb", [P, NB, NT, TOPK, P], F32))
    ysum = ctx.enter_context(nc.sbuf_tensor("ysum", [P, NB, NT, P], F32))
    res = ctx.enter_context(nc.sbuf_tensor("res", [P, NB, NT, P], F32))
    loaded = [ctx.enter_context(nc.semaphore(f"cb_load{b}")) for b in range(NB)]
    added, done, stored = (ctx.enter_context(nc.semaphore("cb_" + n)) for n in ("added", "done", "stored"))
    yv = yk.rearrange("(b i p k) d -> b p i (k d)", b=NB, i=NT, k=TOPK)
    ov = out.rearrange("b (i p) d -> b p i d", p=P)
    block = ctx.enter_context(nc.Block())

    @block.sync
    def _(sp):
        for b in range(NB):
            sp.dma_start(yb[:, b].rearrange("p i k d -> p i (k d)"), yv[b]).then_inc(loaded[b], 16)

    @block.vector
    def _(dve):
        for b in range(NB):
            dve.wait_ge(loaded[b], 16)
            nc.vector.tensor_tensor(ysum[:, b], yb[:, b, :, 0, :], yb[:, b, :, 1, :], ALU.add).then_inc(added, 1)
            dve.wait_ge(added, b + 1)
            nc.vector.tensor_tensor(res[:, b], ysum[:, b], x2b[:, b * NT:(b + 1) * NT, :], ALU.add).then_inc(done, 1)

    @block.scalar
    def _(act):
        for b in range(NB):
            act.wait_ge(done, b + 1)
            act.dma_start(ov[b], res[:, b]).then_inc(stored, 16)
        act.wait_ge(stored, 16 * NB)


def build(nc, x, w_inT, b_in, w_outT, b_out, wqT, wscale, fbias, WqT, bq, WkT, bk, WvT, bv, nscale, wrT,
          w_up_in, w_dn_in, out):
    x1 = nc.dram_tensor("x1_dram", [NB, T, P], F32).ap()
    xs = nc.dram_tensor("expert_rows", [NE * CAP + P, ROW], F32).ap()
    yk = nc.dram_tensor("results", [TOKENS * TOPK, P], F32).ap()
    with ExitStack() as ctx:
        layer0(nc, ctx, x, w_inT, b_in, w_outT, b_out, wqT, wscale, fbias, x1)
    with ExitStack() as outer:
        def sb(name, shape, dt=F32):
            return outer.enter_context(nc.sbuf_tensor(name, shape, dt))

        x2b = sb("x2b", [P, NB * NT, P])
        tab = sb("tab", [1, 2, NTILES], I32)
        w_up = sb("w_up", [P, NE, 2 * HID])
        w_dn = sb("w_dn", [P, NE * 2, P])
        with ExitStack() as ctx:
            layer1(nc, ctx, x1, WqT, bq, WkT, bk, WvT, bv, nscale, wrT, xs, x2b, tab, w_up, w_dn, w_up_in, w_dn_in)
        with ExitStack() as ctx:
            experts(nc, ctx, xs, yk, w_up, w_dn, tab)
        with ExitStack() as ctx:
            combine(nc, ctx, yk, x2b, out)


def by_parity(w):
    import numpy as np

    qk = w[:2 * P].reshape((2, H // 2, 2, HD) + w.shape[1:])
    return np.concatenate([np.moveaxis(qk, 1, 3).reshape((2 * P,) + w.shape[1:]), w[2 * P:]])


def kernel(**inputs):
    import concourse.bacc as bacc
    import numpy as np
    from concourse.bass_utils import run_bass_kernel_spmd

    a = {k: np.asarray(v) for k, v in inputs.items()}
    arrays = {
        "x": a["L0_attn_x"], "w_inT": by_parity(a["L0_attn_w_in"]).T, "b_in": by_parity(a["L0_attn_b_in"]),
        "w_outT": a["L0_attn_w_out"].T, "b_out": a["L0_attn_b_out"],
        "wqT": np.ascontiguousarray(a["L0_ffn_weight_q"].T).view(np.int32), "wscale": a["L0_ffn_weight_scale"], "fbias": a["L0_ffn_bias"],
        "WqT": a["L1_attn_Wq"].T, "bq": a["L1_attn_bq"], "WkT": a["L1_attn_Wk"].T, "bk": a["L1_attn_bk"],
        "WvT": a["L1_attn_Wv"].T, "bv": a["L1_attn_bv"],
        "nscale": a["L1_ffn_norm_scale"], "wrT": a["L1_ffn_w_router"].T,
        "w_up": a["L1_ffn_w_up"].transpose(2, 0, 1),
        "w_dn": a["L1_ffn_w_down"].reshape(NE, P, HID // P, P).transpose(3, 0, 2, 1).reshape(P, NE * 2, P),
    }
    arrays = {"in_" + k: np.ascontiguousarray(v) for k, v in arrays.items()}
    nc = bacc.Bacc("TRN2", target_bir_lowering=False, num_devices=1)
    args = [nc.dram_tensor(k, v.shape, mybir.dt.from_np(v.dtype), kind="ExternalInput").ap()
            for k, v in arrays.items()]
    args.append(nc.dram_tensor("out", [NB, T, P], F32, kind="ExternalOutput").ap())
    build(nc, *args)
    r = run_bass_kernel_spmd(nc, [arrays], core_ids=[0])
    return r.results[0]["out"]
```

```python
from contextlib import ExitStack

import concourse.bass as bass
from concourse import mybir

F32 = mybir.dt.float32
BF16 = mybir.dt.bfloat16
I32 = mybir.dt.int32
U32 = mybir.dt.uint32
ALU = mybir.AluOpType
ACT = mybir.ActivationFunctionType
AX = mybir.AxisListType

P = 128
NB = 8
T = 512
NT = T // P
H = 16
HD = P // H
HG = 4
STEPS = H // HG
UNITS = 2 * NT
SLOTS = STEPS * UNITS
MAGIC = 12582912.0
NEG = -1e30
ONE_PAIR = 1.0 + 16256 / 2 ** 23
QTERMS = (0, 0, 0, 1, 1, 2)
KTERMS = (0, 1, 2, 0, 1, 0)
NTERM = len(QTERMS)
MROW = NTERM * HD
QRUNS = ((0, 3, 0), (3, 2, 1), (5, 1, 2))
KRUNS = ((0, 3), (3, 2), (5, 1))
NLOAD = 2 * (len(QRUNS) + len(KRUNS) + 1)


def window(t):
    lo, hi = max(0, t - 1), min(NT, t + 2)
    return lo * P, (hi - lo) * P


def piece_of(k):
    short, j = k % 2 == 0, k // 2
    return ((0, NT - 1) if short else (1, NT - 2))[j // HG], j % HG


def bank_of(step, n, banks):
    return banks[n % 2 if len(banks) == 2 else (2 * UNITS * step + n) % len(banks)]


def ahead(u, first):
    if first and u < UNITS // 2:
        return [(1 + u // 2, v) for v in ((4, 5), (6, 7), (0, 1), (2, 3))[u]]
    return [(2, u % UNITS)]


def k_slot(h):
    return h % 2 * (H // 2) + h // 2


def layer0(nc, ctx, x, w_inT, b_in, w_outT, b_out, wqT, wscale, fbias, x1_dram, buf, later):
    parts_dram = nc.dram_tensor("parts_dram", [NB + 1, 2, 3, P, T], BF16).ap()
    base_dram = nc.dram_tensor("base_dram", [NB + 1, P, NT, P], F32).ap()

    def sb(name, shape, dt=F32):
        return ctx.enter_context(nc.sbuf_tensor(name, shape, dt))

    def sem(name):
        return ctx.enter_context(nc.semaphore(name))

    w_in = sb("w_in", [P, 3 * P])
    w_out = sb("w_out", [P, P])
    wq8 = sb("wq8", [P, P // 4], mybir.dt.int32)
    wq = sb("wq", [P, P], BF16)
    b_col = sb("b_col", [P, 2])
    bq_col = sb("bq_col", [P, 1])
    bv_row = sb("bv_row", [P, P])
    ws_row = sb("ws_row", [P, P])
    bo_row = sb("bo_row", [P, P])
    fb_row = sb("fb_row", [P, P])
    bsum_row = sb("bsum_row", [P, P])
    ident = buf["ident"]
    ident16 = sb("ident16", [P, P], BF16)
    mask = sb("mask", [P, 2, P], BF16)
    mask_lo, mask_hi = mask[:, 0, :], mask[:, 1, :]
    mhalf = sb("mhalf", [P, NT])
    xb = sb("xb", [P, NT, P])
    stats = sb("stats", [P, NT, 6])
    mv = sb("mv", [P, NT, 2])
    veps = sb("veps", [P, NT])
    rstd = sb("rstd", [P, NT])
    xn = sb("xn", [P, NT, P])
    amax = sb("amax", [P, NT])
    xscale = sb("xscale", [P, NT])
    xrec = sb("xrec", [P, NT])
    t1 = sb("t1", [P, NT, P])
    t2 = sb("t2", [P, NT, P])
    xq = sb("xq", [P, NT, P], BF16)
    xqT = sb("xqT", [P, T], BF16)
    base0 = sb("base0", [P, NT, P])
    base1 = sb("base1", [P, NT, P])
    ffn = sb("ffn", [P, NT, P])
    base2 = sb("base2", [P, NT, P])
    base_r = sb("base_r", [P, NT, P])
    xnT = [sb(f"xnT{i}", [P, T]) for i in range(2)]
    qf, kf, rq, rk = (sb(n, [P, T]) for n in ("qf", "kf", "rq", "rk"))
    qp = sb("qp", [P, 3, T], BF16)
    kp = sb("kp", [P, 3, T], BF16)
    Qs = [sb(f"Qs{i}", [P, H // 2, T], BF16) for i in range(2)]
    Ks = [sb(f"Ks{i}", [P, H, T], BF16) for i in range(2)]
    Va = [sb(f"Va{i}", [P, NT, H, 32]) for i in range(2)]
    mneg = sb("mneg", [P, 2, NT * HG])
    mp = sb("mp", [P, 2, NT, 8], BF16)
    mT = sb("mT", [8, 2, T], BF16)
    Pb = sb("Pb", [P, NT, HG, 3 * P])
    cs = sb("cs", [P, HG, T])
    rec = sb("rec", [P, NT, H])
    ctxn = sb("ctxn", [P, NT, P])
    ctxT = sb("ctxT", [P, T])
    x1s, dma_x1 = buf["x1s"], buf["x1_stored"]

    A = [ctx.enter_context(nc.psum_tensor(f"A{i}", [P, 512], F32)) for i in range(2)]
    SB = [ctx.enter_context(nc.psum_tensor(f"SB{i}", [P, 2, 512], F32)) for i in range(2)]
    PV = ctx.enter_context(nc.psum_tensor("PV", [P, 512], F32))
    misc = ctx.enter_context(nc.psum_tensor("misc", [P, 512], F32))
    early = [A[0], A[1]] + [SB[i][:, j, :] for i in range(2) for j in range(2)]
    misc16 = misc[:, 0:256].bitcast(BF16)

    sp_passed, pool_passed, dve_passed = sem("sp_passed"), sem("pool_passed"), sem("dve_passed")
    names = """dma_w dma_x dma_base_r dma_base_w dma_pq dma_pk dma_stack dma_m dma_later pool_later
    pool_const pool_fill dve_fill pool_rs pool_ve pool_t1 pool_t2 pool_xq pool_b0 pool_b1 pool_b2 pool_rq pool_q3 pool_rk pool_k3
    pool_mask dve_const dve_bn dve_ag dve_xn dve_amax dve_xs dve_xr dve_ffn dve_max dve_mp dve_v dve_rec dve_ctx dve_x1
    act_bq act_xnT act_xqT act_qf act_q1 act_q2 act_kf act_k1 act_k2 act_exp act_pv act_mT act_ctxT
    pe_xnT pe_q pe_k pe_xqT pe_ffn pe_v pe_A pe_B pe_PV pe_mT pe_ctx pe_ctxT pe_out""".split()
    s = {n: sem(n) for n in names}
    (dma_w, dma_x, dma_base_r, dma_base_w, dma_pq, dma_pk, dma_stack, dma_m, dma_later, pool_later,
     pool_const, pool_fill, dve_fill, pool_rs, pool_ve, pool_t1, pool_t2, pool_xq, pool_b0, pool_b1, pool_b2,
     pool_rq, pool_q3, pool_rk, pool_k3,
     pool_mask, dve_const, dve_bn, dve_ag, dve_xn, dve_amax, dve_xs, dve_xr, dve_ffn, dve_max, dve_mp, dve_v,
     dve_rec, dve_ctx, dve_x1,
     act_bq, act_xnT, act_xqT, act_qf, act_q1, act_q2, act_kf, act_k1, act_k2, act_exp, act_pv, act_mT, act_ctxT,
     pe_xnT, pe_q, pe_k, pe_xqT, pe_ffn, pe_v, pe_A, pe_B, pe_PV, pe_mT, pe_ctx, pe_ctxT, pe_out) = (
        s[n] for n in names)

    NCONST = 8
    MASKS = (1, 3, 5, 6)
    NMASK = MASKS[-1]

    def batches(eng, body):
        body(0, 0, True, False)
        with eng.Fori(0, (NB - 2) // 2) as i:
            body(2 * i + 1, 1, False, False)
            body(2 * i + 2, 0, False, False)
        body(NB - 1, 1, False, True)

    block = ctx.enter_context(nc.Block())

    @block.sync
    def _(sp):
        def wait(sem, value):
            sp.wait_ge(sem, value)
            if not isinstance(value, int):
                sp.sem_inc(sp_passed)

        xv = x.rearrange("b (i p) d -> b p i d", p=P)
        x1v = x1_dram.rearrange("b (i p) d -> b p i d", p=P)

        def load_x(g):
            sp.dma_start(xb[:], xv[g]).then_inc(dma_x, 16)

        def store_parts(g, which):
            tile, done, ready = ((qp, dma_pq, pool_q3), (kp, dma_pk, pool_k3))[which]
            wait(ready, g + 1)
            sp.dma_start(parts_dram[g, which].rearrange("s e t -> e s t"), tile[:]).then_inc(done, 16)

        def load_q(g, pg):
            wait(dma_pq, 16 * (g + 1))
            for par in range(2):
                for n, count, part in QRUNS:
                    r0 = 64 * par + HD * n
                    src = parts_dram[g, 0, part].rearrange("(b d a) t -> b d (a t)", b=2, d=HD)[par]
                    sp.dma_start(Qs[pg][r0:r0 + count * HD, :, :].rearrange("r a t -> r (a t)"),
                                 src.unsqueeze(0).to_broadcast([count, HD, H // 2 * T])).then_inc(dma_stack, 16)
                r0 = 64 * par + MROW
                sp.dma_start(Qs[pg][r0:r0 + 2, :, :], Qs[pg][r0 + 2:r0 + 4, :, :]).then_inc(dma_stack, 16)

        def load_k(g, pg):
            wait(dma_pk, 16 * (g + 1))
            for par in range(2):
                for n, count in KRUNS:
                    r0 = 64 * par + HD * n
                    src = parts_dram[g, 1].rearrange("s (b d a) t -> b s d (a t)", b=2, d=HD)[par, 0:count]
                    heads = Ks[pg][r0:r0 + count * HD, par * H // 2:(par + 1) * H // 2, :]
                    sp.dma_start(heads.rearrange("r a t -> r (a t)"), src).then_inc(dma_stack, 16)

        def place_max(step, hg, pg):
            wait(act_mT, step + 1)
            if not (isinstance(step, int) and step == 0):
                wait(dma_m, 32 * step)
            for par in range(2):
                r0 = 64 * par + MROW
                sp.dma_start(Qs[pg][r0:r0 + 2, 2 * hg:2 * hg + 2, :],
                             mT[4 * par:4 * par + 4, hg % 2, :]).then_inc(dma_m, 16)

        sp.dma_start(xb[:], xv[0]).then_inc(dma_x, 16)
        sp.dma_start(w_in[:], w_inT).then_inc(dma_w, 16)
        sp.dma_start(w_out[:], w_outT).then_inc(dma_w, 16)
        sp.dma_start(wq8[:], wqT).then_inc(dma_w, 16)
        sp.dma_start(b_col[:], b_in[0:2 * P].rearrange("(c p) -> p c", p=P),
                     allow_slow_non_contiguous=True).then_inc(dma_w, 16)
        for row, src in ((bv_row, b_in[2 * P:3 * P]), (ws_row, wscale), (bo_row, b_out), (fb_row, fbias)):
            sp.dma_start(row[:], src.partition_broadcast(P)).then_inc(dma_w, 16)
        wait(pool_b0, 1)
        wait(dve_xn, NT)
        load_x(1)
        store_parts(0, 0)
        store_parts(0, 1)
        wait(pool_fill, 1)
        load_q(0, 0)
        wait(dve_fill, 2)
        load_k(0, 0)
        wait(pool_b2, 1)
        sp.dma_start(base_dram[0], base2[:]).then_inc(dma_base_w, 16)
        store_parts(1, 0)
        store_parts(1, 1)
        place_max(0, 0, 0)
        wait(pool_b2, 2)
        sp.dma_start(base_dram[1], base2[:]).then_inc(dma_base_w, 16)
        wait(pool_fill, 4)
        wait(dve_fill, 4)

        def body(b, p, first, last):
            o = 1 - p
            if not last:
                wait(pool_b0, b + 2)
                wait(dve_xn, NT * (b + 2))
                load_x((b + 2) % NB)
                if not first:
                    wait(pe_B, SLOTS * b)
                load_q(b + 1, o)
            place_max(STEPS * b + 1, 1, p)
            if not last:
                load_k(b + 1, o)
            if not first:
                wait(dma_base_w, 16 * b)
                sp.dma_start(base_r[:], base_dram[b - 1]).then_inc(dma_base_r, 16)
            place_max(STEPS * b + 2, 2, p)
            if not first:
                wait(dve_x1, b)
                sp.dma_start(x1v[b - 1], x1s[:]).then_inc(dma_x1, 16)
            place_max(STEPS * b + 3, 3, p)
            if not last:
                store_parts(b + 2, 0)
                place_max(STEPS * b + 4, 0, o)
                store_parts(b + 2, 1)
                wait(pool_b2, b + 3)
                sp.dma_start(base_dram[b + 2], base2[:]).then_inc(dma_base_w, 16)

        batches(sp, body)
        wait(dma_x1, 16 * 2)
        for i in range(2):
            sp.dma_start(buf["xb"][i][:], x1v[i]).then_inc(dma_later, 16)
        for dst, src in later:
            sp.dma_start(dst[:], src).then_inc(dma_later, 16)
        wait(dve_x1, NB - 1)
        sp.dma_start(base_r[:], base_dram[NB - 1]).then_inc(dma_base_r, 16)
        wait(dve_x1, NB)
        sp.dma_start(x1v[NB - 1], x1s[:]).then_inc(dma_x1, 16)
        wait(dma_base_w, 16 * (NB + 1))
        wait(dma_stack, 16 * NLOAD * NB)
        wait(dma_later, 16 * (2 + len(later)))

    @block.gpsimd
    def _(pool):
        def wait(sem, value):
            pool.wait_ge(sem, value)
            if not isinstance(value, int):
                pool.sem_inc(pool_passed)

        pool.memset(ident[:], 0.0).then_inc(pool_const, 1)
        pool.memset(ident16[:], 0.0).then_inc(pool_const, 1)
        pool.memset(mask_lo, 0.0).then_inc(pool_const, 1)
        pool.memset(mask_hi, 0.0).then_inc(pool_const, 1)
        pool.memset(mhalf[:], -0.5).then_inc(pool_const, 1)
        wait(pool_const, 5)
        for m in (ident, ident16):
            pool.affine_select(out=m[:], in_=m[:], compare_op=ALU.not_equal, fill=1.0, base=0,
                               pattern=[[-1, P]], channel_multiplier=1).then_inc(pool_const, 1)
        pool.affine_select(out=mask_lo, in_=mask_lo, compare_op=ALU.is_ge, fill=NEG, base=0,
                           pattern=[[1, P]], channel_multiplier=-1).then_inc(pool_const, 1)
        pool.affine_select(out=mask_hi, in_=mask_hi, compare_op=ALU.is_ge, fill=NEG, base=0,
                           pattern=[[-1, P]], channel_multiplier=1).then_inc(pool_const, 1)
        def fill_q(i):
            pool.memset(Qs[i][:].bitcast(F32), 0.0).then_inc(pool_fill, 1)

        def fill_k(i):
            pool.memset(Ks[i][:].bitcast(F32), ONE_PAIR).then_inc(pool_fill, 1)

        fill_q(0)

        def rstd_of(g):
            wait(dve_ag, NT * (g + 1))
            pool.tensor_scalar(veps[:], mv[:, :, 1], 1e-5, None, ALU.add).then_inc(pool_ve, 1)
            wait(pool_ve, g + 1)
            pool.tensor_tensor(rstd[:], veps[:], mhalf[:], ALU.pow).then_inc(pool_rs, 1)

        def base_x(g):
            wait(dve_xn, NT * (g + 1))
            if not (isinstance(g, int) and g == 0):
                wait(pool_b1, g)
            pool.tensor_tensor(base0[:], xb[:], xn[:], ALU.add).then_inc(pool_b0, 1)

        def quant_scale(g):
            wait(dve_xr, g + 1)
            for i in range(NT):
                pool.tensor_scalar(t1[:, i, :], xn[:, i, :], xrec[:, i:i + 1], MAGIC, ALU.mult, ALU.add)\
                    .then_inc(pool_t1, 1)

        def quant_clip(g):
            wait(pool_t1, NT * (g + 1))
            pool.tensor_scalar(t2[:], t1[:], MAGIC - 128, MAGIC + 127, ALU.max, ALU.min).then_inc(pool_t2, 1)

        def quant_int(g):
            wait(pool_t2, g + 1)
            if not (isinstance(g, int) and g == 0):
                wait(pe_xqT, g)
            pool.tensor_scalar(xq[:], t2[:], MAGIC, None, ALU.subtract).then_inc(pool_xq, 1)

        def base_bias(g):
            wait(pool_b0, g + 1)
            pool.tensor_tensor(base1[:], base0[:], bsum_row[:].unsqueeze(1).to_broadcast([P, NT, P]), ALU.add)\
                .then_inc(pool_b1, 1)

        def base_ffn(g):
            wait(pool_b1, g + 1)
            wait(dve_ffn, NT * (g + 1))
            if not (isinstance(g, int) and g == 0):
                wait(dma_base_w, 16 * g)
            pool.tensor_tensor(base2[:], base1[:], ffn[:], ALU.add).then_inc(pool_b2, 1)

        def rest(g, which):
            full, tile, out, done, first_part, last_part, n = (
                (qf, qp, rq, pool_rq, act_q1, pool_q3, act_qf), (kf, kp, rk, pool_rk, act_k1, pool_k3, act_kf))[which]
            wait(n, g + 1)
            wait(first_part, g + 1)
            pool.tensor_tensor(out[:], full[:], tile[:, 0, :], ALU.subtract).then_inc(done, 1)

        def third(g, which):
            tile, r, done, second, last = ((qp, rq, pool_q3, act_q2, dma_pq), (kp, rk, pool_k3, act_k2, dma_pk))[which]
            wait(second, g + 1)
            if not (isinstance(g, int) and g == 0):
                wait(last, 16 * g)
            pool.tensor_tensor(tile[:, 2, :], r[:], tile[:, 1, :], ALU.subtract).then_inc(done, 1)

        def masks(b, hg, kt):
            wait(act_exp, SLOTS * b + UNITS * hg + 2 * kt + 2)
            if kt > 0:
                blk = Pb[:, kt, :, 0:P]
                pool.affine_select(out=blk, in_=blk, compare_op=ALU.is_ge, fill=0.0, base=0,
                                   pattern=[[0, HG], [1, P]], channel_multiplier=-1).then_inc(pool_mask, 1)
            if kt < NT - 1:
                w = window(kt)[1]
                blk = Pb[:, kt, :, w - P:w]
                pool.affine_select(out=blk, in_=blk, compare_op=ALU.is_ge, fill=0.0, base=0,
                                   pattern=[[0, HG], [-1, P]], channel_multiplier=1).then_inc(pool_mask, 1)

        rstd_of(0)
        base_x(0)
        fill_k(0)
        quant_scale(0)
        rest(0, 0)
        third(0, 0)
        rest(0, 1)
        rstd_of(1)
        third(0, 1)
        fill_k(1)
        quant_clip(0)
        quant_int(0)
        rest(1, 0)
        rest(1, 1)
        third(1, 0)
        third(1, 1)
        wait(dve_const, 2)
        base_bias(0)
        base_x(1)
        base_ffn(0)
        quant_scale(1)
        quant_clip(1)
        quant_int(1)
        fill_q(1)
        base_bias(1)
        base_ffn(1)

        def body(b, p, first, last):
            g = b + 2
            for u in range(SLOTS):
                if not last:
                    if u == 8:
                        rstd_of(g)
                    if u == 14:
                        base_x(g)
                    if u == 16:
                        quant_scale(g)
                    if u == 18:
                        quant_clip(g)
                    if u == 20:
                        quant_int(g)
                    if u == 22:
                        rest(g, 0)
                    if u == 24:
                        rest(g, 1)
                        third(g, 0)
                    if u == 26:
                        third(g, 1)
                    if u == 28:
                        base_bias(g)
                    if u == 30:
                        base_ffn(g)
                if u % 2 == 1:
                    masks(b, u // UNITS, (u % UNITS) // 2)

        batches(pool, body)
        for dst, value in ((buf["tri"], 1.0), (buf["ones"], 1.0), (buf["mhalf"], -0.5)):
            pool.memset(dst[:], value).then_inc(pool_later, 1)
        wait(pool_later, 3)
        pool.affine_select(out=buf["tri"][:], in_=buf["tri"][:], compare_op=ALU.is_gt, fill=0.0, base=0,
                           pattern=[[1, P]], channel_multiplier=-1).then_inc(pool_later, 1)

    @block.scalar
    def _(act):
        act.wait_ge(dma_w, 16 * NCONST)
        SC = float(HD) ** -0.5
        act.activation(bq_col[:], b_col[:, 0:1], ACT.Copy, scale=SC).then_inc(act_bq, 1)

        def evac_xnT(g, pg):
            act.wait_ge(pe_xnT, g + 1)
            act.activation(xnT[pg][:], misc[:], ACT.Copy).then_inc(act_xnT, 1)

        def evac_q(g):
            act.wait_ge(pe_q, g + 1)
            if isinstance(g, int) and g == 0:
                act.wait_ge(act_bq, 1)
            else:
                act.wait_ge(pool_rq, g)
                act.wait_ge(dma_pq, 16 * g)
            act.activation(qf[:], misc[:], ACT.Identity, bias=bq_col[:, 0:1], scale=SC).then_inc(act_qf, 1)
            act.activation(qp[:, 0, :], misc[:], ACT.Identity, bias=bq_col[:, 0:1], scale=SC).then_inc(act_q1, 1)

        def evac_k(g):
            act.wait_ge(pe_k, g + 1)
            if not (isinstance(g, int) and g == 0):
                act.wait_ge(pool_rk, g)
                act.wait_ge(dma_pk, 16 * g)
            act.activation(kf[:], misc[:], ACT.Identity, bias=b_col[:, 1:2]).then_inc(act_kf, 1)
            act.activation(kp[:, 0, :], misc[:], ACT.Identity, bias=b_col[:, 1:2]).then_inc(act_k1, 1)

        def second(g, which):
            tile, r, need, done = ((qp, rq, pool_rq, act_q2), (kp, rk, pool_rk, act_k2))[which]
            act.wait_ge(need, g + 1)
            act.activation(tile[:, 1, :], r[:], ACT.Copy).then_inc(done, 1)

        def evac_xqT(g):
            act.wait_ge(pe_xqT, g + 1)
            act.activation(xqT[:], misc16, ACT.Copy).then_inc(act_xqT, 1)

        def evac_mT(step, hg):
            act.wait_ge(pe_mT, step + 1)
            if not (isinstance(step, int) and step < 2):
                act.wait_ge(dma_m, 32 * (step - 1))
            act.activation(mT[:, hg % 2, :], misc16[0:8, :], ACT.Copy).then_inc(act_mT, 1)

        def exp(b, u):
            hg, kt, half = u // UNITS, (u % UNITS) // 2, u % 2
            w = window(kt)[1]
            act.wait_ge(pe_B, SLOTS * b + u + 1)
            if not (isinstance(b, int) and b == 0 and hg == 0) and half == 0:
                act.wait_ge(pe_PV, NT * (STEPS * b + hg - 1) + kt + 1)
            act.activation(Pb[:, kt, 2 * half:2 * half + 2, 0:w], SB[u % 2][:, :, 0:w], ACT.Exp).then_inc(act_exp, 1)

        def evac_pv(step, hg):
            act.wait_ge(pe_PV, NT * (step + 1))
            if hg == 0 and not (isinstance(step, int) and step == 0):
                act.wait_ge(pe_ctx, step)
            act.activation(cs[:, hg, :], PV[:], ACT.Copy).then_inc(act_pv, 1)

        def evac_ctxT(g):
            act.wait_ge(pe_ctxT, g + 1)
            act.activation(ctxT[:], misc[:], ACT.Copy).then_inc(act_ctxT, 1)

        evac_xnT(0, 0)
        evac_q(0)
        second(0, 0)
        evac_k(0)
        second(0, 1)
        evac_xnT(1, 1)
        evac_q(1)
        evac_k(1)
        evac_xqT(0)
        second(1, 0)
        second(1, 1)
        evac_mT(0, 0)
        evac_xqT(1)

        def body(b, p, first, last):
            for u in range(SLOTS):
                exp(b, u)
                if u % UNITS == 4 and not (first and u == 4):
                    evac_pv(STEPS * b + u // UNITS - 1, (u // UNITS - 1) % STEPS)
                if (u % UNITS == 2 if u >= UNITS or not first else u == 3) and not (last and u // UNITS == STEPS - 1):
                    evac_mT(STEPS * b + u // UNITS + 1, (u // UNITS + 1) % STEPS)
                if u == 12 and not first:
                    evac_ctxT(b - 1)
                if not last:
                    if u == 16:
                        evac_xnT(b + 2, p)
                    if u == 20:
                        evac_q(b + 2)
                    if u == 22:
                        evac_k(b + 2)
                    if u == 23:
                        second(b + 2, 0)
                    if u == 24:
                        evac_xqT(b + 2)
                    if u == 25:
                        second(b + 2, 1)

        batches(act, body)
        evac_pv(STEPS * NB - 1, STEPS - 1)
        evac_ctxT(NB - 1)

    @block.vector
    def _(dve):
        def bn(g, tiles):
            dve.wait_ge(dma_x, 16 * (g + 1))
            for i in tiles:
                nc.vector.bn_stats(stats[:, i, :], xb[:, i, :]).then_inc(dve_bn, 1)

        def ag(g):
            for i in range(NT):
                dve.wait_ge(dve_bn, NT * g + i + 1)
                if not isinstance(g, int):
                    dve.sem_inc(dve_passed)
                nc.vector.bn_aggr(mv[:, i, :], stats[:, i, :]).then_inc(dve_ag, 1)

        def norm(g, tiles):
            if 0 in tiles:
                dve.wait_ge(pool_rs, g + 1)
                if not (isinstance(g, int) and g == 0):
                    dve.wait_ge(pe_xnT, g)
                    dve.wait_ge(pool_t1, NT * g)
            for i in tiles:
                nc.vector.tensor_scalar(xn[:, i, :], xb[:, i, :], mv[:, i, 0:1], rstd[:, i:i + 1],
                                        ALU.subtract, ALU.mult).then_inc(dve_xn, 1)

        def absmax(g):
            dve.wait_ge(dve_xn, NT * (g + 1))
            nc.vector.tensor_reduce(amax[:], xn[:], AX.X, ALU.max, apply_absolute_value=True).then_inc(dve_amax, 1)

        def scales(g):
            dve.wait_ge(dve_amax, g + 1)
            if not (isinstance(g, int) and g == 0):
                dve.wait_ge(dve_ffn, NT * g)
            nc.vector.tensor_scalar(xscale[:], amax[:], 1e-6, 1.0 / 127.0, ALU.max, ALU.mult).then_inc(dve_xs, 1)
            dve.wait_ge(dve_xs, g + 1)
            nc.vector.reciprocal(xrec[:], xscale[:]).then_inc(dve_xr, 1)

        def ffn_out(g, tiles):
            if 0 in tiles:
                dve.wait_ge(pe_ffn, g + 1)
                if not (isinstance(g, int) and g == 0):
                    dve.wait_ge(pool_b2, g)
            for i in tiles:
                nc.vector.scalar_tensor_tensor(ffn[:, i, :], misc[:, i * P:(i + 1) * P], xscale[:, i:i + 1],
                                               ws_row[:], ALU.mult, ALU.mult).then_inc(dve_ffn, 1)

        def evac_v(g, pg):
            dve.wait_ge(pe_v, g + 1)
            if isinstance(g, int) and g == 0:
                dve.wait_ge(dve_const, 6)
            elif not (isinstance(g, int) and g == 1):
                dve.wait_ge(pe_PV, STEPS * NT * (g - 1))
            nc.vector.tensor_tensor(Va[pg][:, :, :, 0:HD], misc[:].rearrange("p (i h d) -> p i h d", i=NT, d=HD),
                                    bv_row[:].rearrange("p (h d) -> p h d", d=HD).unsqueeze(1)
                                    .to_broadcast([P, NT, H, HD]), ALU.add).then_inc(dve_v, 1)

        def maxima(step, u, par, banks=A):
            for n in (2 * u, 2 * u + 1):
                qb, h = piece_of(n)
                dve.wait_ge(pe_A, 16 * step + n + 1)
                nc.vector.tensor_reduce(mneg[:, par, qb * HG + h:qb * HG + h + 1],
                                        bank_of(step, n, banks)[:, 0:window(qb)[1]], AX.X, ALU.max,
                                        negate=True).then_inc(dve_max, 1)

        def max_parts(step, par):
            dve.wait_ge(dve_max, 16 * (step + 1))
            if not (isinstance(step, int) and step < 2):
                dve.wait_ge(pe_mT, step - 1)
            src = mneg[:, par, :].rearrange("p (q a b) -> p q b a", a=2, b=2)
            dst = mp[:, par, :, :].rearrange("p q (b s a) -> p q b s a", b=2, s=2)
            nc.vector.tensor_copy(dst[:, :, :, 0, :], src).then_inc(dve_mp, 1)
            dve.wait_ge(dve_mp, 2 * step + 1)
            nc.vector.tensor_tensor(dst[:, :, :, 1, :], src, dst[:, :, :, 0, :], ALU.subtract).then_inc(dve_mp, 1)

        def context(g, qb, bank):
            v = bank[:].rearrange("p (h w) -> p h w", w=32)
            dve.wait_ge(pe_ctx, NT * g + qb + 1)
            nc.vector.reciprocal(rec[:, qb, :], v[:, :, HD:HD + 1].rearrange("p h w -> p (h w)")).then_inc(dve_rec, 1)
            dve.wait_ge(dve_rec, NT * g + qb + 1)
            nc.vector.tensor_tensor(ctxn[:, qb, :].rearrange("p (h d) -> p h d", d=HD), v[:, :, 0:HD],
                                    rec[:, qb, :].unsqueeze(2).to_broadcast([P, H, HD]), ALU.mult).then_inc(dve_ctx, 1)

        def out_x1(g):
            dve.wait_ge(pe_out, g + 1)
            dve.wait_ge(dma_base_r, 16 * (g + 1))
            nc.vector.tensor_tensor(x1s[:].rearrange("p i d -> p (i d)"), misc[:],
                                    base_r[:].rearrange("p i d -> p (i d)"), ALU.add).then_inc(dve_x1, 1)

        def clear_k(i):
            for par in range(2):
                heads = slice(H // 2, H) if par == 0 else slice(0, H // 2)
                nc.vector.memset(Ks[i][64 * par:64 * par + 64, heads, :].bitcast(F32), 0.0).then_inc(dve_fill, 1)

        bn(0, range(NT))
        ag(0)
        norm(0, range(NT))
        absmax(0)
        scales(0)
        dve.wait_ge(dma_w, 16 * NCONST)
        nc.vector.tensor_copy(wq[:], wq8[:].bitcast(mybir.dt.int8)).then_inc(dve_const, 1)
        nc.vector.tensor_tensor(bsum_row[:], bo_row[:], fb_row[:], ALU.add).then_inc(dve_const, 1)
        dve.wait_ge(pool_fill, 2)
        clear_k(0)
        bn(1, range(NT))
        ag(1)
        norm(1, range(NT))
        for va in Va:
            nc.vector.memset(va[:], 0.0).then_inc(dve_const, 1)
        dve.wait_ge(dve_const, 4)
        for va in Va:
            nc.vector.memset(va[:, :, :, HD:HD + 1], 1.0).then_inc(dve_const, 1)
        dve.wait_ge(pool_fill, 3)
        clear_k(1)
        ffn_out(0, range(NT))
        evac_v(0, 0)
        absmax(1)
        scales(1)
        for u in range(UNITS):
            maxima(0, u, 0, early)
        max_parts(0, 0)
        for u in range(UNITS // 2):
            maxima(1, u, 1, early)
        ffn_out(1, range(NT))

        def body(b, p, first, last):
            for u in range(SLOTS):
                hg = u // UNITS
                step = STEPS * b + hg
                if u == 2 and first:
                    max_parts(1, 1)
                for n, v in ahead(u, first):
                    if not (last and hg + n >= STEPS):
                        maxima(step + n, v, (hg + n) % 2)
                if u % UNITS == 1 and not (first and hg == 0) and not (last and hg == STEPS - 1):
                    max_parts(step + 1, (hg + 1) % 2)
                if u == 3 and not last:
                    evac_v(b + 1, 1 - p)
                if u in (5, 7, 9, 11) and not first:
                    context(b - 1, (u - 5) // 2, misc)
                if u == 15 and not first:
                    out_x1(b - 1)
                if not last:
                    if u in (4, 6):
                        bn(b + 2, range(u - 4, u - 2))
                    if u == 7:
                        ag(b + 2)
                    if 10 <= u < 14:
                        norm(b + 2, [u - 10])
                    if u == 14:
                        absmax(b + 2)
                    if u == 15:
                        scales(b + 2)
                    if u >= SLOTS - NT:
                        ffn_out(b + 2, [u - (SLOTS - NT)])
            if not first:
                dve.wait_ge(dma_x1, 16 * b)

        batches(dve, body)
        for qb in range(NT):
            context(NB - 1, qb, (misc, A[0], A[1], PV)[qb])
        out_x1(NB - 1)

    @block.tensor
    def _(pe):
        def turn_xn(g, before):
            pe.wait_ge(dve_xn, NT * (g + 1))
            pe.wait_ge(*before)
            for i in range(NT):
                mm = nc.tensor.transpose(misc[:, i * P:(i + 1) * P], xn[:, i, :], ident[:])
            mm.then_inc(pe_xnT, 1)

        def project(g, pg, which, done, before):
            pe.wait_ge(act_xnT, g + 1)
            pe.wait_ge(*before)
            nc.tensor.matmul(misc[:], w_in[:, which * P:(which + 1) * P], xnT[pg][:], start=True, stop=True)\
                .then_inc(done, 1)

        def values(g, pg, before):
            pe.wait_ge(act_xnT, g + 1)
            pe.wait_ge(*before)
            for i in range(NT):
                mm = nc.tensor.matmul(misc[:, i * P:(i + 1) * P], xnT[pg][:, i * P:(i + 1) * P],
                                      w_in[:, 2 * P:3 * P], start=True, stop=True)
            mm.then_inc(pe_v, 1)

        def turn_xq(g, before):
            pe.wait_ge(pool_xq, g + 1)
            pe.wait_ge(*before)
            for i in range(NT):
                mm = nc.tensor.transpose(misc16[:, i * P:(i + 1) * P], xq[:, i, :], ident16[:])
            mm.then_inc(pe_xqT, 1)

        def ffn_mm(g, before):
            pe.wait_ge(act_xqT, g + 1)
            pe.wait_ge(*before)
            for i in range(NT):
                mm = nc.tensor.matmul(misc[:, i * P:(i + 1) * P], xqT[:, i * P:(i + 1) * P], wq[:],
                                      start=True, stop=True)
            mm.then_inc(pe_ffn, 1)

        def piece(step, n, hgs, pg, banks=A):
            qb, h = piece_of(n)
            h += HG * hgs
            lo, w = window(qb)
            idx = 16 * step + n
            if not (isinstance(step, int) and idx < len(banks)):
                pe.wait_ge(dve_max, idx - len(banks) + 1)
            out = bank_of(step, n, banks)
            nc.tensor.matmul(out[:, 0:w], Qs[pg][:, h // 2, qb * P:(qb + 1) * P], Ks[pg][:, k_slot(h), lo:lo + w],
                             start=True, stop=True)
            if 0 < qb < NT - 1:
                ends, masks = out[:, 0:4 * P].rearrange("p (n w) -> p n w", w=2 * P)[:, :, 0:P], mask[:]
            else:
                ends, masks = (out[:, w - P:w], mask_hi) if qb == 0 else (out[:, 0:P], mask_lo)
            mm = nc.tensor.matmul(ends, ident16[:], masks, start=False, stop=True, skip_group_check=True)
            mm.then_inc(pe_A, 1)

        def turn_max(step, par, before):
            pe.wait_ge(dve_mp, 2 * (step + 1))
            pe.wait_ge(*before)
            for qb in range(NT):
                mm = nc.tensor.transpose(misc16[0:8, qb * P:(qb + 1) * P], mp[:, par, qb, :], ident16[:])
            mm.then_inc(pe_mT, 1)

        def scores(b, u, p):
            hg, kt, half = u // UNITS, (u % UNITS) // 2, u % 2
            lo, w = window(kt)
            if u % UNITS == 0:
                pe.wait_ge(dma_m, 32 * (STEPS * b + hg + 1))
            if not (isinstance(b, int) and b == 0 and u < 2):
                pe.wait_ge(act_exp, SLOTS * b + u - 1)
            else:
                pe.wait_ge(dve_max, 3 * UNITS - 2 + 2 * u)
            for j in range(2):
                h = HG * hg + 2 * half + j
                mm = nc.tensor.matmul(SB[u % 2][:, j, 0:w], Ks[p][:, k_slot(h), kt * P:(kt + 1) * P],
                                      Qs[p][:, h // 2, lo:lo + w], start=True, stop=True)
            mm.then_inc(pe_B, 1)

        def attend(step, hg, kt, p):
            pe.wait_ge(pool_mask, NMASK * step + MASKS[kt])
            if kt == 0 and not (isinstance(step, int) and step == 0):
                pe.wait_ge(act_pv, step)
            lo, w = window(kt)
            for c in range(HG):
                mm = nc.tensor.matmul(PV[32 * c:32 * c + 32, lo:lo + w], Va[p][:, kt, HG * hg + c, :],
                                      Pb[:, kt, c, 0:w], start=kt == 0, stop=True, skip_group_check=True,
                                      tile_position=(0, 32 * c))
            mm.then_inc(pe_PV, 1)

        def turn_ctx(g, qb, bank, before):
            pe.wait_ge(act_pv, STEPS * (g + 1))
            pe.wait_ge(*before)
            for hg in range(STEPS):
                mm = nc.tensor.transpose(bank[:, hg * P:(hg + 1) * P], cs[:, hg, qb * P:(qb + 1) * P], ident[:])
            mm.then_inc(pe_ctx, 1)

        def turn_ctxn(g, before):
            pe.wait_ge(dve_ctx, NT * (g + 1))
            pe.wait_ge(*before)
            for qb in range(NT):
                mm = nc.tensor.transpose(misc[:, qb * P:(qb + 1) * P], ctxn[:, qb, :], ident[:])
            mm.then_inc(pe_ctxT, 1)

        def out_mm(g):
            pe.wait_ge(act_ctxT, g + 1)
            for i in range(NT):
                mm = nc.tensor.matmul(misc[:, i * P:(i + 1) * P], ctxT[:, i * P:(i + 1) * P], w_out[:],
                                      start=True, stop=True)
            mm.then_inc(pe_out, 1)

        pe.wait_ge(pool_const, 9)
        pe.wait_ge(dma_w, 16 * NCONST)
        pe.wait_ge(dve_const, 1)
        turn_xn(0, (dve_xn, NT))
        project(0, 0, 0, pe_q, (act_xnT, 1))
        project(0, 0, 1, pe_k, (act_q1, 1))
        turn_xn(1, (act_k1, 1))
        project(1, 1, 0, pe_q, (act_xnT, 2))
        project(1, 1, 1, pe_k, (act_q1, 2))
        turn_xq(0, (act_k1, 2))
        pe.wait_ge(dve_const, 1)
        ffn_mm(0, (act_xqT, 1))
        values(0, 0, (dve_ffn, NT))
        pe.wait_ge(dma_stack, 16 * NLOAD)
        for n in range(2 * UNITS):
            piece(0, n, 0, 0, early)
        turn_max(0, 0, (dve_v, 1))
        for n in range(UNITS):
            piece(1, n, 1, 0, early)
            if n == 3:
                turn_xq(1, (act_mT, 1))
        ffn_mm(1, (act_xqT, 2))

        def body(b, p, first, last):
            o = 1 - p
            for u in range(SLOTS):
                hg, v = u // UNITS, u % UNITS
                step = STEPS * b + hg
                if not last and u == 2 * UNITS:
                    pe.wait_ge(dma_stack, 16 * NLOAD * (b + 2))
                scores(b, u, p)
                for k, unit in ahead(u, first):
                    if not (last and hg + k >= STEPS):
                        for n in (2 * unit, 2 * unit + 1):
                            piece(step + k, n, (hg + k) % STEPS, p if hg + k < STEPS else o)
                if u == 2 and not first:
                    turn_max(step + 1, 1, (dve_ffn, NT * ((b + 2) if not last else NB)))
                elif u == 3 and first:
                    turn_max(step + 1, 1, (dve_ffn, 2 * NT))
                elif u == 10:
                    turn_max(step + 1, 0, (dve_ctx, NT * (b - 1) + 3) if not first else (act_mT, step + 1))
                elif u == 18:
                    turn_max(step + 1, 1, (act_xnT, b + 3) if not last else (dve_x1, b))
                elif u == 26 and not last:
                    turn_max(step + 1, 0, (act_xqT, b + 3))
                if u == 3 and not last:
                    values(b + 1, o, (act_mT, STEPS * b + 2))
                if not first:
                    if u in (5, 7, 9, 11):
                        turn_ctx(b - 1, (u - 5) // 2, misc, {5: (dve_v, b + 2) if not last else (act_mT, STEPS * b + 2),
                                                       11: (act_mT, STEPS * b + 3)}
                                 .get(u, (dve_ctx, NT * (b - 1) + (u - 5) // 2)))
                    if u == 12:
                        turn_ctxn(b - 1, (act_mT, STEPS * b + 3))
                    if u == 14:
                        out_mm(b - 1)
                if not last:
                    if u == 16:
                        turn_xn(b + 2, (dve_x1, b) if not first else (act_mT, STEPS * b + 3))
                    if u == 20:
                        project(b + 2, p, 0, pe_q, (act_mT, STEPS * b + 4))
                    if u == 22:
                        project(b + 2, p, 1, pe_k, (act_q1, b + 3))
                    if u == 24:
                        turn_xq(b + 2, (act_k1, b + 3))
                    if u == 28:
                        ffn_mm(b + 2, (act_mT, STEPS * b + 5))
                if v in (1, 3) and not (first and hg == 0):
                    attend(step - 1, (hg - 1) % STEPS, NT - 2 + v // 2, p if hg else o)
                elif v in (5, 7):
                    attend(step, hg, (v - 5) // 2, p)

        batches(pe, body)
        attend(STEPS * NB - 1, STEPS - 1, NT - 2, 1)
        attend(STEPS * NB - 1, STEPS - 1, NT - 1, 1)
        for qb in range(NT):
            turn_ctx(NB - 1, qb, (misc, A[0], A[1], PV)[qb], (act_mT, STEPS * NB))
        turn_ctxn(NB - 1, (act_mT, STEPS * NB))
        out_mm(NB - 1)


NE = 8
HID = 256
TOPK = 2
TOKENS = NB * T
ROW = P + 2
CAP = TOKENS + P
NTILES = -(-(TOKENS * TOPK + NE * (P - 1)) // P // 8) * 8


def layer1_inputs(nc, ctx):

    def sb(name, shape, dt=F32):
        return ctx.enter_context(nc.sbuf_tensor("l1_" + name, shape, dt))

    buf = {n: sb(n, [P, P]) for n in ("wq", "wk", "wv", "bvr")}
    buf.update({n: sb(n, [P, 1]) for n in ("bqc", "bkc", "nsc")})
    buf["wr"] = sb("wr", [P, NE])
    buf["ident"] = sb("ident", [P, P])
    buf["tri"] = sb("tri", [P, P], BF16)
    buf["ones"] = sb("ones", [P, P], BF16)
    buf["mhalf"] = sb("mhalf", [P, NT])
    buf["xb"] = [sb(f"xb{i}", [P, NT, P]) for i in range(2)]
    buf["x1s"] = sb("x1s", [P, NT, P])
    buf["x1_stored"] = ctx.enter_context(nc.semaphore("x1_stored"))
    return buf


def layer1(nc, ctx, x1, buf, xs, x2b, tab, w_up, w_dn, w_up_in, w_dn_in):

    def sb(name, shape, dt=F32):
        return ctx.enter_context(nc.sbuf_tensor(name, shape, dt))

    def sem(name):
        return ctx.enter_context(nc.semaphore(name))

    wq, wk, wv, bvr, bqc, bkc, nsc, wr = (
        buf[n] for n in ("wq", "wk", "wv", "bvr", "bqc", "bkc", "nsc", "wr"))
    ident, tri, ones, mhalf, xb = (buf[n] for n in ("ident", "tri", "ones", "mhalf", "xb"))
    bqs = sb("l1_bqs", [P, 1])
    wrs = sb("l1_wrs", [P, NE])
    iota8i = sb("iota8i", [P, NE], I32)
    iota8 = sb("iota8", [P, NE])
    ebase = sb("ebase", [P, NE])
    dest_i = sb("dest_i", [P, NT * TOPK], I32)
    dest = sb("dest", [P, NT * TOPK])
    tile_i = sb("tile_i", [1, NTILES], I32)
    tile_f = sb("tile_f", [1, NTILES])
    nine_i = sb("nine_i", [1, NE + 1], I32)
    nine_f = sb("nine_f", [1, NE + 1])
    upto = sb("upto", [1, NE, NE])
    padrow = sb("padrow", [P, ROW])

    stats = sb("l1_stats", [P, NT, 6])
    mv = sb("l1_mv", [P, NT, 2])
    arg = sb("l1_arg", [P, 2, NT])
    inv = [sb(f"l1_inv{i}", [P, 2, NT]) for i in range(2)]
    mhalves = sb("l1_mhalves", [P, 2, NT])
    xn = [sb(f"l1_xn{i}", [P, NT, P]) for i in range(2)]
    junk = sb("l1_junk", [P, NT, P])
    ssq = sb("l1_ssq", [P, NT])
    base = [sb(f"l1_base{i}", [P, NT, P]) for i in range(2)]
    xnT = sb("l1_xnT", [P, T])
    qT = [sb(f"l1_qT{i}", [P, T]) for i in range(2)]
    kT = [sb(f"l1_kT{i}", [P, T]) for i in range(2)]
    v = [sb(f"l1_v{i}", [P, NT, P]) for i in range(2)]
    mneg = sb("l1_mneg", [P, NT])
    ssum = sb("l1_ssum", [P, NT])
    srec = sb("l1_srec", [P, NT])
    vs = sb("l1_vs", [P, NT, P])
    pr = sb("l1_pr", [P, NT, T])
    sc = sb("sc", [P, NT, NE])
    mx = sb("mx", [P, NT, NE])
    ix = sb("ix", [P, NT, NE], U32)
    ixf = sb("ixf", [P, NT, NE])
    oh = [sb(f"oh{i}", [P, NT, TOPK, NE]) for i in range(2)]
    dm = sb("dm", [P, NT])
    em = sb("em", [P, NT])
    den = sb("den", [P, NT])
    w1 = sb("w1", [P, NT])
    w2 = sb("w2", [P, NT])
    M = [sb(f"M{i}", [P, NT, NE], BF16) for i in range(2)]
    S = [sb(f"S{i}", [P, NE], BF16) for i in range(2)]
    msum = sb("msum", [P, NE])
    Re = sb("Re", [P, NT, NE])
    prod = sb("prod", [P, NT, TOPK, NE])
    posf = sb("posf", [P, NT, TOPK])
    pos = [sb(f"pos{i}", [P, NT, TOPK], U32) for i in range(2)]
    pay = [sb(f"pay{i}", [P, TOPK, NT, ROW]) for i in range(2)]
    cnt = sb("cnt", [P, NE])
    padp = sb("padp", [1, NE])
    padi = sb("padi", [1, NE], I32)
    nt_a = sb("nt_a", [P, NE])
    nt_f = sb("nt_f", [P, NE])
    cprod = sb("cprod", [1, NE, NE])
    cum = sb("cum", [1, NE])
    vals = sb("vals", [1, NE + 1])
    cx = sb("cx", [1, NE])
    le = sb("le", [1, NTILES, NE])
    et = sb("et", [1, NTILES])
    oh9 = sb("oh9", [1, NTILES, NE + 1])
    pv9 = sb("pv9", [1, NTILES, NE + 1])
    bt = sb("bt", [1, NTILES])
    bt2 = sb("bt2", [1, NTILES])

    Sb = [ctx.enter_context(nc.psum_tensor(f"l1_S{i}", [P, 512], F32)) for i in range(NT)]
    XV = ctx.enter_context(nc.psum_tensor("l1_XV", [P, 512], F32))
    QK = ctx.enter_context(nc.psum_tensor("l1_QK", [P, 512], F32))
    RT = ctx.enter_context(nc.psum_tensor("l1_RT", [P, 512], F32))
    OU = ctx.enter_context(nc.psum_tensor("l1_OU", [P, 512], F32))
    sp_passed, pool_passed, dve_passed = (sem("l1s_passed_" + n) for n in ("sp", "pool", "dve"))
    names = """x pad_hw const cdve ve rms_e inv base pay1 pay2 up sq xnT qT kT exp em bqs
        bn ag xn max v rec vs out ra rb fin
        p_xnT p_q p_k p_v p_r p_rank p_S p_out p_cnt sc_dma pad_dma""".split()
    s = {n: sem("l1s_" + n) for n in names}
    dma_x, dma_pad_hw, dma_up, dma_dn = s["x"], s["pad_hw"], sem("l1s_w_up"), sem("l1s_w_dn")
    pool_const, pool_ve, pool_me, pool_inv, pool_base = (s[n] for n in "const ve rms_e inv base".split())
    act_pay1, act_pay2, act_up, act_sq, act_xnT, act_q, act_k, act_exp, act_em, act_bqs = (
        s[n] for n in "pay1 pay2 up sq xnT qT kT exp em bqs".split())
    dve_const, dve_bn, dve_ag, dve_xn, dve_max, dve_v, dve_rec, dve_vs, dve_out, dve_ra, dve_rb, dve_fin = (
        s[n] for n in "cdve bn ag xn max v rec vs out ra rb fin".split())
    pe_xnT, pe_q, pe_k, pe_v, pe_r, pe_rank, pe_S, pe_out, pe_cnt = (
        s[n] for n in "p_xnT p_q p_k p_v p_r p_rank p_S p_out p_cnt".split())
    dma_rows, dma_pads = [sem(f"l1s_rows{i}") for i in range(2)], s["pad_dma"]

    NCP = 5
    RA = 13
    RB = 11
    ISC = float(P) ** -0.5

    def batches(eng, body):
        body(0, 0, False, 0)
        with eng.Fori(0, (NB - 2) // 2) as i:
            body(2 * i + 1, 1, False, i + 1)
            body(2 * i + 2, 0, False, i + 1)
        body(NB - 1, 1, True, 0)

    block = ctx.enter_context(nc.Block())

    @block.sync
    def _(sp):
        def wait(sem, value):
            sp.wait_ge(sem, value)
            if not isinstance(value, int):
                sp.sem_inc(sp_passed)

        xv = x1.rearrange("b (i p) d -> b p i d", p=P)
        wait(buf["x1_stored"], 16 * NB)
        sp.dma_start(w_up[:], w_up_in).then_inc(dma_up, 16)
        sp.dma_start(w_dn[:], w_dn_in).then_inc(dma_dn, 16)
        wait(dve_const, 2)
        sp.dma_start(xs[NE * CAP:NE * CAP + P, :], padrow[:]).then_inc(dma_pad_hw, 16)

        def body(g, p, last, prior):
            if not last:
                wait(pool_base, g + 1)
                if not (isinstance(g, int) and g == 0):
                    wait(dma_x, 16 * g)
                sp.dma_start(xb[p][:], xv[(g + 2) % NB]).then_inc(dma_x, 16)

        batches(sp, body)
        wait(dma_pad_hw, 16)
        wait(dma_dn, 16)
        wait(dve_fin, 3)
        for e in range(NE):
            row = sp.value_load(padi[0:1, e:e + 1], min_val=0, max_val=NE * CAP - P)
            sp.dma_start(xs[bass.ds(row, P), :], padrow[:]).then_inc(dma_pads, 16)
        wait(dma_pads, 16 * NE)

    @block.gpsimd
    def _(pool):
        def wait(sem, value):
            pool.wait_ge(sem, value)
            if not isinstance(value, int):
                pool.sem_inc(pool_passed)

        def root_0():
            wait(dve_ag, NT)
            pool.tensor_scalar(arg[:, 0, :], mv[:, :, 1], 1e-5, None, ALU.add).then_inc(pool_ve, 1)
            wait(pool_ve, 1)
            pool.tensor_tensor(inv[1][:, 0, :], arg[:, 0, :], mhalf[:], ALU.pow).then_inc(pool_inv, 1)

        def roots(g, pg):
            wait(act_sq, NT * (g + 1))
            pool.tensor_scalar(arg[:, 1, :], ssq[:], 1.0 / P, 1e-6, ALU.mult, ALU.add).then_inc(pool_me, 1)
            wait(dve_ag, NT * (g + 2))
            pool.tensor_scalar(arg[:, 0, :], mv[:, :, 1], 1e-5, None, ALU.add).then_inc(pool_ve, 1)
            wait(pool_me, g + 1)
            wait(pool_ve, g + 2)
            pool.tensor_tensor(inv[pg][:], arg[:], mhalves[:], ALU.pow).then_inc(pool_inv, 1)

        def base_of(g, pg):
            wait(dve_xn, NT * (g + 1))
            if not (isinstance(g, int) and g < 2):
                wait(dve_out, g - 1)
            pool.tensor_tensor(base[pg][:], xb[pg][:], xn[pg][:], ALU.add).then_inc(pool_base, 1)

        def scatter(g, p):
            wait(dve_rb, RB * (g + 1))
            wait(act_pay2, g + 1)
            for i in range(NT):
                for k in range(TOPK):
                    pool.indirect_dma_start(
                        out=xs[:, :], out_offset=bass.IndirectOffsetOnAxis(ap=pos[p][:, i, k:k + 1], axis=0),
                        in_=pay[p][:, k, i, :], in_offset=None).then_inc(dma_rows[p], 16)

        root_0()
        pool.memset(mhalves[:], -0.5).then_inc(pool_const, 1)
        pool.iota(iota8i[:], [[1, NE]], base=0, channel_multiplier=0).then_inc(pool_const, 1)
        pool.iota(dest_i[:], [[TOPK * P, NT], [1, TOPK]], base=0, channel_multiplier=TOPK).then_inc(pool_const, 1)
        pool.iota(tile_i[:], [[1, NTILES]], base=0, channel_multiplier=0).then_inc(pool_const, 1)
        pool.iota(nine_i[:], [[1, NE + 1]], base=0, channel_multiplier=0).then_inc(pool_const, 1)
        wait(pool_const, NCP)
        roots(0, 0)
        base_of(0, 0)

        def body(g, p, last, prior):
            if not last:
                roots(g + 1, 1 - p)
                base_of(g + 1, 1 - p)
            scatter(g, p)

        batches(pool, body)
        for rows in dma_rows:
            wait(rows, 16 * TOPK * NT * NB // 2)

    @block.scalar
    def _(act):
        act.activation(bqs[:], bqc[:], ACT.Copy, scale=ISC).then_inc(act_bqs, 1)

        def squares(g, pg):
            act.wait_ge(pool_inv, g + 1)
            for i in range(NT):
                act.wait_ge(dve_xn, NT * g + i + 1)
                act.activation(junk[:, i, :], xn[pg][:, i, :], ACT.Square, accum_out=ssq[:, i:i + 1]).then_inc(act_sq, 1)

        def evac_xnT(g):
            act.wait_ge(pe_xnT, g + 1)
            act.activation(xnT[:], XV[:], ACT.Copy).then_inc(act_xnT, 1)

        def evac_q(g, pg):
            act.wait_ge(pe_q, g + 1)
            act.activation(qT[pg][:], QK[:], ACT.Identity, bias=bqs[:, 0:1], scale=ISC).then_inc(act_q, 1)

        def evac_k(g, pg):
            act.wait_ge(pe_k, g + 1)
            act.activation(kT[pg][:], QK[:], ACT.Identity, bias=bkc[:, 0:1]).then_inc(act_k, 1)

        def gate_exp(g):
            act.wait_ge(dve_ra, RA * (g + 1))
            act.wait_ge(dve_rb, RB * g)
            act.activation(em[:], dm[:], ACT.Exp).then_inc(act_em, 1)

        def rows_of(g, pg, before):
            act.wait_ge(dma_rows[pg], 16 * TOPK * NT * before)
            act.wait_ge(pool_inv, g + 2)
            for i in range(NT):
                act.activation(pay[pg][:, 0, i, 0:P], xn[pg][:, i, :], ACT.Copy, scale=inv[pg][:, 1, i:i + 1])\
                    .then_inc(act_pay1, 1)
            act.wait_ge(act_pay1, NT * (g + 1))
            act.activation(pay[pg][:, 1, :, 0:P], pay[pg][:, 0, :, 0:P], ACT.Copy).then_inc(act_pay2, 1)

        def scale_up(g):
            act.wait_ge(dma_up, 16)
            w = w_up[:, bass.ds(g, 1), :].rearrange("p a d -> p (a d)")
            act.activation(w, w, ACT.Copy, scale=nsc[:, 0:1]).then_inc(act_up, 1)

        act.wait_ge(act_bqs, 1)
        squares(0, 0)
        evac_xnT(0)
        evac_q(0, 0)
        evac_k(0, 0)
        squares(1, 1)
        rows_of(0, 0, 0)

        def body(g, p, last, prior):
            if not last:
                evac_xnT(g + 1)
            for kt in range(NT):
                act.wait_ge(dve_max, NT * g + kt + 1)
                act.wait_ge(pe_out, g)
                act.wait_ge(dve_rec, NT * g)
                act.activation(pr[:, kt, :], Sb[kt][:], ACT.Exp, bias=mneg[:, kt:kt + 1],
                               accum_out=ssum[:, kt:kt + 1]).then_inc(act_exp, 1)
            if not last:
                evac_q(g + 1, 1 - p)
            gate_exp(g)
            if not last:
                evac_k(g + 1, 1 - p)
                squares(g + 2, p)
                rows_of(g + 1, 1 - p, prior)
            scale_up(g)

        batches(act, body)

    @block.vector
    def _(dve):
        def stat(g, pg):
            if not (isinstance(g, int) and g < 2):
                dve.wait_ge(dma_x, 16 * (g - 1))
            if not (isinstance(g, int) and g == 0):
                dve.wait_ge(pool_ve, g)
            for i in range(NT):
                nc.vector.bn_stats(stats[:, i, :], xb[pg][:, i, :]).then_inc(dve_bn, 1)
            for i in range(NT):
                dve.wait_ge(dve_bn, NT * g + i + 1)
                if not isinstance(g, int):
                    dve.sem_inc(dve_passed)
                nc.vector.bn_aggr(mv[:, i, :], stats[:, i, :]).then_inc(dve_ag, 1)

        def norm_of(g, pg):
            dve.wait_ge(pool_inv, g + 1)
            if not (isinstance(g, int) and g < 2):
                dve.wait_ge(act_pay2, g - 1)
            for i in range(NT):
                nc.vector.tensor_scalar(xn[pg][:, i, :], xb[pg][:, i, :], mv[:, i, 0:1], inv[1 - pg][:, 0, i:i + 1],
                                        ALU.subtract, ALU.mult).then_inc(dve_xn, 1)

        def evac_v(g, pg):
            dve.wait_ge(pe_v, g + 1)
            nc.vector.tensor_tensor(v[pg][:], XV[:].rearrange("p (i d) -> p i d", i=NT),
                                    bvr[:].unsqueeze(1).to_broadcast([P, NT, P]), ALU.add).then_inc(dve_v, 1)

        def route_a(g, pg):
            done = [RA * g]

            def step(ins, wait=True):
                ins.then_inc(dve_ra, 1)
                done[0] = done[0] + 1
                if wait:
                    dve.wait_ge(dve_ra, done[0])
                    if not isinstance(g, int):
                        dve.sem_inc(dve_passed)

            dve.wait_ge(pe_r, g + 1)
            dve.wait_ge(act_em, g)
            step(nc.vector.tensor_tensor(sc[:], RT[:, 0:NT * NE].rearrange("p (i e) -> p i e", e=NE),
                                         inv[pg][:, 1, :].unsqueeze(2).to_broadcast([P, NT, NE]), ALU.mult))
            for i in range(NT):
                step(nc.vector.max(mx[:, i, :], sc[:, i, :]), i == NT - 1)
            for i in range(NT):
                step(nc.vector.max_index(ix[:, i, :], mx[:, i, :], sc[:, i, :]), i == NT - 1)
            step(nc.vector.tensor_copy(ixf[:], ix[:]))
            step(nc.vector.tensor_tensor(oh[pg][:], iota8[:].unsqueeze(1).unsqueeze(1).to_broadcast([P, NT, TOPK, NE]),
                                         ixf[:, :, 0:TOPK].unsqueeze(3).to_broadcast([P, NT, TOPK, NE]), ALU.is_equal))
            step(nc.vector.tensor_tensor(M[pg][:], oh[pg][:, :, 0, :], oh[pg][:, :, 1, :], ALU.add), False)
            step(nc.vector.tensor_tensor(dm[:], mx[:, :, 1], mx[:, :, 0], ALU.subtract))

        def ranks(g, last):
            dve.wait_ge(pe_rank, g + 1)
            if last:
                dve.wait_ge(pe_cnt, 1)
            if not (isinstance(g, int) and g == 0):
                dve.wait_ge(dve_rb, RB * g)
            nc.vector.tensor_tensor(Re[:], RT[:, 64:64 + NT * NE].rearrange("p (i e) -> p i e", e=NE),
                                    ebase[:].unsqueeze(1).to_broadcast([P, NT, NE]), ALU.add).then_inc(dve_rb, 1)

        def route_b(g, p):
            done = [RB * g]

            def step(ins, wait=True):
                ins.then_inc(dve_rb, 1)
                done[0] = done[0] + 1
                if wait:
                    dve.wait_ge(dve_rb, done[0])

            dve.wait_ge(act_pay2, g + 1)
            done[0] = done[0] + 1
            dve.wait_ge(dve_rb, done[0])
            step(nc.vector.tensor_tensor(prod[:], oh[p][:], Re[:].unsqueeze(2).to_broadcast([P, NT, TOPK, NE]),
                                         ALU.mult))
            step(nc.vector.tensor_reduce(posf[:], prod[:], AX.X, ALU.add))
            step(nc.vector.tensor_copy(pos[p][:], posf[:]), False)
            step(nc.vector.tensor_reduce(msum[:], M[p][:].rearrange("p i e -> p e i"), AX.X, ALU.add))
            step(nc.vector.tensor_tensor(S[1 - p][:], S[p][:], msum[:], ALU.add), False)
            step(nc.vector.tensor_scalar(dest[:], dest[:], float(TOPK * T), None, ALU.add))
            dve.wait_ge(act_em, g + 1)
            step(nc.vector.tensor_scalar(den[:], em[:], 1.0, None, ALU.add))
            step(nc.vector.tensor_copy(
                pay[p][:, :, :, P + 1].bitcast(I32).rearrange("p k i -> p i k"),
                dest[:].rearrange("p (i k) -> p i k", k=TOPK)))
            step(nc.vector.reciprocal(pay[p][:, 0, :, P], den[:]))
            step(nc.vector.tensor_tensor(pay[p][:, 1, :, P], em[:], pay[p][:, 0, :, P], ALU.mult), False)

        stat(0, 0)
        nc.vector.memset(padrow[:], 0.0).then_inc(dve_const, 1)
        dve.wait_ge(dve_const, 1)
        nc.vector.memset(padrow[:, P + 1:P + 2].bitcast(I32), TOKENS * TOPK).then_inc(dve_const, 1)
        nc.vector.tensor_scalar(wrs[:], wr[:], nsc[:, 0:1], None, ALU.mult).then_inc(dve_const, 1)
        norm_of(0, 0)
        stat(1, 1)
        dve.wait_ge(pool_const, NCP)
        nc.vector.tensor_copy(iota8[:], iota8i[:]).then_inc(dve_const, 1)
        nc.vector.tensor_scalar(ebase[:], iota8i[:], float(CAP), None, ALU.mult).then_inc(dve_const, 1)
        nc.vector.tensor_scalar(dest[:], dest_i[:], -float(TOPK * T), None, ALU.add).then_inc(dve_const, 1)
        nc.vector.tensor_copy(tile_f[:], tile_i[:]).then_inc(dve_const, 1)
        nc.vector.tensor_copy(nine_f[:], nine_i[:]).then_inc(dve_const, 1)
        nc.vector.memset(S[0][:], 0.0).then_inc(dve_const, 1)
        dve.wait_ge(dve_const, 9)
        nc.vector.tensor_tensor(upto[:], iota8[0:1, :].unsqueeze(1).to_broadcast([1, NE, NE]),
                                iota8[0:1, :].unsqueeze(2).to_broadcast([1, NE, NE]), ALU.is_le).then_inc(dve_const, 1)
        evac_v(0, 0)
        norm_of(1, 1)
        dve.wait_ge(dve_const, 10)
        route_a(0, 0)

        fin = [0]

        def step(ins, wait=True):
            ins.then_inc(dve_fin, 1)
            fin[0] += 1
            if wait:
                dve.wait_ge(dve_fin, fin[0])

        def rows_to_pad():
            dve.wait_ge(pe_cnt, 1)
            step(nc.vector.tensor_copy(cnt[:], RT[:, 128:128 + NE]))
            step(nc.vector.tensor_tensor(padp[:], cnt[0:1, :], ebase[0:1, :], ALU.add))
            step(nc.vector.tensor_copy(padi[:], padp[:]), False)

        def body(g, p, last, prior):
            o = 1 - p
            if last:
                ranks(g, last)
                rows_to_pad()
            for kt in range(NT):
                dve.wait_ge(pe_S, NT * g + kt + 1)
                dve.wait_ge(act_exp, NT * g)
                nc.vector.tensor_reduce(mneg[:, kt:kt + 1], Sb[kt][:], AX.X, ALU.max, negate=True)\
                    .then_inc(dve_max, 1)
            if not last:
                ranks(g, last)
                stat(g + 2, p)
            for kt in range(NT):
                dve.wait_ge(act_exp, NT * g + kt + 1)
                dve.wait_ge(pe_out, g)
                nc.vector.reciprocal(srec[:, kt:kt + 1], ssum[:, kt:kt + 1]).then_inc(dve_rec, 1)
                dve.wait_ge(dve_rec, NT * g + kt + 1)
                dve.wait_ge(dve_v, g + 1)
                nc.vector.tensor_scalar(vs[:, kt, :], v[p][:, kt, :], srec[:, kt:kt + 1], ISC, ALU.mult, ALU.mult)\
                    .then_inc(dve_vs, 1)
            route_b(g, p)
            if not last:
                evac_v(g + 1, o)
                norm_of(g + 2, p)
                route_a(g + 1, o)
            dve.wait_ge(pe_out, g + 1)
            dve.wait_ge(pool_base, g + 1)
            nc.vector.tensor_tensor(x2b[:, bass.ds(g * NT, NT), :], OU[:].rearrange("p (i d) -> p i d", i=NT),
                                    base[p][:], ALU.add).then_inc(dve_out, 1)

        batches(dve, body)
        step(nc.vector.tensor_scalar(nt_a[:], cnt[:], 1.0 / P, (P - 1) / P - (P - 1) / (2 * P), ALU.mult, ALU.add))
        step(nc.vector.tensor_scalar(nt_f[:], nt_a[:], MAGIC, MAGIC, ALU.add, ALU.subtract))
        step(nc.vector.tensor_tensor(cprod[:], upto[:], nt_f[0:1, :].unsqueeze(1).to_broadcast([1, NE, NE]), ALU.mult))
        step(nc.vector.tensor_reduce(cum[:], cprod[:], AX.X, ALU.add))
        step(nc.vector.tensor_tensor(cx[:], cum[:], nt_f[0:1, :], ALU.subtract))
        step(nc.vector.scalar_tensor_tensor(vals[:, 0:NE], cx[:], -float(P), ebase[0:1, :], ALU.mult, ALU.add), False)
        step(nc.vector.memset(vals[:, NE:NE + 1], float(NE * CAP)))
        step(nc.vector.tensor_tensor(le[:], cum[:].unsqueeze(1).to_broadcast([1, NTILES, NE]),
                                     tile_f[:].unsqueeze(2).to_broadcast([1, NTILES, NE]), ALU.is_le))
        step(nc.vector.tensor_reduce(et[:], le[:], AX.X, ALU.add))
        step(nc.vector.tensor_tensor(oh9[:], nine_f[:].unsqueeze(1).to_broadcast([1, NTILES, NE + 1]),
                                     et[:].unsqueeze(2).to_broadcast([1, NTILES, NE + 1]), ALU.is_equal))
        step(nc.vector.tensor_tensor(pv9[:], oh9[:], vals[:].unsqueeze(1).to_broadcast([1, NTILES, NE + 1]), ALU.mult))
        step(nc.vector.tensor_reduce(bt[:], pv9[:], AX.X, ALU.add))
        step(nc.vector.scalar_tensor_tensor(bt2[:], tile_f[:], float(P), bt[:], ALU.mult, ALU.add))
        step(nc.vector.tensor_scalar(tab[:, 0, :], bt2[:], float(NE * CAP), None, ALU.min), False)
        step(nc.vector.tensor_scalar(tab[:, 1, :], et[:], float(NE - 1), None, ALU.min))

    @block.tensor
    def _(pe):

        def turn(g, pg):
            pe.wait_ge(dve_xn, NT * (g + 1))
            pe.wait_ge(dve_v, g)
            for i in range(NT):
                mm = nc.tensor.transpose(XV[:, i * P:(i + 1) * P], xn[pg][:, i, :], ident[:])
            mm.then_inc(pe_xnT, 1)

        def rank(g, p, last):
            pe.wait_ge(dve_ra, RA * (g + 1))
            if not (isinstance(g, int) and g == 0):
                pe.wait_ge(dve_rb, RB * g)
            for i in range(NT):
                out = RT[:, 64 + i * NE:64 + (i + 1) * NE]
                nc.tensor.matmul(out, tri[:], M[p][:, i, :], start=True, stop=False)
                for j in range(i):
                    nc.tensor.matmul(out, ones[:], M[p][:, j, :], start=False, stop=False)
                mm = nc.tensor.matmul(out, ones[:], S[p][:], start=False, stop=True)
            mm.then_inc(pe_rank, 1)
            if last:
                out = RT[:, 128:128 + NE]
                for j in range(NT):
                    nc.tensor.matmul(out, ones[:], M[p][:, j, :], start=j == 0, stop=False)
                nc.tensor.matmul(out, ones[:], S[p][:], start=False, stop=True).then_inc(pe_cnt, 1)

        def q(g):
            pe.wait_ge(act_xnT, g + 1)
            pe.wait_ge(act_k, g)
            nc.tensor.matmul(QK[:], wq[:], xnT[:], start=True, stop=True).then_inc(pe_q, 1)

        def k(g):
            pe.wait_ge(act_q, g + 1)
            nc.tensor.matmul(QK[:], wk[:], xnT[:], start=True, stop=True).then_inc(pe_k, 1)

        def values(g):
            for i in range(NT):
                mm = nc.tensor.matmul(XV[:, i * P:(i + 1) * P], xnT[:, i * P:(i + 1) * P], wv[:],
                                      start=True, stop=True)
            mm.then_inc(pe_v, 1)

        def router(g):
            if not (isinstance(g, int) and g == 0):
                pe.wait_ge(dve_rb, RB * (g - 1) + 1)
            for i in range(NT):
                mm = nc.tensor.matmul(RT[:, i * NE:(i + 1) * NE], xnT[:, i * P:(i + 1) * P], wrs[:],
                                      start=True, stop=True)
            mm.then_inc(pe_r, 1)

        turn(0, 0)
        q(0)
        values(0)
        k(0)
        pe.wait_ge(dve_const, 3)
        router(0)

        def body(g, p, last, prior):
            o = 1 - p
            if last:
                rank(g, p, last)
            else:
                turn(g + 1, o)
            pe.wait_ge(act_k, g + 1)
            pe.wait_ge(act_exp, NT * g)
            for kt in range(NT):
                nc.tensor.matmul(Sb[kt][:], kT[p][:, kt * P:(kt + 1) * P], qT[p][:], start=True, stop=True)\
                    .then_inc(pe_S, 1)
            if not last:
                rank(g, p, last)
            if not last:
                q(g + 1)
                values(g + 1)
                router(g + 1)
                k(g + 1)
            pe.wait_ge(dve_vs, NT * (g + 1))
            pe.wait_ge(dve_out, g)
            for i in range(NT):
                for kt in range(NT):
                    mm = nc.tensor.matmul(OU[:, i * P:(i + 1) * P], pr[:, kt, i * P:(i + 1) * P], vs[:, kt, :],
                                          start=kt == 0, stop=kt == NT - 1)
            mm.then_inc(pe_out, 1)

        batches(pe, body)


def experts(nc, ctx, xs, yk, w_up, w_dn, tab, ident):

    def sb(name, shape, dt=F32):
        return ctx.enter_context(nc.sbuf_tensor(name, shape, dt))

    def sem(name):
        return ctx.enter_context(nc.semaphore(name))

    R = 8
    xt = [sb(f"xt{i}", [P, ROW]) for i in range(R)]
    xT = [sb(f"xT{i}", [P, P]) for i in range(2)]
    sg = [sb(f"sg{i}", [P, HID]) for i in range(2)]
    h = [sb(f"h{i}", [P, HID]) for i in range(2)]
    hT = [sb(f"hT{i}", [P, HID]) for i in range(2)]
    y = [sb(f"y{i}", [P, P]) for i in range(R)]
    XT = [ctx.enter_context(nc.psum_tensor(f"XT{i}", [P, 512], F32)) for i in range(2)]
    UP = [ctx.enter_context(nc.psum_tensor(f"UP{i}", [P, 512], F32)) for i in range(2)]
    HT = [ctx.enter_context(nc.psum_tensor(f"HT{i}", [P, 512], F32)) for i in range(2)]
    DN = [ctx.enter_context(nc.psum_tensor(f"DN{i}", [P, 512], F32)) for i in range(2)]
    act_table, act_xT, act_silu, act_y, dve_h, dve_hT, pe_xT, pe_up, pe_hT, pe_dn = (
        sem("ex_" + n) for n in "table xT silu yo h hT pxT pup phT pdn".split())
    sp_passed, pool_passed = sem("ex_sp_passed"), sem("ex_pool_passed")
    dma_t = [sem(f"ex_t{i}") for i in range(R)]
    dma_y = [sem(f"ex_y{i}") for i in range(R)]

    def tiles(eng, body):
        body(0, 0)
        with eng.Fori(1, NTILES // R - 1) as i:
            body(i * R, i)
        body(NTILES - R, NTILES // R - 1)

    def lag(t0, t, n):
        return not isinstance(t0, int) or t0 + t >= n

    def more(t0, r):
        return not isinstance(t0, int) or t0 + r + 1 < NTILES

    block = ctx.enter_context(nc.Block())

    @block.sync
    def _(sp):
        def wait(sem, value):
            sp.wait_ge(sem, value)
            if not isinstance(value, int):
                sp.sem_inc(sp_passed)

        def load(t, r):
            row = sp.value_load(tab[0:1, 0, bass.ds(t, 1)], min_val=0, max_val=NE * CAP)
            sp.dma_start(xt[r][:], xs[bass.ds(row, P), :]).then_inc(dma_t[r], 16)

        for r in range(R):
            load(r, r)
        with sp.Fori(1, NTILES // R) as i:
            for r in range(R):
                wait(dma_y[r], 16 * i)
                load(R * i + r, r)

    @block.gpsimd
    def _(pool):
        def wait(sem, value):
            pool.wait_ge(sem, value)
            if not isinstance(value, int):
                pool.sem_inc(pool_passed)

        def body(t0, i):
            for r in range(R):
                wait(act_y, t0 + r + 1)
                pool.indirect_dma_start(
                    out=yk[:, :], out_offset=bass.IndirectOffsetOnAxis(ap=xt[r][:, P + 1:P + 2].bitcast(U32), axis=0),
                    in_=y[r][:], in_offset=None, bounds_check=TOKENS * TOPK - 1, oob_is_err=False)\
                    .then_inc(dma_y[r], 16)

        tiles(pool, body)
        for r in range(R):
            wait(dma_y[r], 16 * (NTILES // R))

    @block.scalar
    def _(act):
        def evac_xT(t, r):
            act.wait_ge(pe_xT, t + 1)
            act.activation(xT[r % 2][:], XT[r % 2][:, 0:P], ACT.Copy).then_inc(act_xT, 1)

        def evac_y(t, r):
            act.wait_ge(pe_dn, t + 1)
            act.activation(y[r][:], DN[r % 2][:, 0:P], ACT.Copy).then_inc(act_y, 1)

        act.activation(sg[0][:, 0:1], ident[:, 0:1], ACT.Silu).then_inc(act_table, 1)
        act.wait_ge(act_table, 1)
        evac_xT(0, 0)

        def body(t0, i):
            for r in range(R):
                t = t0 + r
                if lag(t0, 0, R):
                    act.wait_ge(dma_y[r], 16 * i)
                if more(t0, r):
                    evac_xT(t + 1, (r + 1) % R)
                act.wait_ge(pe_up, t + 1)
                if lag(t0, r, 2):
                    act.wait_ge(dve_h, t - 1)
                act.activation(sg[r % 2][:], UP[r % 2][:, HID:2 * HID], ACT.Silu).then_inc(act_silu, 1)
                if lag(t0, r, 2):
                    evac_y(t - 2, (r - 2) % R)

        tiles(act, body)
        for t in (NTILES - 2, NTILES - 1):
            evac_y(t, t % R)

    @block.vector
    def _(dve):
        def turned(t, r):
            dve.wait_ge(pe_hT, t + 1)
            nc.vector.tensor_copy(hT[r % 2][:], HT[r % 2][:, 0:HID]).then_inc(dve_hT, 1)

        def body(t0, i):
            for r in range(R):
                t = t0 + r
                if lag(t0, r, 1):
                    turned(t - 1, r - 1)
                dve.wait_ge(act_silu, t + 1)
                nc.vector.scalar_tensor_tensor(h[r % 2][:], sg[r % 2][:], xt[r][:, P:P + 1], UP[r % 2][:, 0:HID],
                                               ALU.mult, ALU.mult).then_inc(dve_h, 1)

        tiles(dve, body)
        turned(NTILES - 1, NTILES - 1)

    @block.tensor
    def _(pe):
        def turn(t, r, before):
            pe.wait_ge(dma_t[r], 16 * before)
            nc.tensor.transpose(XT[r % 2][:, 0:P], xt[r][:, 0:P], ident[:]).then_inc(pe_xT, 1)

        def expert_of(t):
            return pe.value_load(tab[0:1, 1, bass.ds(t, 1)], min_val=0, max_val=NE - 1)

        def turn_h(t, r, some):
            pe.wait_ge(dve_h, t + 1)
            if some:
                pe.wait_ge(dve_hT, t - 1)
            for j in range(2):
                mm = nc.tensor.transpose(HT[r % 2][:, j * P:(j + 1) * P], h[r % 2][:, j * P:(j + 1) * P], ident[:])
            mm.then_inc(pe_hT, 1)

        def down(t, r, some, e):
            pe.wait_ge(dve_hT, t + 1)
            if some:
                pe.wait_ge(act_y, t - 1)
            for j in range(2):
                mm = nc.tensor.matmul(DN[r % 2][:, 0:P], hT[r % 2][:, j * P:(j + 1) * P],
                                      w_dn[:, bass.ds(e * 2 + j, 1), :].rearrange("p a d -> p (a d)"),
                                      start=j == 0, stop=j == 1)
            mm.then_inc(pe_dn, 1)

        turn(0, 0, 1)
        kept = {n: pe.alloc_register(name) for n, name in ((-2, "last_but_one"), (-1, "last"), (0, "first"))}

        def expert_kept(n):
            return pe.snap(kept[n], min_val=0, max_val=NE - 1)

        pe.reg_load(kept[0], tab[0:1, 1, 0:1])

        def body(t0, i):
            experts_of = {n: expert_kept(n) for n in kept if lag(t0, n, 0)}
            for r in range(R):
                t = t0 + r
                pe.wait_ge(act_xT, t + 1)
                if lag(t0, r, 2):
                    pe.wait_ge(dve_h, t - 1)
                nc.tensor.matmul(UP[r % 2][:], xT[r % 2][:],
                                 w_up[:, bass.ds(experts_of[r], 1), :].rearrange("p a d -> p (a d)"),
                                 start=True, stop=True).then_inc(pe_up, 1)
                if r < R - 1:
                    experts_of[r + 1] = expert_of(t + 1)
                elif more(t0, r):
                    pe.reg_load(kept[0], tab[0:1, 1, bass.ds(t + 1, 1)])
                if more(t0, r):
                    turn(t + 1, (r + 1) % R, i + 1 if r < R - 1 else i + 2)
                if lag(t0, r, 1):
                    turn_h(t - 1, (r - 1) % R, lag(t0, r, 3))
                if lag(t0, r, 2):
                    down(t - 2, (r - 2) % R, lag(t0, r, 4), experts_of[r - 2])
            for n in (-2, -1):
                pe.reg_mov(kept[n], experts_of[R + n])

        tiles(pe, body)
        turn_h(NTILES - 1, NTILES - 1, True)
        for t in (NTILES - 2, NTILES - 1):
            down(t, t, True, expert_kept(t - NTILES))


def combine(nc, ctx, yk, x2b, out):
    yb = ctx.enter_context(nc.sbuf_tensor("yb", [P, NB, NT, TOPK, P], F32))
    ysum = ctx.enter_context(nc.sbuf_tensor("ysum", [P, NB, NT, P], F32))
    res = ctx.enter_context(nc.sbuf_tensor("res", [P, NB, NT, P], F32))
    loaded = [ctx.enter_context(nc.semaphore(f"cb_load{b}")) for b in range(NB)]
    added, done, stored = (ctx.enter_context(nc.semaphore("cb_" + n)) for n in ("added", "done", "stored"))
    yv = yk.rearrange("(b i p k) d -> b p i (k d)", b=NB, i=NT, k=TOPK)
    ov = out.rearrange("b (i p) d -> b p i d", p=P)
    block = ctx.enter_context(nc.Block())

    @block.sync
    def _(sp):
        for b in range(NB):
            sp.dma_start(yb[:, b].rearrange("p i k d -> p i (k d)"), yv[b]).then_inc(loaded[b], 16)

    @block.vector
    def _(dve):
        for b in range(NB):
            dve.wait_ge(loaded[b], 16)
            nc.vector.tensor_tensor(ysum[:, b], yb[:, b, :, 0, :], yb[:, b, :, 1, :], ALU.add).then_inc(added, 1)
            dve.wait_ge(added, b + 1)
            nc.vector.tensor_tensor(res[:, b], ysum[:, b], x2b[:, b * NT:(b + 1) * NT, :], ALU.add).then_inc(done, 1)

    @block.scalar
    def _(act):
        for b in range(NB):
            act.wait_ge(done, b + 1)
            act.dma_start(ov[b], res[:, b]).then_inc(stored, 16)
        act.wait_ge(stored, 16 * NB)


def build(nc, x, w_inT, b_in, w_outT, b_out, wqT, wscale, fbias, WqT, bq, WkT, bk, WvT, bv, nscale, wrT,
          w_up_in, w_dn_in, out):
    x1 = nc.dram_tensor("x1_dram", [NB, T, P], F32).ap()
    xs = nc.dram_tensor("expert_rows", [NE * CAP + P, ROW], F32).ap()
    yk = nc.dram_tensor("results", [TOKENS * TOPK, P], F32).ap()
    with ExitStack() as outer:
        def sb(name, shape, dt=F32):
            return outer.enter_context(nc.sbuf_tensor(name, shape, dt))

        buf = layer1_inputs(nc, outer)
        column = {"bqc": bq, "bkc": bk, "nsc": nscale}
        later = [(buf[n], src) for n, src in (("wq", WqT), ("wk", WkT), ("wv", WvT), ("wr", wrT))]
        later += [(buf[n], column[n].rearrange("(p a) -> p a", a=1)) for n in column]
        later += [(buf[n], src.partition_broadcast(P)) for n, src in (("bvr", bv),)]
        with ExitStack() as ctx:
            layer0(nc, ctx, x, w_inT, b_in, w_outT, b_out, wqT, wscale, fbias, x1, buf, later)
        x2b = sb("x2b", [P, NB * NT, P])
        tab = sb("tab", [1, 2, NTILES], I32)
        w_up = sb("w_up", [P, NE, 2 * HID])
        w_dn = sb("w_dn", [P, NE * 2, P])
        with ExitStack() as ctx:
            layer1(nc, ctx, x1, buf, xs, x2b, tab, w_up, w_dn, w_up_in, w_dn_in)
        with ExitStack() as ctx:
            experts(nc, ctx, xs, yk, w_up, w_dn, tab, buf["ident"])
        with ExitStack() as ctx:
            combine(nc, ctx, yk, x2b, out)


def by_parity(w):
    import numpy as np

    qk = w[:2 * P].reshape((2, H // 2, 2, HD) + w.shape[1:])
    return np.concatenate([np.moveaxis(qk, 1, 3).reshape((2 * P,) + w.shape[1:]), w[2 * P:]])


def kernel(**inputs):
    import concourse.bacc as bacc
    import numpy as np
    from concourse.bass_utils import run_bass_kernel_spmd

    a = {k: np.asarray(v) for k, v in inputs.items()}
    arrays = {
        "x": a["L0_attn_x"], "w_inT": by_parity(a["L0_attn_w_in"]).T, "b_in": by_parity(a["L0_attn_b_in"]),
        "w_outT": a["L0_attn_w_out"].T, "b_out": a["L0_attn_b_out"],
        "wqT": np.ascontiguousarray(a["L0_ffn_weight_q"].T).view(np.int32), "wscale": a["L0_ffn_weight_scale"], "fbias": a["L0_ffn_bias"],
        "WqT": a["L1_attn_Wq"].T, "bq": a["L1_attn_bq"], "WkT": a["L1_attn_Wk"].T, "bk": a["L1_attn_bk"],
        "WvT": a["L1_attn_Wv"].T, "bv": a["L1_attn_bv"],
        "nscale": a["L1_ffn_norm_scale"], "wrT": a["L1_ffn_w_router"].T,
        "w_up": a["L1_ffn_w_up"].transpose(2, 0, 1),
        "w_dn": a["L1_ffn_w_down"].reshape(NE, P, HID // P, P).transpose(3, 0, 2, 1).reshape(P, NE * 2, P),
    }
    arrays = {"in_" + k: np.ascontiguousarray(v) for k, v in arrays.items()}
    nc = bacc.Bacc("TRN2", target_bir_lowering=False, num_devices=1)
    args = [nc.dram_tensor(k, v.shape, mybir.dt.from_np(v.dtype), kind="ExternalInput").ap()
            for k, v in arrays.items()]
    args.append(nc.dram_tensor("out", [NB, T, P], F32, kind="ExternalOutput").ap())
    build(nc, *args)
    r = run_bass_kernel_spmd(nc, [arrays], core_ids=[0])
    return r.results[0]["out"]
```
